# Optimizing a Trainium2 kernel written in Bass

```python
import numpy as np
import jax
import jax.numpy as jnp

def _softmax(x, axis=-1):
    return jax.nn.softmax(x, axis=axis)

def _gelu(x):
    return jax.nn.gelu(x, approximate=True)

def _silu(x):
    return jax.nn.silu(x)

def _sigmoid(x):
    return jax.nn.sigmoid(x)

def _layernorm(x, axis=-1, eps=1e-05):
    m = jnp.mean(x, axis=axis, keepdims=True)
    v = jnp.var(x, axis=axis, keepdims=True)
    return (x - m) / jnp.sqrt(v + eps)

def _scatter_add(tgt, idx, src, axis=0):
    return tgt.at[idx].add(src)

def _segment_sum(src, seg, n):
    return jax.ops.segment_sum(src, seg, n)
kernel_name = 'mk_seq_postln_d1_jaxref_r8_88bb48'

def setup_inputs(seed: int=0):
    np.random.seed(seed)
    _w = jnp.asarray

    def _L0_attn_setup():
        import jax, jax.numpy as jnp
        import numpy as np
        D_MODEL = 256
        N_HEADS = 16
        D_HEAD = D_MODEL // N_HEADS
        B, S = (2, 256)
        EPS = 1e-05

        def _mhsa(X, ln_g, ln_b, Wq, bq, Wk, bk, Wv, bv, Wo, bo):
            n_ctx = X.shape[-2]
            mu = jnp.mean(X, axis=-1, keepdims=True)
            var = jnp.mean(jnp.square(X - mu), axis=-1, keepdims=True)
            Xn = (X - mu) * jax.lax.rsqrt(var + EPS) * ln_g + ln_b

            def split_heads(t):
                return t.reshape(t.shape[:-1] + (N_HEADS, D_HEAD)).swapaxes(-2, -3)
            Q = split_heads(Xn @ Wq + bq)
            K = split_heads(Xn @ Wk + bk)
            V = split_heads(Xn @ Wv + bv)
            scores = jnp.einsum('bhqd,bhkd->bhqk', Q, K) / jnp.sqrt(jnp.float32(D_HEAD))
            causal = jnp.tril(jnp.ones((n_ctx, n_ctx), dtype=bool))
            scores = jnp.where(causal, scores, jnp.float32(-jnp.inf))
            A = jax.nn.softmax(scores, axis=-1)
            AV = jnp.einsum('bhqk,bhkd->bhqd', A, V)
            AV = AV.swapaxes(-2, -3).reshape(X.shape[:-1] + (D_MODEL,))
            return AV @ Wo + bo
        key = jax.random.key(seed)
        ks = jax.random.split(key, 10)
        sd = 1.0 / np.sqrt(D_MODEL)
        inp = {'X': jax.random.normal(ks[0], (B, S, D_MODEL), dtype=jnp.float32), 'ln_g': jnp.ones((D_MODEL,), jnp.float32), 'ln_b': jnp.zeros((D_MODEL,), jnp.float32), 'Wq': jax.random.uniform(ks[1], (D_MODEL, D_MODEL), jnp.float32, -sd, sd), 'bq': jax.random.uniform(ks[2], (D_MODEL,), jnp.float32, -sd, sd), 'Wk': jax.random.uniform(ks[3], (D_MODEL, D_MODEL), jnp.float32, -sd, sd), 'bk': jax.random.uniform(ks[4], (D_MODEL,), jnp.float32, -sd, sd), 'Wv': jax.random.uniform(ks[5], (D_MODEL, D_MODEL), jnp.float32, -sd, sd), 'bv': jax.random.uniform(ks[6], (D_MODEL,), jnp.float32, -sd, sd), 'Wo': jax.random.uniform(ks[7], (D_MODEL, D_MODEL), jnp.float32, -sd, sd), 'bo': jax.random.uniform(ks[8], (D_MODEL,), jnp.float32, -sd, sd)}
        return inp
    _L0_attn_in = _L0_attn_setup()

    def _L0_ffn_setup():
        import jax, jax.numpy as jnp
        import numpy as np
        E = 64
        K = 6
        CAP = 64
        SCALE = 1.0
        H = 256
        I = 96
        SI = I * 2
        B, S = (2, 128)

        def _moe(x, gate_w, gate_up_proj, down_proj, shared_gate_w, shared_up_w, shared_down_w):
            b, s, h = x.shape
            T = b * s
            xf = x.reshape(T, h)
            scores = jax.nn.softmax(xf @ gate_w.T, axis=-1)
            topk_w, topk_idx = jax.lax.top_k(scores, K)
            topk_w = topk_w * SCALE
            flat_e = topk_idx.reshape(-1)
            order = jnp.argsort(flat_e)
            sorted_e = flat_e[order]
            sorted_tok = (order // K).astype(jnp.int32)
            sorted_w = topk_w.reshape(-1)[order]
            counts = jnp.zeros((E,), jnp.int32).at[flat_e].add(1)
            offsets = jnp.cumsum(counts) - counts
            pos = jnp.arange(T * K, dtype=jnp.int32) - offsets[sorted_e]
            buf_tok = jnp.full((E, CAP), T, jnp.int32).at[sorted_e, pos].set(sorted_tok, mode='drop')
            buf_w = jnp.zeros((E, CAP), x.dtype).at[sorted_e, pos].set(sorted_w, mode='drop')
            xp = jnp.concatenate([xf, jnp.zeros((1, h), x.dtype)], axis=0)
            gx = xp[buf_tok]
            gu = jnp.einsum('ech,ehi->eci', gx, gate_up_proj)
            g, u = jnp.split(gu, 2, axis=-1)
            hid = jax.nn.silu(g) * u
            eo = jnp.einsum('eci,eih->ech', hid, down_proj) * buf_w[..., None]
            routed = jnp.zeros((T + 1, h), x.dtype).at[buf_tok.reshape(-1)].add(eo.reshape(-1, h))[:T]
            shared = jax.nn.silu(xf @ shared_gate_w.T) * (xf @ shared_up_w.T) @ shared_down_w.T
            return (routed + shared).reshape(b, s, h)
        key = jax.random.key(seed)
        ks = jax.random.split(key, 7)
        x = jax.random.normal(ks[0], (B, S, H), jnp.float32)
        gate_w = jax.random.normal(ks[1], (E, H), jnp.float32) * 0.02
        gate_up_proj = jax.random.normal(ks[2], (E, H, 2 * I), jnp.float32) * 0.02
        down_proj = jax.random.normal(ks[3], (E, I, H), jnp.float32) * 0.02
        shared_gate_w = jax.random.normal(ks[4], (SI, H), jnp.float32) * 0.02
        shared_up_w = jax.random.normal(ks[5], (SI, H), jnp.float32) * 0.02
        shared_down_w = jax.random.normal(ks[6], (H, SI), jnp.float32) * 0.02
        return dict(x=x, gate_w=gate_w, gate_up_proj=gate_up_proj, down_proj=down_proj, shared_gate_w=shared_gate_w, shared_up_w=shared_up_w, shared_down_w=shared_down_w)
    _L0_ffn_in = _L0_ffn_setup()
    _d = {'L0_attn_X': _L0_attn_in['X'], 'L0_attn_ln_g': _L0_attn_in['ln_g'], 'L0_attn_ln_b': _L0_attn_in['ln_b'], 'L0_attn_Wq': _L0_attn_in['Wq'], 'L0_attn_bq': _L0_attn_in['bq'], 'L0_attn_Wk': _L0_attn_in['Wk'], 'L0_attn_bk': _L0_attn_in['bk'], 'L0_attn_Wv': _L0_attn_in['Wv'], 'L0_attn_bv': _L0_attn_in['bv'], 'L0_attn_Wo': _L0_attn_in['Wo'], 'L0_attn_bo': _L0_attn_in['bo'], 'L0_ffn_gate_w': _L0_ffn_in['gate_w'], 'L0_ffn_gate_up_proj': _L0_ffn_in['gate_up_proj'], 'L0_ffn_down_proj': _L0_ffn_in['down_proj'], 'L0_ffn_shared_gate_w': _L0_ffn_in['shared_gate_w'], 'L0_ffn_shared_up_w': _L0_ffn_in['shared_up_w'], 'L0_ffn_shared_down_w': _L0_ffn_in['shared_down_w']}
    _x0 = _d['L0_attn_X']
    _d['L0_attn_X'] = jax.random.normal(jax.random.fold_in(jax.random.key(seed), 1), (8, 256, 256), dtype=_x0.dtype)
    del _x0
    return _d

def reference(L0_attn_X, L0_attn_ln_g, L0_attn_ln_b, L0_attn_Wq, L0_attn_bq, L0_attn_Wk, L0_attn_bk, L0_attn_Wv, L0_attn_bv, L0_attn_Wo, L0_attn_bo, L0_ffn_gate_w, L0_ffn_gate_up_proj, L0_ffn_down_proj, L0_ffn_shared_gate_w, L0_ffn_shared_up_w, L0_ffn_shared_down_w):

    def _L0_attn_ref(X, ln_g, ln_b, Wq, bq, Wk, bk, Wv, bv, Wo, bo):
        import jax, jax.numpy as jnp
        import numpy as np
        D_MODEL = 256
        N_HEADS = 16
        D_HEAD = D_MODEL // N_HEADS
        B, S = (2, 256)
        EPS = 1e-05

        def _mhsa(X, ln_g, ln_b, Wq, bq, Wk, bk, Wv, bv, Wo, bo):
            n_ctx = X.shape[-2]
            mu = jnp.mean(X, axis=-1, keepdims=True)
            var = jnp.mean(jnp.square(X - mu), axis=-1, keepdims=True)
            Xn = (X - mu) * jax.lax.rsqrt(var + EPS) * ln_g + ln_b

            def split_heads(t):
                return t.reshape(t.shape[:-1] + (N_HEADS, D_HEAD)).swapaxes(-2, -3)
            Q = split_heads(Xn @ Wq + bq)
            K = split_heads(Xn @ Wk + bk)
            V = split_heads(Xn @ Wv + bv)
            scores = jnp.einsum('bhqd,bhkd->bhqk', Q, K) / jnp.sqrt(jnp.float32(D_HEAD))
            causal = jnp.tril(jnp.ones((n_ctx, n_ctx), dtype=bool))
            scores = jnp.where(causal, scores, jnp.float32(-jnp.inf))
            A = jax.nn.softmax(scores, axis=-1)
            AV = jnp.einsum('bhqk,bhkd->bhqd', A, V)
            AV = AV.swapaxes(-2, -3).reshape(X.shape[:-1] + (D_MODEL,))
            return AV @ Wo + bo
        return _mhsa(X, ln_g, ln_b, Wq, bq, Wk, bk, Wv, bv, Wo, bo)

    def _L0_ffn_ref(x, gate_w, gate_up_proj, down_proj, shared_gate_w, shared_up_w, shared_down_w):
        import jax, jax.numpy as jnp
        import numpy as np
        E = 64
        K = 6
        CAP = 64
        SCALE = 1.0
        H = 256
        I = 96
        SI = I * 2
        B, S = (2, 128)

        def _moe(x, gate_w, gate_up_proj, down_proj, shared_gate_w, shared_up_w, shared_down_w):
            b, s, h = x.shape
            T = b * s
            xf = x.reshape(T, h)
            scores = jax.nn.softmax(xf @ gate_w.T, axis=-1)
            topk_w, topk_idx = jax.lax.top_k(scores, K)
            topk_w = topk_w * SCALE
            flat_e = topk_idx.reshape(-1)
            order = jnp.argsort(flat_e)
            sorted_e = flat_e[order]
            sorted_tok = (order // K).astype(jnp.int32)
            sorted_w = topk_w.reshape(-1)[order]
            counts = jnp.zeros((E,), jnp.int32).at[flat_e].add(1)
            offsets = jnp.cumsum(counts) - counts
            pos = jnp.arange(T * K, dtype=jnp.int32) - offsets[sorted_e]
            buf_tok = jnp.full((E, CAP), T, jnp.int32).at[sorted_e, pos].set(sorted_tok, mode='drop')
            buf_w = jnp.zeros((E, CAP), x.dtype).at[sorted_e, pos].set(sorted_w, mode='drop')
            xp = jnp.concatenate([xf, jnp.zeros((1, h), x.dtype)], axis=0)
            gx = xp[buf_tok]
            gu = jnp.einsum('ech,ehi->eci', gx, gate_up_proj)
            g, u = jnp.split(gu, 2, axis=-1)
            hid = jax.nn.silu(g) * u
            eo = jnp.einsum('eci,eih->ech', hid, down_proj) * buf_w[..., None]
            routed = jnp.zeros((T + 1, h), x.dtype).at[buf_tok.reshape(-1)].add(eo.reshape(-1, h))[:T]
            shared = jax.nn.silu(xf @ shared_gate_w.T) * (xf @ shared_up_w.T) @ shared_down_w.T
            return (routed + shared).reshape(b, s, h)
        return _moe(x, gate_w, gate_up_proj, down_proj, shared_gate_w, shared_up_w, shared_down_w)
    x = L0_attn_X
    x = _layernorm(x + _L0_attn_ref(x, L0_attn_ln_g, L0_attn_ln_b, L0_attn_Wq, L0_attn_bq, L0_attn_Wk, L0_attn_bk, L0_attn_Wv, L0_attn_bv, L0_attn_Wo, L0_attn_bo), axis=-1)
    x = _layernorm(x + _L0_ffn_ref(x, L0_ffn_gate_w, L0_ffn_gate_up_proj, L0_ffn_down_proj, L0_ffn_shared_gate_w, L0_ffn_shared_up_w, L0_ffn_shared_down_w), axis=-1)
    return x

_drawn_inputs = setup_inputs


def setup_inputs(seed=0):
    import zlib

    import numpy as np

    out = dict(_drawn_inputs(seed))
    spreads = {'L0_attn_ln_g': (1.0, 0.6), 'L0_attn_ln_b': (0.0, 0.1)}
    factors = {'L0_attn_Wq': 2.982,
     'L0_attn_bq': 8.0,
     'L0_attn_Wk': 2.947,
     'L0_attn_bk': 8.0,
     'L0_ffn_gate_w': 8.0,
     'L0_ffn_gate_up_proj': 8.0,
     'L0_ffn_down_proj': 8.0,
     'L0_ffn_shared_gate_w': 3.918,
     'L0_ffn_shared_up_w': 3.846,
     'L0_ffn_shared_down_w': 3.854}
    for name, (base, spread) in spreads.items():
        noise = np.random.default_rng([zlib.crc32(name.encode()), seed]).standard_normal(out[name].shape)
        drawn = base * np.exp(spread * noise) if base else spread * noise
        out[name] = jnp.asarray(drawn.astype(out[name].dtype))
    for name, factor in factors.items():
        out[name] = (out[name] * factor).astype(out[name].dtype)
    return out
```

```python
from contextlib import ExitStack

import numpy as np

import concourse.bass as bass
from concourse import mybir

ALU = mybir.AluOpType
ACT = mybir.ActivationFunctionType
AX = mybir.AxisListType.X
F32 = mybir.dt.float32
BF16 = mybir.dt.bfloat16
U32 = mybir.dt.uint32

P = 128
D = 256
KD = D // P
NB = 8
S = 256
TILES = S // P
NT = NB * TILES
T = NB * S
NH = 16
DH = D // NH
HH = P // DH
E = 64
TOPK = 6
CAP = 64
FI = 96
SI = 2 * FI
NSLOT = E * CAP
NPAIR = E // 2
EPS = 1e-5
Q_SCALE = DH ** -0.5
COPIES = ((0, 3), (3, 2), (5, 1))
STACK = 6 * DH
NEGMAX = 3
MASKED = -1e30
SENT = 2
C_PROB = D
C_SENT = C_PROB + E
C_SLOT = C_SENT + SENT
C_DEST = C_SLOT + 8
ROW = C_DEST + 8
AWAY = 65536.0
ROUTE_STEPS = 18
WRING = 8
GRING = 4
RRING = 3


def moe_block_kernel(nc, io):
    with ExitStack() as ctx:
        def sb(name, shape, dt=F32):
            return ctx.enter_context(nc.sbuf_tensor(name, shape, dt))

        def sem(name):
            return ctx.enter_context(nc.semaphore(name))

        def sems(name, n):
            return [sem(f"{name}{i}") for i in range(n)]

        def dram(name, shape, dt=F32):
            return nc.dram_tensor(name, shape, dt, kind="Internal").ap()

        parts_d = dram("parts_d", (2, 4, 3, P, S), BF16)
        slots_d = dram("slots_d", (NSLOT, ROW))
        routed_d = dram("routed_d", (T * TOPK, D))
        x1_d = dram("x1_d", (T, D))

        ident = sb("ident", [P, P])
        ident_bf = sb("ident_bf", [P, P], BF16)
        before = sb("before", [P, P], BF16)
        ones_bf = sb("ones_bf", [P, P], BF16)
        upper = sb("upper", [P, P], BF16)
        slot_base = sb("slot_base", [P, TILES, E])
        neg_half = sb("neg_half", [P, TILES])
        own_slot = sb("own_slot", [P, 1])
        wq = sb("wq", [P, KD, D])
        wk = sb("wk", [P, KD, D])
        wv = sb("wv", [P, KD, D])
        wo = sb("wo", [P, NH // 4, D])
        wgate = sb("wgate", [P, KD, E + 2 * SI])
        wsd = sb("wsd", [FI, 2, D])
        cols = sb("cols", [P, 8])
        bias_row = sb("bias_row", [1, 2, D])
        bias_part = sb("bias_part", [1, 3, 2, D], BF16)
        bias_rest = sb("bias_rest", [1, 2, D])
        bias3 = sb("bias3", [3, 2, D], BF16)

        x_all = sb("x_all", [P, NT, D])
        stats1 = sb("stats1", [P, TILES, 6])
        mv1 = sb("mv1", [P, TILES, 2])
        ve1 = sb("ve1", [P, TILES])
        rstd1 = sb("rstd1", [P, TILES])
        xn = sb("xn", [P, TILES, D])
        xnT = sb("xnT", [P, KD, S])
        parts = sb("parts", [P, 4, 3, S], BF16)
        rest = sb("rest", [P, 4, S])
        qs = sb("qs", [STACK + NEGMAX, 2, NH, S], BF16)
        ks = sb("ks", [STACK + NEGMAX, 2, NH, S], BF16)
        vs = sb("vs", [P, 2, TILES, NH, 2 * DH])

        negmax = sb("negmax", [P, TILES, NH])
        negmax_rest = sb("negmax_rest", [P, TILES, NH])
        negmax_part = sb("negmax_part", [P, TILES, 3, NH], BF16)
        negmaxT = sb("negmaxT", [3 * NH, S], BF16)

        probs = sb("probs", [P, 2, 3 * 512])
        rowsum = sb("rowsum", [P, S])
        rinv = sb("rinv", [P, S])
        oT = sb("oT", [P, NH // 4, S])

        z = sb("z", [P, TILES, D])
        stats2 = sb("stats2", [P, TILES, 6])
        mv2 = sb("mv2", [P, TILES, 2])
        ve2 = sb("ve2", [P, TILES])
        rstd2 = sb("rstd2", [P, TILES])
        row = sb("row", [P, 2, TILES, ROW])
        x1T = sb("x1T", [P, KD, S])
        logits = sb("logits", [P, TILES, E])
        lmax = sb("lmax", [P, TILES])
        lexp = sb("lexp", [P, TILES, E])
        lsum = sb("lsum", [P, TILES])
        linv = sb("linv", [P, TILES])
        top8 = sb("top8", [P, TILES, 8])
        left = sb("left", [P, TILES, E + SENT])
        chosen = sb("chosen", [P, TILES, E], BF16)
        earlier = sb("earlier", [P, TILES, E], BF16)
        kept = sb("kept", [P, TILES, E])
        slot = sb("slot", [P, TILES, E])
        away = sb("away", [P, TILES, 8])
        slot_idx = sb("slot_idx", [P, 2, TILES, 8], U32)
        hraw = sb("hraw", [P, NT, 2 * SI])

        wgu = sb("wgu", [P, WRING, 2, KD, 2 * FI])
        wdn = sb("wdn", [FI, WRING, 2, D])
        zeros = sb("zeros", [P, 4 * ROW])
        h_gate = sb("h_gate", [P, 2, SI])
        h = sb("h", [P, 2, SI])
        hT = sb("hT", [FI, 2, 2, P])
        gate = sb("gate", [P, 2, FI])
        hid = sb("hid", [P, 2, FI])
        hidT = sb("hidT", [FI, 2, P])
        match = sb("match", [P, 8])
        found = sb("found", [P, 1])
        no_token = sb("no_token", [P, 1])
        dest_idx = sb("dest_idx", [P, GRING], U32)
        stats3 = sb("stats3", [P, 2, 6])
        mv3 = sb("mv3", [P, 2, 2])
        ve3 = sb("ve3", [P, 2])
        rstd3 = sb("rstd3", [P, 4])
        shift3 = sb("shift3", [P, 2])

        attend_flat = probs[:].rearrange("p a b -> p (a b)")
        x1_again = attend_flat[:, 0:2 * TILES * D].rearrange("p (i t d) -> p i t d", i=2, t=TILES)
        gx = attend_flat[:, 2 * TILES * D:2 * TILES * D + GRING * ROW].rearrange("p (c r) -> p c r", c=GRING)
        eo = oT[:]
        gxT = z[:].rearrange("p i (k q) -> p i k q", k=KD)
        half_sum = xn[:]
        result = rest[:]
        weights_flat = wgu[:].rearrange("p n e k i -> p (n e k i)")
        routed = weights_flat[:, 0:RRING * TOPK * D].rearrange("p (c j d) -> p c j d", c=RRING, j=TOPK)
        y = weights_flat[:, RRING * TOPK * D:(RRING * TOPK + 4) * D].rearrange("p (c d) -> p c d", c=4)

        psM = [ctx.enter_context(nc.psum_tensor(f"psM{i}", [P, 512], F32)) for i in range(2)]
        psE = [ctx.enter_context(nc.psum_tensor(f"psE{i}", [P, 512], F32)) for i in range(2)]
        psO = [ctx.enter_context(nc.psum_tensor(f"psO{i}", [P, 512], F32)) for i in range(2)]
        psG = [ctx.enter_context(nc.psum_tensor(f"psG{i}", [P, 512], F32)) for i in range(2)]

        wq_in = sem("wq_in")
        wkv_in = sem("wkv_in")
        weights_in = sem("weights_in")
        small_in = sem("small_in")
        bias3_in = sem("bias3_in")
        filled = sem("filled")
        x_in = sems("x_in", 3)
        consts = sem("consts")
        pool_step = sem("pool_step")
        setup_v = sem("setup_v")
        route_init = sem("route_init")
        bias_split = sem("bias_split")
        stats1_done = sem("stats1_done")
        mv1_done = sem("mv1_done")
        ve1_done = sem("ve1_done")
        rstd1_done = sem("rstd1_done")
        xn_done = sem("xn_done")
        xT_ps = sem("xT_ps")
        xnT_done = sem("xnT_done")
        qk_ps = sem("qk_ps")
        part1_done = sem("part1_done")
        rest_done = sem("rest_done")
        part2_done = sem("part2_done")
        part3_done = sem("part3_done")
        v_ps = sem("v_ps")
        vs_done = sem("vs_done")
        parts_out = sems("parts_out", 2)
        stack_in = sems("stack_in", 2)
        peak_ps = sem("peak_ps")
        peak_read = sem("peak_read")
        negmax_step = sem("negmax_step")
        negmaxT_ps = sem("negmaxT_ps")
        negmaxT_done = sem("negmaxT_done")
        negmax_in = sems("negmax_in", 2)
        score_ps = sem("score_ps")
        exp_done = sem("exp_done")
        masked = sem("masked")
        pv_ps = sem("pv_ps")
        rowsum_done = sem("rowsum_done")
        rinv_done = sem("rinv_done")
        oT_done = sem("oT_done")
        wo_ps = sem("wo_ps")
        z_done = sem("z_done")
        stats2_done = sem("stats2_done")
        mv2_done = sem("mv2_done")
        ve2_done = sem("ve2_done")
        rstd2_done = sem("rstd2_done")
        x1_done = sem("x1_done")
        x1T_ps = sem("x1T_ps")
        x1T_done = sem("x1T_done")
        gate_ps = sem("gate_ps")
        logits_done = sem("logits_done")
        hraw_done = sem("hraw_done")
        route_step = sem("route_step")
        lexp_done = sem("lexp_done")
        rank_ps = sem("rank_ps")
        rank_read = sem("rank_read")
        x1_out = sems("x1_out", 2)
        sent = sems("sent", 2)
        h_silu = sem("h_silu")
        h_done = sem("h_done")
        hT_ps = sem("hT_ps")
        hT_done = sem("hT_done")
        sd_ps = sem("sd_ps")
        sh_done = sem("sh_done")
        x1_back = sems("x1_back", 2)
        dest_cols = sem("dest_cols")
        slots_in = sems("slots_in", GRING)
        wexp_first = sem("wexp_first")
        wexp_in = sems("wexp_in", WRING)
        gT_ps = sem("gT_ps")
        gT_done = sem("gT_done")
        gu_ps = sem("gu_ps")
        silu_done = sem("silu_done")
        hid_done = sem("hid_done")
        hidT_ps = sem("hidT_ps")
        hidT_done = sem("hidT_done")
        dn_ps = sem("dn_ps")
        eo_low = sem("eo_low")
        eo_high = sem("eo_high")
        dest_step = sem("dest_step")
        dest_done = sem("dest_done")
        eo_out = sems("eo_out", GRING)
        routed_in = sems("routed_in", RRING)
        half_ps = sem("half_ps")
        half_done = sem("half_done")
        y_done = sem("y_done")
        stats3_done = sem("stats3_done")
        mv3_done = sem("mv3_done")
        ve3_done = sem("ve3_done")
        rstd3_done = sem("rstd3_done")
        shift3_done = sem("shift3_done")
        result_done = sem("result_done")
        out_out = sems("out_out", 4)


        def count(b, per, k):
            it, c = b
            v = per * c + k
            return v if it is None else it * (2 * per) + v

        def count_half(b, per, k):
            it, c = b
            v = per * (c // 2) + k
            return v if it is None else it * per + v

        def wait(eng, s, value):
            if isinstance(value, int) and value <= 0:
                return
            eng.wait_ge(s, value)

        def wait_alone(eng, s, value):
            if isinstance(value, int) and value <= 0:
                return
            eng.wait_ge(s, value)
            if not isinstance(value, int):
                eng.nop(nofuse=True)

        def later(b, n):
            return (b[0], b[1] + n)

        def par(b):
            return b[1] % 2

        def tile_of(b, t):
            return count(b, TILES, t)

        def steps(eng, step):
            step((None, 0), None, None)
            step((None, 1), (None, 0), None)
            with eng.Fori(0, (NB - 2) // 2) as it:
                for s in range(2):
                    step((it, 2 + s), (it, 1 + s), (it, s))
            step(None, (None, NB - 1), (None, NB - 2))
            step(None, None, (None, NB - 1))

        def tile_steps(eng, *parts_of_step):
            for c in range(2):
                for t in range(TILES):
                    for f in parts_of_step:
                        f((None, c), t)
            with eng.Fori(0, NB // 2 - 1) as it:
                for c in (2, 3):
                    for t in range(TILES):
                        for f in parts_of_step:
                            f((it, c), t)

        def pair_steps(eng, step):
            for c in range(WRING):
                step((None, c))
            with eng.Fori(0, NPAIR // WRING - 2) as it:
                for c in range(WRING, 2 * WRING):
                    step((it, c))
            for c in range(NPAIR - WRING, NPAIR):
                step((None, c))

        def nth(p, per, k):
            it, c = p
            v = per * c + k
            return v if it is None else it * (WRING * per) + v

        def nth_slot(p, ring, per, k):
            it, c = p
            v = per * (c // ring) + k
            return v if it is None else it * (WRING // ring * per) + v

        block = ctx.enter_context(nc.Block())

        @block.sync
        def _(sp):
            x_rows = io["X"].rearrange("b (t p) d -> p (b t) d", p=P)
            sp.dma_start(x_all[:, 0:TILES], x_rows[:, 0:TILES]).then_inc(x_in[0], 16)
            sp.dma_start(cols[:], io["cols"]).then_inc(small_in, 16)
            sp.dma_start(bias_row[:], io["bias_row"]).then_inc(small_in, 16)
            for w, name, s in ((wq, "Wq", wq_in), (wk, "Wk", wkv_in), (wv, "Wv", wkv_in)):
                sp.dma_start(w[:], io[name].rearrange("(k p) n -> p k n", p=P)).then_inc(s, 16)
            sp.dma_start(x_all[:, TILES:2 * TILES], x_rows[:, TILES:2 * TILES]).then_inc(x_in[1], 16)
            sp.dma_start(wgate[:], io["Wgate"].rearrange("(k p) n -> p k n", p=P)).then_inc(weights_in, 16)
            sp.dma_start(wsd[:], io["Wsd"].rearrange("(k p) n -> p k n", p=FI)).then_inc(weights_in, 16)
            sp.wait_ge(setup_v, 1)
            wo_rows = io["Wo"].rearrange("(g j d) n -> j d g n", j=4, d=DH)
            for j in range(4):
                sp.dma_start(wo[32 * j:32 * j + DH], wo_rows[j]).then_inc(weights_in, 16)
            sp.dma_start(x_all[:, 2 * TILES:], x_rows[:, 2 * TILES:]).then_inc(x_in[2], 16)
            sp.wait_ge(bias_split, 5)
            for c in range(3):
                sp.dma_start(bias3[c:c + 1], bias_part[0:1, c]).then_inc(bias3_in, 16)

            def stack(b):
                wait_alone(sp, stack_in[par(b)], count_half(b, 16 * 12, 0))
                wait_alone(sp, part3_done, count(b, 2, 2))
                sp.dma_start(parts_d[par(b)].rearrange("m c p t -> p (m c) t"),
                             parts[:].rearrange("p m c t -> p (m c) t")).then_inc(parts_out[par(b)], 16)
                wait_alone(sp, parts_out[par(b)], count_half(b, 16, 16))
                wait_alone(sp, score_ps, count(b, 12, -12))
                src = parts_d[par(b)].rearrange("m c (d h) t -> m (c d) (h t)", h=HH)
                for m in range(2):
                    heads = slice(HH * m, HH * m + HH)
                    for part, (c0, n) in enumerate(COPIES):
                        sp.dma_start(qs[DH * c0:DH * (c0 + n), par(b), heads, :],
                                     src[m, 0:DH * n]).then_inc(stack_in[par(b)], 16)
                        sp.dma_start(ks[DH * c0:DH * (c0 + n), par(b), heads, :],
                                     src[2 + m, DH * part:DH * (part + 1)].unsqueeze(0).broadcast_to(
                                         (n, DH, HH * S))).then_inc(stack_in[par(b)], 16)

            def negmax_rows(b):
                wait_alone(sp, negmaxT_done, count(b, 1, 1))
                for c in range(3):
                    sp.dma_start(qs[STACK + c:STACK + c + 1, par(b)],
                                 negmaxT[NH * c:NH * (c + 1), :]).then_inc(negmax_in[par(b)], 16)

            x1_rows = x1_d.rearrange("(b t p) d -> b p t d", t=TILES, p=P)

            def keep_x1(b):
                wait_alone(sp, x1_done, count(b, TILES, TILES))
                sp.dma_start(x1_rows[bass.ds(count(b, 1, 0), 1)].rearrange("o p t d -> p (o t) d"),
                             row[:, par(b), :, 0:D]).then_inc(x1_out[par(b)], 16)

            def step(f, m, a):
                if f:
                    stack(f)
                if m:
                    negmax_rows(m)
                if a:
                    keep_x1(a)

            steps(sp, step)

            for i in range(2):
                sp.wait_ge(x1_out[i], 16 * NB // 2)

            def load_x1(b, t):
                if t == 0:
                    wait_alone(sp, sh_done, count(b, TILES, -TILES))
                    sp.dma_start(x1_again[:, par(b)], x1_rows[bass.ds(count(b, 1, 0), 1)].rearrange(
                        "o p t d -> p (o t) d")).then_inc(x1_back[par(b)], 16)

            tile_steps(sp, load_x1)

            for i in range(2):
                sp.wait_ge(sent[i], 16 * 6 * TILES * NB // 2)

            slot_rows = slots_d.rearrange("(n p) r -> p n r", p=P)
            gu_rows = io["gate_up"].rearrange("(n e) (k p) i -> n p e k i", e=2, p=P)
            dn_rows = io["down"].rearrange("(n e) i d -> n i e d", e=2)

            def load_pair(p):
                c = p[1] % GRING
                wait_alone(sp, eo_low, nth(p, 1, 1 - GRING))
                wait_alone(sp, eo_high, nth(p, 1, 1 - GRING))
                wait_alone(sp, dest_done, nth(p, 1, 1 - GRING))
                sp.dma_start(gx[:, c], slot_rows[:, bass.ds(nth(p, 1, 0), 1)].rearrange(
                    "p o r -> p (o r)")).then_inc(slots_in[c], 16)

            def load_weights(p):
                c, n = p[1] % WRING, nth(p, 1, 0)
                wait_alone(sp, dn_ps, nth(p, 1, 1 - WRING))
                for e in range(2):
                    sp.dma_start(wgu[:, c, e], gu_rows[bass.ds(n, 1), :, e].rearrange(
                        "o p k i -> p (o k) i")).then_inc(wexp_in[c], 16)
                sp.dma_start(wdn[:, c], dn_rows[bass.ds(n, 1)].rearrange("o i e d -> i (o e) d")).then_inc(
                    wexp_in[c], 16)

            def load(p):
                if p[1] >= WRING:
                    load_weights(p)
                load_pair(p)

            pair_steps(sp, load)

            for c in range(GRING):
                sp.wait_ge(eo_out[c], 16 * NPAIR // GRING)
            routed_rows = routed_d.rearrange("(n p j) d -> n p j d", p=P, j=TOPK)
            out_rows = io["out"].rearrange("b (t p) d -> (b t) p d", p=P)
            for n in range(NT):
                c = n % RRING
                wait_alone(sp, y_done, n - RRING + 1)
                sp.dma_start(routed[:, c], routed_rows[n]).then_inc(routed_in[c], 16)
                if n >= 2:
                    sp.wait_ge(result_done, n - 1)
                    sp.dma_start(out_rows[n - 2], result[:, (n - 2) % 4]).then_inc(out_out[(n - 2) % 4], 16)
            for n in range(NT - 2, NT):
                sp.wait_ge(result_done, n + 1)
                sp.dma_start(out_rows[n], result[:, n % 4]).then_inc(out_out[n % 4], 16)
            for c in range(4):
                sp.wait_ge(out_out[c], 16 * NT // 4)

        @block.gpsimd
        def _(pool):
            g = nc.gpsimd
            g.memset(zeros[:], 0.0).then_inc(pool_step, 1)
            g.memset(ident[:], 0.0).then_inc(pool_step, 1)
            g.memset(before[:], 1.0).then_inc(pool_step, 1)
            g.memset(upper[:], 0.0).then_inc(pool_step, 1)
            g.memset(neg_half[:], -0.5).then_inc(consts, 1)
            g.memset(ones_bf[:], 1.0).then_inc(consts, 1)
            pool.wait_ge(pool_step, 4)
            g.affine_select(ident[:], ident[:], [[-1, P]], ALU.not_equal, 1.0, base=0,
                            channel_multiplier=1).then_inc(consts, 1)
            g.affine_select(before[:], before[:], [[1, P]], ALU.is_gt, 0.0, base=0,
                            channel_multiplier=-1).then_inc(consts, 1)
            g.affine_select(upper[:], upper[:], [[-1, P]], ALU.is_ge, MASKED, base=0,
                            channel_multiplier=1).then_inc(consts, 1)
            g.iota(slot_base[:], [[0, TILES], [CAP, E]], base=1, channel_multiplier=0,
                   allow_small_or_imprecise_dtypes=True).then_inc(consts, 1)
            g.iota(own_slot[:], [[0, 1]], base=1 - P, channel_multiplier=1,
                   allow_small_or_imprecise_dtypes=True).then_inc(consts, 1)
            for i in range(2):
                g.iota(row[:, i, :, C_DEST:C_DEST + 8], [[TOPK * P, TILES], [1, 8]],
                       base=1 + (i - 2) * TOPK * S, channel_multiplier=TOPK,
                       allow_small_or_imprecise_dtypes=True).then_inc(consts, 1)
            flat = slots_d.rearrange("(p n) r -> p (n r)", p=P)
            for i in range(NSLOT // P // 4):
                pool.dma_start(flat[:, i * 4 * ROW:(i + 1) * 4 * ROW], zeros[:]).then_inc(filled, 16)
            gu_rows = io["gate_up"].rearrange("(n e) (k p) i -> n p e k i", e=2, p=P)
            dn_rows = io["down"].rearrange("(n e) i d -> n i e d", e=2)
            for p in range(WRING):
                for e in range(2):
                    pool.dma_start(wgu[:, p, e], gu_rows[p, :, e]).then_inc(wexp_first, 16)
                pool.dma_start(wdn[:, p], dn_rows[p]).then_inc(wexp_first, 16)
            flat = routed_d.rearrange("(p n) d -> p (n d)", p=P)
            blank = 4 * D
            per_part = T * TOPK // P * D
            for lo in range(0, per_part, 12 * blank):
                pool.dma_start(flat[:, lo:lo + 12 * blank].rearrange("p (n w) -> p n w", w=blank),
                               zeros[:, 0:blank].unsqueeze(1).broadcast_to((P, 12, blank))).then_inc(filled, 16)
            fills = NSLOT // P // 4 + per_part // (12 * blank)

            def power_in(b):
                wait_alone(pool, mv1_done, count(b, TILES, TILES))
                g.tensor_scalar(ve1[:], mv1[:, :, 1], EPS, None, ALU.add).then_inc(ve1_done, 1)
                wait(pool, ve1_done, count(b, 1, 1))
                g.tensor_tensor(rstd1[:], ve1[:], neg_half[:], ALU.pow).then_inc(rstd1_done, 1)

            def power_mid(b):
                wait_alone(pool, mv2_done, count(b, TILES, TILES))
                g.tensor_scalar(ve2[:], mv2[:, :, 1], EPS, None, ALU.add).then_inc(ve2_done, 1)
                wait(pool, ve2_done, count(b, 1, 1))
                g.tensor_tensor(rstd2[:], ve2[:], neg_half[:], ALU.pow).then_inc(rstd2_done, 1)

            def mask(b, grp):
                cols_ = probs[:, grp % 2]
                wait_alone(pool, exp_done, count(b, 12, 3 * grp + 2))
                v = cols_[:, 0:1024].rearrange("p (h q) -> p h q", h=4)[:, :, 0:P]
                g.affine_select(v, v, [[0, 4], [1, P]], ALU.is_ge, 0.0, base=0,
                                channel_multiplier=-1).then_inc(masked, 1)
                wait_alone(pool, exp_done, count(b, 12, 3 * grp + 3))
                v = cols_[:, 1024:1536].rearrange("p (h q) -> p h q", h=4)
                g.affine_select(v, v, [[0, 4], [1, P]], ALU.is_ge, 0.0, base=0,
                                channel_multiplier=-1).then_inc(masked, 1)

            def dispatch(b):
                wait_alone(pool, sent[par(b)], count_half(b, 16 * 6 * TILES, 0))
                wait_alone(pool, x1_done, count(b, TILES, TILES))
                dest = row[:, par(b), :, C_DEST:C_DEST + 8]
                g.tensor_scalar(dest, dest, float(2 * TOPK * S), None, ALU.add).then_inc(dest_cols, 1)
                wait_alone(pool, dest_cols, count(b, 1, 1))
                wait_alone(pool, route_step, count(b, ROUTE_STEPS, ROUTE_STEPS))
                for t in range(TILES):
                    for j in range(TOPK):
                        g.indirect_dma_start(
                            out=slots_d, out_offset=bass.IndirectOffsetOnAxis(
                                ap=slot_idx[:, par(b), t, j:j + 1], axis=0),
                            in_=row[:, par(b), t, :], in_offset=None, bounds_check=NSLOT - 1,
                            oob_is_err=False).then_inc(sent[par(b)], 16)

            def step(f, m, a):
                if f:
                    power_in(f)
                if m and m[0] is None and m[1] == 0:
                    pool.wait_ge(filled, 16 * fills)
                if a:
                    for grp in range(4):
                        mask(a, grp)
                    power_mid(a)
                    dispatch(a)

            steps(pool, step)

            def scatter(p):
                c = p[1] % GRING
                wait_alone(pool, eo_low, nth(p, 1, 1))
                wait_alone(pool, eo_high, nth(p, 1, 1))
                wait_alone(pool, dest_done, nth(p, 1, 1))
                g.indirect_dma_start(out=routed_d, out_offset=bass.IndirectOffsetOnAxis(
                    ap=dest_idx[:, c:c + 1], axis=0), in_=eo[:, c], in_offset=None,
                    bounds_check=T * TOPK - 1, oob_is_err=False).then_inc(eo_out[c], 16)

            pair_steps(pool, scatter)

            for n in range(NT):
                i = n % 2
                pool.wait_ge(mv3_done, n + 1)
                g.tensor_scalar(ve3[:, i:i + 1], mv3[:, i, 1:2], EPS, None, ALU.add).then_inc(ve3_done, 1)
                pool.wait_ge(ve3_done, n + 1)
                g.tensor_tensor(rstd3[:, n % 4:n % 4 + 1], ve3[:, i:i + 1], neg_half[:, 0:1], ALU.pow).then_inc(
                    rstd3_done, 1)

        @block.scalar
        def _(act):
            s = nc.scalar
            act.wait_ge(small_in, 32)

            def transpose_out(b):
                wait(act, xT_ps, count(b, 1, 1))
                wait(act, v_ps, count(b, 1, 0))
                for k in range(KD):
                    s.activation(xnT[:, k], psG[0][:, k * S:(k + 1) * S], ACT.Identity,
                                 bias=cols[:, 2 + k:3 + k], scale=cols[:, k:k + 1]).then_inc(xnT_done, 1)

            def split_qk(b):
                if b[0] is None and b[1] == 0:
                    act.wait_ge(setup_v, 4)
                before_b = later(b, -1)
                if before_b[0] is not None or before_b[1] >= 0:
                    wait(act, parts_out[par(before_b)], count_half(before_b, 16, 16))
                for i in range(2):
                    wait(act, qk_ps, count(b, 2, i + 1))
                    for m in range(2):
                        s.activation(parts[:, 2 * i + m, 0], psG[1 - i][:, m * S:(m + 1) * S], ACT.Identity,
                                     bias=cols[:, 4 + 2 * i + m:5 + 2 * i + m]).then_inc(part1_done, 1)
                    wait(act, rest_done, count(b, 4, 2 * i + 2))
                    s.copy(parts[:, 2 * i:2 * i + 2, 1], rest[:, 2 * i:2 * i + 2]).then_inc(part2_done, 1)

            def values(b):
                wait(act, v_ps, count(b, 1, 1))
                wait(act, pv_ps, count(b, 4, -4))
                s.copy(vs[:, par(b), :, :, 0:DH],
                       psG[1][:].rearrange("p (t h d) -> p t h d", t=TILES, h=NH)).then_inc(vs_done, 1)

            def exponents(b):
                for u in range(12):
                    grp, j = divmod(u, 3)
                    wait(act, score_ps, count(b, 12, u + 1))
                    if j == 0:
                        wait(act, pv_ps, count(b, 4, max(grp - 1, 0)))
                    s.activation(probs[:, grp % 2, 512 * j:512 * (j + 1)], psE[u % 2][:],
                                 ACT.Exp).then_inc(exp_done, 1)

            def negmax_out(b):
                wait(act, negmaxT_ps, count(b, 1, 1))
                prev = later(b, -1)
                if prev[0] is not None or prev[1] >= 0:
                    wait(act, negmax_in[par(prev)], count_half(prev, 48, 48))
                s.copy(negmaxT[:], psG[1][0:3 * NH, 0:S // 2].bitcast(BF16)).then_inc(negmaxT_done, 1)

            def x1T_out(b):
                wait(act, x1T_ps, count(b, 1, 1))
                wait(act, gate_ps, count(b, 2, 0))
                s.copy(x1T[:].rearrange("p k t -> p (k t)"), psG[0][:]).then_inc(x1T_done, 1)

            def gate_out(b):
                for t in range(TILES):
                    wait(act, gate_ps, count(b, 2, t + 1))
                    wait(act, route_step, count(b, ROUTE_STEPS, 0))
                    s.copy(logits[:, t], psG[1 - t][:, 0:E]).then_inc(logits_done, 1)
                    s.copy(hraw[:, bass.ds(tile_of(b, t), 1)].rearrange("p o n -> p (o n)"),
                           psG[1 - t][:, E:E + 2 * SI]).then_inc(hraw_done, 1)

            def router_exp(b):
                wait(act, route_step, count(b, ROUTE_STEPS, 2))
                s.activation(lexp[:], lexp[:], ACT.Exp).then_inc(lexp_done, 1)

            def step(f, m, a):
                if f:
                    transpose_out(f)
                if a:
                    exponents(a)
                if f:
                    split_qk(f)
                    values(f)
                if m:
                    negmax_out(m)
                if a:
                    x1T_out(a)
                    gate_out(a)
                    router_exp(a)

            steps(act, step)

            act.wait_ge(hraw_done, NT)

            def shared(b, t):
                wait(act, h_done, count(b, TILES, t - 1))
                s.activation(h_gate[:, t], hraw[:, bass.ds(tile_of(b, t), 1), 0:SI].rearrange("p o n -> p (o n)"),
                             ACT.Silu).then_inc(h_silu, 1)

            def shared_T(b, t):
                wait(act, hT_ps, count(b, TILES, t + 1))
                wait(act, sd_ps, count(b, TILES, t - 1))
                s.copy(hT[:, t].rearrange("p c q -> p (c q)"), psM[t][0:FI, 0:2 * P]).then_inc(hT_done, 1)

            tile_steps(act, shared, shared_T)

            def rows_T(p):
                i = p[1] % 2
                wait(act, gT_ps, nth(p, 1, 1))
                wait(act, gu_ps, nth(p, 1, -1))
                s.copy(gxT[:, i].rearrange("p k q -> p (k q)"), psG[i][:, 0:D]).then_inc(gT_done, 1)

            def gates(p):
                i = p[1] % 2
                wait(act, gu_ps, nth(p, 1, 1))
                wait(act, hid_done, nth(p, 1, -1))
                s.activation(gate[:, i], psO[i][:, 0:FI], ACT.Silu).then_inc(silu_done, 1)

            def outputs_high(p):
                i, c = p[1] % 2, p[1] % GRING
                wait(act, dn_ps, nth(p, 1, 1))
                wait(act, eo_out[c], nth_slot(p, GRING, 16, 0))
                s.activation(eo[CAP:2 * CAP, c], psE[i][CAP:2 * CAP, 0:D], ACT.Copy,
                             scale=gx[CAP:2 * CAP, c, bass.ds(nth(p, 2, C_PROB + 1), 1)]).then_inc(eo_high, 1)

            rows_T((None, 0))
            rows_T((None, 1))
            gates((None, 0))

            def pair(p):
                last = p[0] is None and p[1] >= NPAIR - 2
                if not last:
                    rows_T(later(p, 2))
                if not (last and p[1] == NPAIR - 1):
                    gates(later(p, 1))
                outputs_high(p)

            pair_steps(act, pair)

            for n in range(NT):
                i = n % 2
                act.wait_ge(shift3_done, n + 1)
                wait(act, out_out[n % 4], 16 * (n // 4))
                s.activation(result[:, n % 4], y[:, n % 4], ACT.Identity, bias=shift3[:, i:i + 1],
                             scale=rstd3[:, n % 4:n % 4 + 1]).then_inc(result_done, 1)

        @block.vector
        def _(dve):
            v = nc.vector
            v.memset(wo[:], 0.0).then_inc(setup_v, 1)
            v.memset(vs[:], 1.0).then_inc(setup_v, 1)
            v.memset(ks[STACK:STACK + NEGMAX], 1.0).then_inc(setup_v, 1)
            v.memset(earlier[:], 0.0).then_inc(route_init, 1)
            v.memset(row[:, :, :, C_SENT:C_SENT + SENT], 2.0).then_inc(rank_read, 1)
            dve.wait_ge(small_in, 32)
            v.tensor_scalar(cols[:, 4:6], cols[:, 4:6], Q_SCALE, None, ALU.mult).then_inc(setup_v, 1)
            rest_row = bias_rest[:]
            v.tensor_copy(bias_part[:, 0], bias_row[:]).then_inc(bias_split, 1)
            dve.wait_ge(bias_split, 1)
            v.tensor_tensor(rest_row, bias_row[:], bias_part[:, 0], ALU.subtract).then_inc(bias_split, 1)
            dve.wait_ge(bias_split, 2)
            v.tensor_copy(bias_part[:, 1], rest_row).then_inc(bias_split, 1)
            dve.wait_ge(bias_split, 3)
            v.tensor_tensor(rest_row, rest_row, bias_part[:, 1], ALU.subtract).then_inc(bias_split, 1)
            dve.wait_ge(bias_split, 4)
            v.tensor_copy(bias_part[:, 2], rest_row).then_inc(bias_split, 1)
            dve.wait_ge(consts, 9)
            v.tensor_copy(ident_bf[:], ident[:]).then_inc(setup_v, 1)
            dve.wait_ge(wq_in, 16)
            v.tensor_scalar(wq[:], wq[:], Q_SCALE, None, ALU.mult).then_inc(setup_v, 1)

            def x_tiles(b, t=None):
                if t is None:
                    return x_all[:, bass.ds(tile_of(b, 0), TILES)]
                return x_all[:, bass.ds(tile_of(b, t), 1)].rearrange("p o d -> p (o d)")

            def norm_in(b):
                wait(dve, x_in[min(b[1], 2)], 16)
                for t in range(TILES):
                    v.bn_stats(stats1[:, t], x_tiles(b, t)).then_inc(stats1_done, 1)
                wait_alone(dve, stats1_done, count(b, TILES, TILES))
                for t in range(TILES):
                    v.bn_aggr(mv1[:, t], stats1[:, t]).then_inc(mv1_done, 1)
                wait(dve, rstd1_done, count(b, 1, 1))
                wait(dve, xT_ps, count(b, 1, 0))
                for t in range(TILES):
                    v.tensor_scalar(xn[:, t], x_tiles(b, t), mv1[:, t, 0:1], rstd1[:, t:t + 1],
                                    ALU.subtract, ALU.mult).then_inc(xn_done, 1)

            def split_qk(b):
                for i in range(2):
                    for m in range(2):
                        mm = 2 * i + m
                        wait(dve, part1_done, count(b, 4, 2 * i + 2))
                        v.scalar_tensor_tensor(rest[:, mm], psG[1 - i][:, m * S:(m + 1) * S],
                                               cols[:, 4 + mm:5 + mm], parts[:, mm, 0], ALU.add,
                                               ALU.subtract).then_inc(rest_done, 1)
                    wait(dve, part2_done, count(b, 2, i + 1))
                    two = slice(2 * i, 2 * i + 2)
                    v.tensor_tensor(parts[:, two, 2], rest[:, two], parts[:, two, 1],
                                    ALU.subtract).then_inc(part3_done, 1)

            def maxima(b, lo, hi):
                for u in range(lo, hi):
                    wait(dve, peak_ps, count(b, 12, u + 1))
                    if u < 4:
                        out, src = negmax[:, 0, 4 * u:4 * u + 4], psM[u % 2][:].rearrange("p (h k) -> p h k", h=4)
                    else:
                        w = u - 4
                        out, src = negmax[:, 1, 2 * w:2 * w + 2], psM[u % 2][:].rearrange("p (h k) -> p h k", h=2)
                    v.tensor_reduce(out, src, AX, ALU.max, negate=True).then_inc(peak_read, 1)

            def negmax_split(b):
                wait(dve, peak_read, count(b, 12, 12))
                wait(dve, negmaxT_ps, count(b, 1, 0))
                v.tensor_copy(negmax_part[:, :, 0], negmax[:]).then_inc(negmax_step, 1)
                wait(dve, negmax_step, count(b, 4, 1))
                v.tensor_tensor(negmax_rest[:], negmax[:], negmax_part[:, :, 0], ALU.subtract).then_inc(
                    negmax_step, 1)
                wait(dve, negmax_step, count(b, 4, 2))
                v.tensor_copy(negmax_part[:, :, 1], negmax_rest[:]).then_inc(negmax_step, 1)
                wait(dve, negmax_step, count(b, 4, 3))
                v.tensor_tensor(negmax_part[:, :, 2], negmax_rest[:], negmax_part[:, :, 1],
                                ALU.subtract).then_inc(negmax_step, 1)

            SUM_ROWS = [DH + i % DH for i in range(2 * DH)]

            def normalise(b, grp):
                if grp == 0:
                    wait_alone(dve, wo_ps, count(b, 1, 0))
                wait_alone(dve, pv_ps, count(b, 4, grp + 1))
                v.stream_shuffle(rowsum[:], psO[grp % 2][:, 0:S], SUM_ROWS).then_inc(rowsum_done, 1)
                wait(dve, rowsum_done, count(b, 4, grp + 1))
                v.reciprocal(rinv[:], rowsum[:]).then_inc(rinv_done, 1)
                wait(dve, rinv_done, count(b, 4, grp + 1))
                v.tensor_tensor(oT[:, grp], psO[grp % 2][:, 0:S], rinv[:], ALU.mult).then_inc(oT_done, 1)

            def norm_mid(b):
                wait(dve, wo_ps, count(b, 1, 1))
                v.tensor_tensor(z[:], psG[0][:].rearrange("p (t d) -> p t d", t=TILES), x_tiles(b),
                                ALU.add).then_inc(z_done, 1)
                wait(dve, z_done, count(b, 1, 1))
                for t in range(TILES):
                    v.bn_stats(stats2[:, t], z[:, t]).then_inc(stats2_done, 1)
                wait_alone(dve, stats2_done, count(b, TILES, TILES))
                for t in range(TILES):
                    v.bn_aggr(mv2[:, t], stats2[:, t]).then_inc(mv2_done, 1)

            def norm_mid_end(b):
                wait(dve, rstd2_done, count(b, 1, 1))
                wait(dve, sent[par(b)], count_half(b, 16 * 6 * TILES, 0))
                wait(dve, x1_out[par(b)], count_half(b, 16, 0))
                for t in range(TILES):
                    v.tensor_scalar(row[:, par(b), t, 0:D], z[:, t], mv2[:, t, 0:1], rstd2[:, t:t + 1],
                                    ALU.subtract, ALU.mult).then_inc(x1_done, 1)

            def route(b):
                r = row[:, par(b)]
                done = [0]

                def chained(ins):
                    done[0] += 1
                    ins.then_inc(route_step, 1)
                    wait_alone(dve, route_step, count(b, ROUTE_STEPS, done[0]))

                def loose(ins):
                    done[0] += 1
                    ins.then_inc(route_step, 1)

                wait(dve, logits_done, count(b, TILES, TILES))
                chained(v.reduce_max(lmax[:], logits[:], AX))
                loose(v.tensor_tensor(lexp[:], logits[:], lmax[:].unsqueeze(2).broadcast_to((P, TILES, E)),
                                      ALU.subtract))
                wait(dve, lexp_done, count(b, 1, 1))
                chained(v.reduce_sum(lsum[:], lexp[:], AX))
                chained(v.reciprocal(linv[:], lsum[:]))
                chained(v.tensor_tensor(r[:, :, C_PROB:C_PROB + E], lexp[:],
                                        linv[:].unsqueeze(2).broadcast_to((P, TILES, E)), ALU.mult))
                loose(v.max(top8[:, 0], r[:, 0, C_PROB:C_SENT + SENT]))
                chained(v.max(top8[:, 1], r[:, 1, C_PROB:C_SENT + SENT]))
                loose(v.match_replace(left[:, 0], top8[:, 0], r[:, 0, C_PROB:C_SENT + SENT], -1.0))
                chained(v.match_replace(left[:, 1], top8[:, 1], r[:, 1, C_PROB:C_SENT + SENT], -1.0))
                chained(v.tensor_scalar(chosen[:], left[:, :, 0:E], 0.0, None, ALU.is_lt))
                loose(v.tensor_tensor(earlier[:, 1], earlier[:, 0], chosen[:, 0], ALU.add))
                wait(dve, rank_ps, count(b, 1, 1))
                rank = psG[1][:, 0:TILES * E].rearrange("p (t e) -> p t e", t=TILES)
                loose(v.scalar_tensor_tensor(kept[:], rank, float(CAP), chosen[:], ALU.is_lt, ALU.mult))
                v.tensor_tensor(slot[:], rank, slot_base[:], ALU.add).then_inc(rank_read, 1)
                wait_alone(dve, rank_read, count(b, 1, 2))
                loose(v.tensor_tensor(earlier[:, 0], earlier[:, 1], chosen[:, 1], ALU.add))
                chained(v.tensor_tensor(slot[:], slot[:], kept[:], ALU.mult))
                loose(v.max(r[:, 0, C_SLOT:C_SLOT + 8], slot[:, 0]))
                chained(v.max(r[:, 1, C_SLOT:C_SLOT + 8], slot[:, 1]))
                chained(v.tensor_scalar(away[:], r[:, :, C_SLOT:C_SLOT + 8], 0.0, AWAY, ALU.is_equal, ALU.mult))
                loose(v.scalar_tensor_tensor(slot_idx[:, par(b)], r[:, :, C_SLOT:C_SLOT + 8], -1.0, away[:],
                                             ALU.add, ALU.add))
                assert done[0] == ROUTE_STEPS

            def step(f, m, a):
                if f:
                    norm_in(f)
                if a:
                    for grp in range(4):
                        normalise(a, grp)
                if f:
                    split_qk(f)
                if m:
                    maxima(m, 0, 6)
                if a:
                    norm_mid(a)
                if m:
                    maxima(m, 6, 12)
                    negmax_split(m)
                if a:
                    norm_mid_end(a)
                    route(a)

            dve.wait_ge(route_init, 1)
            dve.wait_ge(rank_read, 1)
            steps(dve, step)

            def shared(b, t):
                wait(dve, h_silu, count(b, TILES, t + 1))
                wait(dve, hT_ps, count(b, TILES, t - 1))
                v.tensor_tensor(h[:, t], h_gate[:, t],
                                hraw[:, bass.ds(tile_of(b, t), 1), SI:2 * SI].rearrange("p o n -> p (o n)"),
                                ALU.mult).then_inc(h_done, 1)

            def shared_out(b, t):
                if t == 0:
                    wait(dve, x1_back[par(b)], count_half(b, 16, 16))
                wait(dve, sd_ps, count(b, TILES, t + 1))
                v.tensor_tensor(x_tiles(b, t), psE[t][:, 0:D], x1_again[:, par(b), t], ALU.add).then_inc(sh_done, 1)

            tile_steps(dve, shared, shared_out)

            def destinations(p):
                c = p[1] % GRING
                wait_alone(dve, slots_in[c], nth_slot(p, GRING, 16, 16))
                v.tensor_scalar(own_slot[:], own_slot[:], float(P), None, ALU.add).then_inc(dest_step, 1)
                wait_alone(dve, dest_step, nth(p, 3, 1))
                v.scalar_tensor_tensor(match[:], gx[:, c, C_SLOT:C_SLOT + 8], own_slot[:], gx[:, c, C_DEST:C_DEST + 8],
                                       ALU.is_equal, ALU.mult, accum_out=found[:]).then_inc(dest_step, 1)
                wait_alone(dve, dest_step, nth(p, 3, 2))
                v.tensor_scalar(no_token[:], found[:], 0.0, AWAY, ALU.is_equal, ALU.mult).then_inc(dest_step, 1)
                wait_alone(dve, dest_step, nth(p, 3, 3))
                wait_alone(dve, eo_out[c], nth_slot(p, GRING, 16, 0))
                v.scalar_tensor_tensor(dest_idx[:, c:c + 1], found[:], -1.0, no_token[:], ALU.add,
                                       ALU.add).then_inc(dest_done, 1)

            def hidden(p):
                i = p[1] % 2
                wait(dve, silu_done, nth(p, 1, 1))
                wait(dve, hidT_ps, nth(p, 1, -1))
                v.tensor_tensor(hid[:, i], psO[i][:, FI:2 * FI], gate[:, i], ALU.mult).then_inc(hid_done, 1)

            def hidden_T(p):
                i = p[1] % 2
                wait(dve, hidT_ps, nth(p, 1, 1))
                wait(dve, dn_ps, nth(p, 1, -1))
                v.tensor_copy(hidT[:, i], psM[i][0:FI, 0:P]).then_inc(hidT_done, 1)

            def outputs_low(p):
                i, c = p[1] % 2, p[1] % GRING
                wait(dve, dn_ps, nth(p, 1, 1))
                wait(dve, eo_out[c], nth_slot(p, GRING, 16, 0))
                v.tensor_scalar(eo[0:CAP, c], psE[i][0:CAP, 0:D],
                                gx[0:CAP, c, bass.ds(nth(p, 2, C_PROB), 1)], None, ALU.mult).then_inc(eo_low, 1)

            destinations((None, 0))
            hidden((None, 0))

            def pair(p):
                last = p[0] is None and p[1] == NPAIR - 1
                hidden_T(p)
                if not last:
                    hidden(later(p, 1))
                outputs_low(p)
                if not last:
                    destinations(later(p, 1))

            pair_steps(dve, pair)

            def shift(n):
                i = n % 2
                dve.wait_ge(rstd3_done, n + 1)
                wait(dve, result_done, n - 1)
                v.tensor_scalar(shift3[:, i:i + 1], mv3[:, i, 0:1], rstd3[:, n % 4:n % 4 + 1], -1.0, ALU.mult,
                                ALU.mult).then_inc(shift3_done, 1)

            for n in range(NT):
                i, c = n % 2, n % RRING
                dve.wait_ge(routed_in[c], 16 * (n // RRING + 1))
                v.reduce_sum(half_sum[:, i], routed[:, c, 3:].rearrange("p j d -> p d j"), AX).then_inc(half_done, 1)
                dve.wait_ge(half_done, n + 1)
                dve.wait_ge(half_ps, n + 1)
                wait(dve, result_done, n - 3)
                v.tensor_tensor(y[:, n % 4], psE[i][:, 0:D], half_sum[:, i], ALU.add).then_inc(y_done, 1)
                dve.wait_ge(y_done, n + 1)
                v.bn_stats(stats3[:, i], y[:, n % 4]).then_inc(stats3_done, 1)
                dve.wait_ge(stats3_done, n + 1)
                v.bn_aggr(mv3[:, i], stats3[:, i]).then_inc(mv3_done, 1)
                if n:
                    shift(n - 1)
            shift(NT - 1)

        @block.tensor
        def _(pe):
            mm = nc.tensor.matmul
            pe.wait_ge(consts, 9)

            def transpose_in(b):
                wait(pe, xn_done, count(b, TILES, TILES))
                wait(pe, rest_done, count(b, 4, 0))
                wait(pe, hraw_done, count(b, TILES, -2 * TILES))
                for k in range(KD):
                    for t in range(TILES):
                        ins = nc.tensor.transpose(psG[0][:, k * S + t * P:k * S + (t + 1) * P],
                                                  xn[:, t, k * P:(k + 1) * P], ident[:])
                ins.then_inc(xT_ps, 1)

            def project(b):
                if b[0] is None and b[1] == 0:
                    pe.wait_ge(setup_v, 6)
                    pe.wait_ge(wkv_in, 32)
                    pe.wait_ge(bias3_in, 48)
                wait(pe, xnT_done, count(b, KD, KD))
                for i, (w, bank) in enumerate(((wq, psG[1]), (wk, psG[0]))):
                    if i == 0:
                        wait(pe, negmaxT_done, count(b, 1, -1))
                        wait(pe, rank_read, count(b, 1, -1))
                        if b[0] is None and b[1] == 1:
                            pe.wait_ge(vs_done, 1)
                    for m in range(2):
                        for k in range(KD):
                            ins = mm(bank[:, m * S:(m + 1) * S], w[:, k, m * P:(m + 1) * P], xnT[:, k],
                                     start=k == 0, stop=k == KD - 1)
                    ins.then_inc(qk_ps, 1)
                wait(pe, rest_done, count(b, 4, 2))
                for t in range(TILES):
                    for k in range(KD):
                        mm(psG[1][:, t * D:(t + 1) * D], xnT[:, k, t * P:(t + 1) * P], wv[:, k],
                           start=k == 0, stop=False)
                    ins = mm(psG[1][:, t * D:(t + 1) * D], ones_bf[0:3, :], bias3[:, 0], start=False, stop=True)
                ins.then_inc(v_ps, 1)

            def peak(b, lo, hi):
                i = par(b)
                if lo == 0:
                    wait(pe, stack_in[i], count_half(b, 16 * 12, 16 * 12))
                for u in range(lo, hi):
                    wait(pe, peak_read, count(b, 12, u - 1))
                    bank = psM[u % 2]
                    if u < 4:
                        for j in range(4):
                            mm(bank[:, j * P:(j + 1) * P], qs[0:STACK, i, 4 * u + j, 0:P],
                               ks[0:STACK, i, 4 * u + j, 0:P], start=j == 0, stop=False, skip_group_check=True)
                        out, mask = bank[:].rearrange("p (h k) -> p h k", h=4), (P, 4, P)
                    else:
                        for j in range(2):
                            mm(bank[:, j * S:(j + 1) * S], qs[0:STACK, i, 2 * (u - 4) + j, P:S],
                               ks[0:STACK, i, 2 * (u - 4) + j, :], start=j == 0, stop=False,
                               skip_group_check=True)
                        out, mask = bank[:].rearrange("p (h k) -> p h k", h=2)[:, :, P:S], (P, 2, P)
                    mm(out, ident_bf[:], upper[:].unsqueeze(1).broadcast_to(mask), start=False, stop=True,
                       skip_group_check=True).then_inc(peak_ps, 1)

            def negmax_T(b, f):
                wait_alone(pe, negmax_step, count(b, 4, 4))
                if f:
                    wait_alone(pe, vs_done, count(f, 1, 1))
                wait_alone(pe, rank_read, count(b, 1, 0))
                for t in range(TILES):
                    ins = nc.tensor.transpose(psG[1][0:3 * NH, t * P // 2:(t + 1) * P // 2].bitcast(BF16),
                                              negmax_part[:, t].rearrange("p c h -> p (c h)"), ident_bf[:])
                ins.then_inc(negmaxT_ps, 1)

            def scores(b, u):
                i = par(b)
                grp, j = divmod(u, 3)
                if u == 0:
                    wait(pe, negmax_in[i], count_half(b, 48, 48))
                wait(pe, exp_done, count(b, 12, max(u - 1, 0)))
                for n in range(2 if j < 2 else 4):
                    h_, width, q0 = (4 * grp + 2 * j + n, S, 0) if j < 2 else (4 * grp + n, P, P)
                    keys = slice(0, P) if j < 2 else slice(P, S)
                    ins = mm(psE[u % 2][:, n * width:(n + 1) * width], ks[:, i, h_, keys], qs[:, i, h_, q0:S],
                             start=True, stop=True)
                ins.then_inc(score_ps, 1)

            def weighted(b, grp):
                i, bank = par(b), psO[grp % 2]
                if grp == 0:
                    wait(pe, vs_done, count(b, 1, 1))
                wait(pe, masked, count(b, 8, 2 * grp + 2))
                wait(pe, oT_done, count(b, 4, max(grp - 1, 0)))
                for j in range(4):
                    mm(bank[32 * j:32 * j + 32, 0:S], vs[:, i, 0, 4 * grp + j], probs[:, grp % 2, j * S:(j + 1) * S],
                       start=True, stop=False, skip_group_check=True)
                for j in range(4):
                    ins = mm(bank[32 * j:32 * j + 32, P:S], vs[:, i, 1, 4 * grp + j],
                             probs[:, grp % 2, 1024 + j * P:1024 + (j + 1) * P], start=False, stop=True,
                             skip_group_check=True)
                ins.then_inc(pv_ps, 1)

            def attend(b):
                for u in range(12):
                    scores(b, u)
                    if u in (4, 7, 10):
                        weighted(b, (u - 4) // 3)
                weighted(b, 3)

            def out_project(b, f):
                if b[0] is None and b[1] == 0:
                    pe.wait_ge(weights_in, 16 * 6)
                wait(pe, oT_done, count(b, 4, 4))
                if f:
                    wait(pe, rest_done, count(f, 4, 4))
                wait(pe, hraw_done, count(b, TILES, 0))
                for t in range(TILES):
                    out = psG[0][:, t * D:(t + 1) * D]
                    for grp in range(4):
                        mm(out, oT[:, grp, t * P:(t + 1) * P], wo[:, grp], start=grp == 0, stop=False)
                    ins = mm(out, ones_bf[0:3, :], bias3[:, 1], start=False, stop=True)
                ins.then_inc(wo_ps, 1)

            def gate_project(b, m):
                wait(pe, x1_done, count(b, TILES, TILES))
                for k in range(KD):
                    for t in range(TILES):
                        ins = nc.tensor.transpose(psG[0][:, k * S + t * P:k * S + (t + 1) * P],
                                                  row[:, par(b), t, k * P:(k + 1) * P], ident[:])
                ins.then_inc(x1T_ps, 1)
                wait(pe, x1T_done, count(b, 1, 1))
                if m:
                    wait(pe, negmaxT_done, count(m, 1, 1))
                wait(pe, rank_read, count(b, 1, 1))
                for t in range(TILES):
                    for k in range(KD):
                        ins = mm(psG[1 - t][:, 0:E + 2 * SI], x1T[:, k, t * P:(t + 1) * P], wgate[:, k],
                                 start=k == 0, stop=k == KD - 1)
                    ins.then_inc(gate_ps, 1)

            def rank(b):
                wait(pe, route_step, count(b, ROUTE_STEPS, 11))
                wait(pe, hraw_done, count(b, TILES, 1))
                out = psG[1][:, 0:TILES * E]
                mm(out, before[:], chosen[:].rearrange("p t e -> p (t e)"), start=True, stop=False)
                mm(out, ones_bf[:], earlier[:].rearrange("p t e -> p (t e)"), start=False,
                   stop=True).then_inc(rank_ps, 1)

            def step(f, m, a):
                if f:
                    transpose_in(f)
                if a:
                    attend(a)
                if f:
                    project(f)
                if m:
                    peak(m, 0, 6)
                if a:
                    out_project(a, f)
                if m:
                    peak(m, 6, 12)
                    negmax_T(m, f)
                if a:
                    gate_project(a, m)
                    rank(a)

            steps(pe, step)

            pe.wait_ge(peak_read, 12 * NB)
            pe.wait_ge(exp_done, 12 * NB)

            def shared_T(b, t):
                wait(pe, h_done, count(b, TILES, t + 1))
                wait(pe, hT_done, count(b, TILES, t - 1))
                for c in range(2):
                    ins = nc.tensor.transpose(psM[t][0:FI, c * P:(c + 1) * P], h[:, t, c * FI:(c + 1) * FI],
                                              ident[:])
                ins.then_inc(hT_ps, 1)

            def shared_down(b, t):
                wait(pe, hT_done, count(b, TILES, t + 1))
                wait(pe, sh_done, count(b, TILES, t - 1))
                for c in range(2):
                    ins = mm(psE[t][:, 0:D], hT[:, t, c], wsd[:, c], start=c == 0, stop=c == 1)
                ins.then_inc(sd_ps, 1)

            tile_steps(pe, shared_T, shared_down)

            pe.wait_ge(wexp_first, 48 * WRING)
            pe.wait_ge(hT_done, NT)
            pe.wait_ge(sh_done, NT)
            pe.wait_ge(route_step, ROUTE_STEPS * NB)
            pe.wait_ge(hraw_done, NT)
            pe.wait_ge(oT_done, 4 * NB)

            def rows_T(p):
                i, c = p[1] % 2, p[1] % GRING
                wait(pe, slots_in[c], nth_slot(p, GRING, 16, 16))
                wait(pe, gT_done, nth(p, 1, -1))
                for k in range(KD):
                    ins = nc.tensor.transpose(psG[i][:, k * P:(k + 1) * P], gx[:, c, k * P:(k + 1) * P], ident[:])
                ins.then_inc(gT_ps, 1)

            def gate_up(p):
                i, c = p[1] % 2, p[1] % WRING
                wait(pe, wexp_in[c], nth_slot(p, WRING, 48, 0))
                wait(pe, gT_done, nth(p, 1, 1))
                wait(pe, hid_done, nth(p, 1, -1))
                for k in range(KD):
                    for e in range(2):
                        ins = mm(psO[i][CAP * e:CAP * (e + 1), 0:2 * FI], gxT[:, i, k, CAP * e:CAP * (e + 1)],
                                 wgu[:, c, e, k], start=k == 0, stop=k == KD - 1)
                ins.then_inc(gu_ps, 1)

            def hidden_T(p):
                i = p[1] % 2
                wait(pe, hid_done, nth(p, 1, 1))
                wait(pe, hidT_done, nth(p, 1, -1))
                nc.tensor.transpose(psM[i][0:FI, 0:P], hid[:, i], ident[:]).then_inc(hidT_ps, 1)

            def down(p):
                i, c = p[1] % 2, p[1] % WRING
                wait(pe, hidT_done, nth(p, 1, 1))
                wait(pe, eo_low, nth(p, 1, -1))
                wait(pe, eo_high, nth(p, 1, -1))
                for e in range(2):
                    ins = mm(psE[i][CAP * e:CAP * (e + 1), 0:D], hidT[:, i, CAP * e:CAP * (e + 1)], wdn[:, c, e],
                             start=True, stop=True)
                ins.then_inc(dn_ps, 1)

            rows_T((None, 0))
            rows_T((None, 1))
            gate_up((None, 0))

            def pair(p):
                last = p[0] is None and p[1] >= NPAIR - 2
                if not last:
                    rows_T(later(p, 2))
                hidden_T(p)
                if not (last and p[1] == NPAIR - 1):
                    gate_up(later(p, 1))
                down(p)

            pair_steps(pe, pair)

            for n in range(NT):
                i, c = n % 2, n % RRING
                pe.wait_ge(routed_in[c], 16 * (n // RRING + 1))
                wait(pe, y_done, n - 1)
                if n < 2:
                    pe.wait_ge(eo_low, NPAIR)
                    pe.wait_ge(eo_high, NPAIR)
                mm(psE[i][:, 0:D], ident[:], x_all[:, n], start=True, stop=False)
                for j in range(3):
                    ins = mm(psE[i][:, 0:D], ident[:], routed[:, c, j], start=False, stop=j == 2)
                ins.then_inc(half_ps, 1)


def kernel(**inputs):
    import concourse.bacc as bacc
    from concourse.bass_utils import run_bass_kernel_spmd

    a = {name: np.asarray(x) for name, x in inputs.items()}

    def by_feature(w):
        return w.reshape(-1, 2, HH, DH).transpose(0, 1, 3, 2).reshape(-1, D)

    def halves(x):
        return x.reshape(2, P).T

    arrays = {
        "X": a["L0_attn_X"],
        "Wq": by_feature(a["L0_attn_Wq"]),
        "Wk": by_feature(a["L0_attn_Wk"]),
        "Wv": a["L0_attn_Wv"],
        "Wo": a["L0_attn_Wo"],
        "cols": np.concatenate([halves(a["L0_attn_ln_g"]), halves(a["L0_attn_ln_b"]),
                                halves(by_feature(a["L0_attn_bq"])), halves(by_feature(a["L0_attn_bk"]))], axis=1),
        "bias_row": np.stack([a["L0_attn_bv"], a["L0_attn_bo"]])[None],
        "Wgate": np.concatenate([a["L0_ffn_gate_w"], a["L0_ffn_shared_gate_w"], a["L0_ffn_shared_up_w"]]).T,
        "Wsd": a["L0_ffn_shared_down_w"].T,
        "gate_up": a["L0_ffn_gate_up_proj"],
        "down": a["L0_ffn_down_proj"],
    }
    arrays = {name: np.ascontiguousarray(x) for name, x in arrays.items()}

    nc = bacc.Bacc("TRN2", target_bir_lowering=False, num_devices=1)
    io = {name: nc.dram_tensor("in_" + name, x.shape, mybir.dt.from_np(x.dtype), kind="ExternalInput").ap()
          for name, x in arrays.items()}
    io["out"] = nc.dram_tensor("out", (NB, S, D), F32, kind="ExternalOutput").ap()
    moe_block_kernel(nc, io)
    r = run_bass_kernel_spmd(nc, [{"in_" + name: x for name, x in arrays.items()}], core_ids=[0])
    return r.results[0]["out"]
```

```python
from contextlib import ExitStack

import numpy as np

import concourse.bass as bass
from concourse import mybir

ALU = mybir.AluOpType
ACT = mybir.ActivationFunctionType
AX = mybir.AxisListType.X
F32 = mybir.dt.float32
BF16 = mybir.dt.bfloat16
U32 = mybir.dt.uint32

P = 128
D = 256
KD = D // P
NB = 8
S = 256
TILES = S // P
NT = NB * TILES
T = NB * S
NH = 16
DH = D // NH
HH = P // DH
E = 64
TOPK = 6
CAP = 64
FI = 96
SI = 2 * FI
NSLOT = E * CAP
NPAIR = E // 2
CLEARS = NSLOT // P // 8
EPS = 1e-5
Q_SCALE = DH ** -0.5
COPIES = ((0, 3), (3, 2), (5, 1))
STACK = 6 * DH
NEGMAX = 3
MASKED = -1e30
SENT = 2
C_PROB = D
C_SENT = C_PROB + E
C_SLOT = C_SENT + SENT
C_DEST = C_SLOT + 8
ROW = C_DEST + 8
AWAY = 65536.0
CHOOSE_STEPS = 11
ROUTE_STEPS = 18
WRING = 8
GRING = 4
RRING = 3


def moe_block_kernel(nc, io):
    with ExitStack() as ctx:
        def sb(name, shape, dt=F32):
            return ctx.enter_context(nc.sbuf_tensor(name, shape, dt))

        def sem(name):
            return ctx.enter_context(nc.semaphore(name))

        def sems(name, n):
            return [sem(f"{name}{i}") for i in range(n)]

        def dram(name, shape, dt=F32):
            return nc.dram_tensor(name, shape, dt, kind="Internal").ap()

        parts_d = dram("parts_d", (2, 4, 3, P, S), BF16)
        slots_d = dram("slots_d", (NSLOT, ROW))
        routed_d = dram("routed_d", (T * TOPK, D))

        ident = sb("ident", [P, P])
        ident_bf = sb("ident_bf", [P, P], BF16)
        before = sb("before", [P, P], BF16)
        ones_bf = sb("ones_bf", [P, P], BF16)
        upper = sb("upper", [P, P], BF16)
        lower = sb("lower", [P, P], BF16)
        slot_base = sb("slot_base", [P, TILES, E])
        neg_half = sb("neg_half", [P, TILES])
        own_slot = sb("own_slot", [P, 1])
        wq = sb("wq", [P, KD, D])
        wk = sb("wk", [P, KD, D])
        wv = sb("wv", [P, KD, D])
        wo = sb("wo", [P, NH // 4, D])
        wgate = sb("wgate", [P, KD, E + 2 * SI])
        wsd = sb("wsd", [FI, 2, D])
        cols = sb("cols", [P, 8])
        bias_row = sb("bias_row", [1, 2, D])
        bias_part = sb("bias_part", [1, 3, 2, D], BF16)
        bias_rest = sb("bias_rest", [1, 2, D])
        bias3 = sb("bias3", [3, 2, D], BF16)

        x_all = sb("x_all", [P, NT, D])
        stats1 = sb("stats1", [P, TILES, 6])
        mv1 = sb("mv1", [P, TILES, 2])
        ve1 = sb("ve1", [P, TILES])
        rstd1 = sb("rstd1", [P, TILES])
        xn = sb("xn", [P, TILES, D])
        xnT = sb("xnT", [P, KD, S])
        parts = sb("parts", [P, 4, 3, S], BF16)
        rest = sb("rest", [P, 4, S])
        qs = sb("qs", [STACK + NEGMAX, 2, NH, S], BF16)
        ks = sb("ks", [STACK + NEGMAX, 2, NH, S], BF16)
        vs = sb("vs", [P, 2, TILES, NH, 2 * DH])

        negmax = sb("negmax", [P, TILES, NH])
        negmax_rest = sb("negmax_rest", [P, TILES, NH])
        negmax_part = sb("negmax_part", [P, TILES, 3, NH], BF16)
        negmaxT = sb("negmaxT", [3 * NH, S], BF16)

        probs = sb("probs", [P, 2, 3 * 512])
        rowsum = sb("rowsum", [P, S])
        rinv = sb("rinv", [P, S])
        oT = sb("oT", [P, NH // 4, S])

        z = sb("z", [P, TILES, D])
        stats2 = sb("stats2", [P, TILES, 6])
        mv2 = sb("mv2", [P, TILES, 2])
        ve2 = sb("ve2", [P, TILES])
        rstd2 = sb("rstd2", [P, TILES])
        row = sb("row", [P, 2, TILES, ROW])
        x1T = sb("x1T", [P, KD, S])
        logits = sb("logits", [P, TILES, E])
        lmax = sb("lmax", [P, TILES])
        lexp = sb("lexp", [P, TILES, E])
        lsum = sb("lsum", [P, TILES])
        linv = sb("linv", [P, TILES])
        top8 = sb("top8", [P, TILES, 8])
        left = sb("left", [P, TILES, E + SENT])
        chosen = sb("chosen", [P, TILES, E], BF16)
        earlier = sb("earlier", [P, TILES, E], BF16)
        kept = sb("kept", [P, TILES, E])
        slot = sb("slot", [P, TILES, E])
        away = sb("away", [P, TILES, 8])
        slot_idx = sb("slot_idx", [P, 2, TILES, 8], U32)
        hraw = sb("hraw", [P, NT, 2 * SI])

        wgu = sb("wgu", [P, WRING, 2, KD, 2 * FI])
        wdn = sb("wdn", [FI, WRING, 2, D])
        zeros = sb("zeros", [P, 4 * ROW])
        h_gate = sb("h_gate", [P, 2, SI])
        h = sb("h", [P, 2, SI])
        hT = sb("hT", [FI, 2, 2, P])
        gate = sb("gate", [P, 2, FI])
        hid = sb("hid", [P, 2, FI])
        hidT = sb("hidT", [FI, 2, P])
        match = sb("match", [P, 8])
        found = sb("found", [P, 1])
        no_token = sb("no_token", [P, 1])
        dest_idx = sb("dest_idx", [P, GRING], U32)
        stats3 = sb("stats3", [P, 2, 6])
        mv3 = sb("mv3", [P, 2, 2])
        ve3 = sb("ve3", [P, 2])
        rstd3 = sb("rstd3", [P, 4])
        shift3 = sb("shift3", [P, 2])

        attend_flat = probs[:].rearrange("p a b -> p (a b)")
        gx = attend_flat[:, 0:GRING * ROW].rearrange("p (c r) -> p c r", c=GRING)
        eo = oT[:]
        gxT = z[:].rearrange("p i (k q) -> p i k q", k=KD)
        half_sum = xn[:]
        result = rest[:]
        weights_flat = wgu[:].rearrange("p n e k i -> p (n e k i)")
        routed = weights_flat[:, 0:RRING * TOPK * D].rearrange("p (c j d) -> p c j d", c=RRING, j=TOPK)
        y = weights_flat[:, RRING * TOPK * D:(RRING * TOPK + 4) * D].rearrange("p (c d) -> p c d", c=4)

        psM = [ctx.enter_context(nc.psum_tensor(f"psM{i}", [P, 512], F32)) for i in range(2)]
        psE = [ctx.enter_context(nc.psum_tensor(f"psE{i}", [P, 512], F32)) for i in range(2)]
        psO = [ctx.enter_context(nc.psum_tensor(f"psO{i}", [P, 512], F32)) for i in range(2)]
        psG = [ctx.enter_context(nc.psum_tensor(f"psG{i}", [P, 512], F32)) for i in range(2)]

        qk_bank = [psG[1], psO[0]]
        peak_bank = [psM[0], psM[1], psE[0], psE[1]]

        wq_in = sem("wq_in")
        wkv_in = sem("wkv_in")
        weights_in = sem("weights_in")
        small_in = sem("small_in")
        bias3_in = sem("bias3_in")
        filled = sem("filled")
        x_in = sems("x_in", 3)
        consts = sem("consts")
        pool_step = sem("pool_step")
        setup_v = sem("setup_v")
        route_init = sem("route_init")
        bias_split = sem("bias_split")
        stats1_done = sem("stats1_done")
        mv1_done = sem("mv1_done")
        ve1_done = sem("ve1_done")
        rstd1_done = sem("rstd1_done")
        xn_done = sem("xn_done")
        xT_ps = sem("xT_ps")
        xnT_done = sem("xnT_done")
        qk_ps = sem("qk_ps")
        part1_done = sem("part1_done")
        rest_done = sem("rest_done")
        part2_done = sem("part2_done")
        part3_done = sem("part3_done")
        v_ps = sem("v_ps")
        vs_done = sem("vs_done")
        parts_out = sems("parts_out", 2)
        stack_in = sems("stack_in", 2)
        peak_ps = sem("peak_ps")
        peak_read = sem("peak_read")
        negmax_step = sem("negmax_step")
        negmaxT_ps = sem("negmaxT_ps")
        negmaxT_done = sem("negmaxT_done")
        negmax_in = sems("negmax_in", 2)
        score_ps = sem("score_ps")
        exp_done = sem("exp_done")
        pv_ps = sem("pv_ps")
        rowsum_done = sem("rowsum_done")
        rinv_done = sem("rinv_done")
        oT_done = sem("oT_done")
        wo_ps = sem("wo_ps")
        z_done = sem("z_done")
        stats2_done = sem("stats2_done")
        mv2_done = sem("mv2_done")
        ve2_done = sem("ve2_done")
        rstd2_done = sem("rstd2_done")
        x1_done = sem("x1_done")
        x1T_ps = sem("x1T_ps")
        x1T_done = sem("x1T_done")
        gate_ps = sem("gate_ps")
        logits_done = sem("logits_done")
        hraw_done = sem("hraw_done")
        route_step = sem("route_step")
        lexp_done = sem("lexp_done")
        rank_ps = sem("rank_ps")
        rank_read = sem("rank_read")
        x1_kept = sem("x1_kept")
        sent = sems("sent", 2)
        h_silu = sem("h_silu")
        h_done = sem("h_done")
        hT_ps = sem("hT_ps")
        hT_done = sem("hT_done")
        sd_ps = sem("sd_ps")
        sh_done = sem("sh_done")
        dest_cols = sem("dest_cols")
        slots_in = sems("slots_in", GRING)
        wexp_first = sem("wexp_first")
        wexp_in = sems("wexp_in", WRING)
        gT_ps = sem("gT_ps")
        gT_done = sem("gT_done")
        gu_ps = sem("gu_ps")
        silu_done = sem("silu_done")
        hid_done = sem("hid_done")
        hidT_ps = sem("hidT_ps")
        hidT_done = sem("hidT_done")
        dn_ps = sem("dn_ps")
        eo_low = sem("eo_low")
        eo_high = sem("eo_high")
        dest_step = sem("dest_step")
        dest_done = sem("dest_done")
        eo_out = sems("eo_out", GRING)
        routed_in = sems("routed_in", RRING)
        half_ps = sem("half_ps")
        half_done = sem("half_done")
        y_done = sem("y_done")
        stats3_done = sem("stats3_done")
        mv3_done = sem("mv3_done")
        ve3_done = sem("ve3_done")
        rstd3_done = sem("rstd3_done")
        shift3_done = sem("shift3_done")
        result_done = sem("result_done")
        out_out = sems("out_out", 4)


        def count(b, per, k):
            it, c = b
            v = per * c + k
            return v if it is None else it * (2 * per) + v

        def count_half(b, per, k):
            it, c = b
            v = per * (c // 2) + k
            return v if it is None else it * per + v

        def wait(eng, s, value):
            if isinstance(value, int) and value <= 0:
                return
            eng.wait_ge(s, value)

        def wait_alone(eng, s, value):
            if isinstance(value, int) and value <= 0:
                return
            eng.wait_ge(s, value)
            if not isinstance(value, int):
                eng.nop(nofuse=True)

        def later(b, n):
            return (b[0], b[1] + n)

        def par(b):
            return b[1] % 2

        def tile_of(b, t):
            return count(b, TILES, t)

        def run(eng, step):
            def at(it, i):
                step(*[(it, b) if 0 <= b < NB else None for b in (i + 1, i, i - 1, i - 2)])
            for i in range(-1, 2):
                at(None, i)
            with eng.Fori(0, 2) as it:
                for i in range(2, 4):
                    at(it, i)
            for i in range(NB - 2, NB + 2):
                at(None, i)

        def tile_steps(eng, first, second):
            def ahead(b, t):
                first(*((b, 1) if t == 0 else (later(b, 1), 0)))
                second(b, t)

            first((None, 0), 0)
            for c in range(2):
                for t in range(TILES):
                    ahead((None, c), t)
            with eng.Fori(0, NB // 2 - 2) as it:
                for c in (2, 3):
                    for t in range(TILES):
                        ahead((it, c), t)
            for c in range(NB - 2, NB):
                for t in range(TILES):
                    if (c, t) == (NB - 1, TILES - 1):
                        second((None, c), t)
                    else:
                        ahead((None, c), t)

        def pair_steps(eng, step):
            for c in range(WRING):
                step((None, c))
            with eng.Fori(0, NPAIR // WRING - 2) as it:
                for c in range(WRING, 2 * WRING):
                    step((it, c))
            for c in range(NPAIR - WRING, NPAIR):
                step((None, c))

        def nth(p, per, k):
            it, c = p
            v = per * c + k
            return v if it is None else it * (WRING * per) + v

        def nth_slot(p, ring, per, k):
            it, c = p
            v = per * (c // ring) + k
            return v if it is None else it * (WRING // ring * per) + v

        block = ctx.enter_context(nc.Block())

        @block.sync
        def _(sp):
            x_rows = io["X"].rearrange("b (t p) d -> p (b t) d", p=P)
            sp.dma_start(x_all[:, 0:TILES], x_rows[:, 0:TILES]).then_inc(x_in[0], 16)
            sp.dma_start(cols[:], io["cols"]).then_inc(small_in, 16)
            sp.dma_start(bias_row[:], io["bias_row"]).then_inc(small_in, 16)
            for w, name, s in ((wq, "Wq", wq_in), (wk, "Wk", wkv_in), (wv, "Wv", wkv_in)):
                sp.dma_start(w[:], io[name].rearrange("(k p) n -> p k n", p=P)).then_inc(s, 16)
            sp.dma_start(x_all[:, TILES:2 * TILES], x_rows[:, TILES:2 * TILES]).then_inc(x_in[1], 16)
            sp.dma_start(wgate[:], io["Wgate"].rearrange("(k p) n -> p k n", p=P)).then_inc(weights_in, 16)
            sp.dma_start(wsd[:], io["Wsd"].rearrange("(k p) n -> p k n", p=FI)).then_inc(weights_in, 16)
            sp.wait_ge(setup_v, 1)
            wo_rows = io["Wo"].rearrange("(g j d) n -> j d g n", j=4, d=DH)
            for j in range(4):
                sp.dma_start(wo[32 * j:32 * j + DH], wo_rows[j]).then_inc(weights_in, 16)
            sp.dma_start(x_all[:, 2 * TILES:], x_rows[:, 2 * TILES:]).then_inc(x_in[2], 16)
            sp.wait_ge(bias_split, 5)
            for c in range(3):
                sp.dma_start(bias3[c:c + 1], bias_part[0:1, c]).then_inc(bias3_in, 16)

            def write_parts(b):
                wait_alone(sp, stack_in[par(b)], count_half(b, 16 * 12, 0))
                wait_alone(sp, part3_done, count(b, 2, 2))
                sp.dma_start(parts_d[par(b)].rearrange("m c p t -> p (m c) t"),
                             parts[:].rearrange("p m c t -> p (m c) t")).then_inc(parts_out[par(b)], 16)

            def stack(b):
                wait_alone(sp, parts_out[par(b)], count_half(b, 16, 16))
                wait_alone(sp, score_ps, count(b, 12, -12))
                src = parts_d[par(b)].rearrange("m c (d h) t -> m (c d) (h t)", h=HH)
                for m in range(2):
                    heads = slice(HH * m, HH * m + HH)
                    for part, (c0, n) in enumerate(COPIES):
                        sp.dma_start(qs[DH * c0:DH * (c0 + n), par(b), heads, :],
                                     src[m, 0:DH * n]).then_inc(stack_in[par(b)], 16)
                        sp.dma_start(ks[DH * c0:DH * (c0 + n), par(b), heads, :],
                                     src[2 + m, DH * part:DH * (part + 1)].unsqueeze(0).broadcast_to(
                                         (n, DH, HH * S))).then_inc(stack_in[par(b)], 16)

            def negmax_rows(b):
                wait_alone(sp, negmaxT_done, count(b, 1, 1))
                for c in range(3):
                    sp.dma_start(qs[STACK + c:STACK + c + 1, par(b)],
                                 negmaxT[NH * c:NH * (c + 1), :]).then_inc(negmax_in[par(b)], 16)

            def step(f, m, a, r):
                if m:
                    negmax_rows(m)
                if f:
                    write_parts(f)
                    stack(f)

            run(sp, step)

            for i in range(2):
                sp.wait_ge(sent[i], 16 * CLEARS + 16 * 6 * TILES * NB // 2)

            slot_rows = slots_d.rearrange("(n p) r -> p n r", p=P)
            gu_rows = io["gate_up"].rearrange("(n e) (k p) i -> n p e k i", e=2, p=P)
            dn_rows = io["down"].rearrange("(n e) i d -> n i e d", e=2)

            def load_pair(p):
                c = p[1] % GRING
                wait_alone(sp, eo_low, nth(p, 1, 1 - GRING))
                wait_alone(sp, eo_high, nth(p, 1, 1 - GRING))
                wait_alone(sp, dest_done, nth(p, 1, 1 - GRING))
                sp.dma_start(gx[:, c], slot_rows[:, bass.ds(nth(p, 1, 0), 1)].rearrange(
                    "p o r -> p (o r)")).then_inc(slots_in[c], 16)

            def load_weights(p):
                c, n = p[1] % WRING, nth(p, 1, 0)
                wait_alone(sp, dn_ps, nth(p, 1, 1 - WRING))
                for e in range(2):
                    sp.dma_start(wgu[:, c, e], gu_rows[bass.ds(n, 1), :, e].rearrange(
                        "o p k i -> p (o k) i")).then_inc(wexp_in[c], 16)
                sp.dma_start(wdn[:, c], dn_rows[bass.ds(n, 1)].rearrange("o i e d -> i (o e) d")).then_inc(
                    wexp_in[c], 16)

            def load(p):
                if p[1] >= WRING:
                    load_weights(p)
                load_pair(p)

            pair_steps(sp, load)

            for c in range(GRING):
                sp.wait_ge(eo_out[c], 16 * NPAIR // GRING)
            routed_rows = routed_d.rearrange("(n p j) d -> n p j d", p=P, j=TOPK)
            out_rows = io["out"].rearrange("b (t p) d -> (b t) p d", p=P)
            for n in range(NT):
                c = n % RRING
                wait_alone(sp, y_done, n - RRING + 1)
                sp.dma_start(routed[:, c], routed_rows[n]).then_inc(routed_in[c], 16)
                if n >= 2:
                    sp.wait_ge(result_done, n - 1)
                    sp.dma_start(out_rows[n - 2], result[:, (n - 2) % 4]).then_inc(out_out[(n - 2) % 4], 16)
            for n in range(NT - 2, NT):
                sp.wait_ge(result_done, n + 1)
                sp.dma_start(out_rows[n], result[:, n % 4]).then_inc(out_out[n % 4], 16)
            for c in range(4):
                sp.wait_ge(out_out[c], 16 * NT // 4)

        @block.gpsimd
        def _(pool):
            g = nc.gpsimd
            def power_in(b):
                wait_alone(pool, mv1_done, count(b, TILES, TILES))
                g.tensor_scalar(ve1[:], mv1[:, :, 1], EPS, None, ALU.add).then_inc(ve1_done, 1)
                wait(pool, ve1_done, count(b, 1, 1))
                g.tensor_tensor(rstd1[:], ve1[:], neg_half[:], ALU.pow).then_inc(rstd1_done, 1)

            g.memset(zeros[:], 0.0).then_inc(pool_step, 1)
            g.memset(ident[:], 0.0).then_inc(pool_step, 1)
            g.memset(before[:], 1.0).then_inc(pool_step, 1)
            g.memset(upper[:], 0.0).then_inc(pool_step, 1)
            g.memset(neg_half[:], -0.5).then_inc(consts, 1)
            g.memset(ones_bf[:], 1.0).then_inc(consts, 1)
            g.memset(lower[:], 0.0).then_inc(pool_step, 1)
            pool.wait_ge(pool_step, 5)
            g.affine_select(ident[:], ident[:], [[-1, P]], ALU.not_equal, 1.0, base=0,
                            channel_multiplier=1).then_inc(consts, 1)
            g.affine_select(before[:], before[:], [[1, P]], ALU.is_gt, 0.0, base=0,
                            channel_multiplier=-1).then_inc(consts, 1)
            g.affine_select(upper[:], upper[:], [[-1, P]], ALU.is_ge, MASKED, base=0,
                            channel_multiplier=1).then_inc(consts, 1)
            g.affine_select(lower[:], lower[:], [[1, P]], ALU.is_ge, MASKED, base=0,
                            channel_multiplier=-1).then_inc(consts, 1)
            g.iota(slot_base[:], [[0, TILES], [CAP, E]], base=1, channel_multiplier=0,
                   allow_small_or_imprecise_dtypes=True).then_inc(consts, 1)
            g.iota(own_slot[:], [[0, 1]], base=1 - P, channel_multiplier=1,
                   allow_small_or_imprecise_dtypes=True).then_inc(consts, 1)
            for i in range(2):
                g.iota(row[:, i, :, C_DEST:C_DEST + 8], [[TOPK * P, TILES], [1, 8]],
                       base=1 + (i - 2) * TOPK * S, channel_multiplier=TOPK,
                       allow_small_or_imprecise_dtypes=True).then_inc(consts, 1)
            power_in((None, 0))
            slots_flat = slots_d.rearrange("(p n) r -> p (n r)", p=P)
            routed_flat = routed_d.rearrange("(p n) d -> p (n d)", p=P)
            routed_piece = T * TOPK // P * D // NB
            blank = 4 * D
            gu_rows = io["gate_up"].rearrange("(n e) (k p) i -> n p e k i", e=2, p=P)
            dn_rows = io["down"].rearrange("(n e) i d -> n i e d", e=2)

            def background(b):
                it, c = b
                n = count(b, 1, 0)
                for e in range(2):
                    pool.dma_start(wgu[:, bass.ds(n, 1), e].rearrange("p o k i -> p (o k) i"),
                                   gu_rows[bass.ds(n, 1), :, e].rearrange("o p k i -> p (o k) i")
                                   ).then_inc(wexp_first, 16)
                pool.dma_start(wdn[:, bass.ds(n, 1)].rearrange("p o e d -> p (o e) d"),
                               dn_rows[bass.ds(n, 1)].rearrange("o i e d -> i (o e) d")).then_inc(wexp_first, 16)
                pool.dma_start(routed_flat[:, bass.ds(n * routed_piece, routed_piece)].rearrange(
                    "p (n w) -> p n w", w=blank), zeros[:, 0:blank].unsqueeze(1).broadcast_to(
                        (P, routed_piece // blank, blank))).then_inc(filled, 16)

            def clear_slots(i):
                for n in range(CLEARS * i, CLEARS * (i + 1)):
                    pool.dma_start(slots_flat[:, n * 4 * ROW:(n + 1) * 4 * ROW], zeros[:]).then_inc(sent[n % 2], 16)

            def power_mid(b):
                wait_alone(pool, mv2_done, count(b, TILES, TILES))
                g.tensor_scalar(ve2[:], mv2[:, :, 1], EPS, None, ALU.add).then_inc(ve2_done, 1)
                wait(pool, ve2_done, count(b, 1, 1))
                g.tensor_tensor(rstd2[:], ve2[:], neg_half[:], ALU.pow).then_inc(rstd2_done, 1)

            def dispatch(b, t):
                if t == 0:
                    wait_alone(pool, sent[par(b)], count_half(b, 16 * 6 * TILES, 16 * CLEARS))
                    dest = row[:, par(b), :, C_DEST:C_DEST + 8]
                    g.tensor_scalar(dest, dest, float(2 * TOPK * S), None, ALU.add).then_inc(dest_cols, 1)
                    wait_alone(pool, dest_cols, count(b, 1, 1))
                    wait_alone(pool, x1_done, count(b, TILES, TILES))
                    wait_alone(pool, route_step, count(b, ROUTE_STEPS, ROUTE_STEPS))
                for j in range(TOPK):
                    g.indirect_dma_start(
                        out=slots_d, out_offset=bass.IndirectOffsetOnAxis(
                            ap=slot_idx[:, par(b), t, j:j + 1], axis=0),
                        in_=row[:, par(b), t, :], in_offset=None, bounds_check=NSLOT - 1,
                        oob_is_err=False).then_inc(sent[par(b)], 16)

            def step(f, m, a, r):
                if f and (f[0] is not None or f[1] > 0):
                    power_in(f)
                if m:
                    background(m)
                if a:
                    power_mid(a)
                if r:
                    dispatch(r, 0)
                    dispatch(r, 1)
                if f and f[0] is None and f[1] < 2:
                    clear_slots(f[1])
                if f and f[0] is None and f[1] == 2:
                    for i in range(2):
                        pool.wait_ge(sent[i], 16 * CLEARS)

            run(pool, step)
            pool.wait_ge(filled, 16 * NB)

            def scatter(p):
                c = p[1] % GRING
                wait_alone(pool, eo_low, nth(p, 1, 1))
                wait_alone(pool, eo_high, nth(p, 1, 1))
                wait_alone(pool, dest_done, nth(p, 1, 1))
                g.indirect_dma_start(out=routed_d, out_offset=bass.IndirectOffsetOnAxis(
                    ap=dest_idx[:, c:c + 1], axis=0), in_=eo[:, c], in_offset=None,
                    bounds_check=T * TOPK - 1, oob_is_err=False).then_inc(eo_out[c], 16)

            pair_steps(pool, scatter)

            for n in range(NT):
                i = n % 2
                pool.wait_ge(mv3_done, n + 1)
                g.tensor_scalar(ve3[:, i:i + 1], mv3[:, i, 1:2], EPS, None, ALU.add).then_inc(ve3_done, 1)
                pool.wait_ge(ve3_done, n + 1)
                g.tensor_tensor(rstd3[:, n % 4:n % 4 + 1], ve3[:, i:i + 1], neg_half[:, 0:1], ALU.pow).then_inc(
                    rstd3_done, 1)

        @block.scalar
        def _(act):
            s = nc.scalar
            act.wait_ge(small_in, 32)

            def transpose_out(b):
                wait(act, xT_ps, count(b, 1, 1))
                wait(act, v_ps, count(b, 1, 0))
                for k in range(KD):
                    s.activation(xnT[:, k], psM[0][:, k * S:(k + 1) * S], ACT.Identity,
                                 bias=cols[:, 2 + k:3 + k], scale=cols[:, k:k + 1]).then_inc(xnT_done, 1)

            def part1(b, i):
                if i == 0:
                    if b[0] is None and b[1] == 0:
                        act.wait_ge(setup_v, 3)
                    before_b = later(b, -1)
                    if before_b[0] is not None or before_b[1] >= 0:
                        wait(act, parts_out[par(before_b)], count_half(before_b, 16, 16))
                wait(act, qk_ps, count(b, 2, i + 1))
                for m in range(2):
                    s.activation(parts[:, 2 * i + m, 0], qk_bank[i][:, m * S:(m + 1) * S], ACT.Identity,
                                 bias=cols[:, 4 + 2 * i + m:5 + 2 * i + m]).then_inc(part1_done, 1)

            def part2(b, i):
                wait(act, rest_done, count(b, 4, 2 * i + 2))
                s.copy(parts[:, 2 * i:2 * i + 2, 1], rest[:, 2 * i:2 * i + 2]).then_inc(part2_done, 1)

            def values(b):
                wait(act, v_ps, count(b, 1, 1))
                wait(act, pv_ps, count(b, 4, -4))
                s.copy(vs[:, par(b), :, :, 0:DH],
                       psG[1][:].rearrange("p (t h d) -> p t h d", t=TILES, h=NH)).then_inc(vs_done, 1)

            def exponents(b, lo, hi):
                for u in range(lo, hi):
                    grp, j = divmod(u, 3)
                    wait(act, score_ps, count(b, 12, u + 1))
                    if j == 0:
                        wait(act, pv_ps, count(b, 4, max(grp - 1, 0)))
                    s.activation(probs[:, grp % 2, 512 * j:512 * (j + 1)], psE[u % 2][:],
                                 ACT.Exp).then_inc(exp_done, 1)

            def negmax_out(b):
                wait(act, negmaxT_ps, count(b, 1, 1))
                prev = later(b, -1)
                if prev[0] is not None or prev[1] >= 0:
                    wait(act, negmax_in[par(prev)], count_half(prev, 48, 48))
                s.copy(negmaxT[:], psO[1][0:3 * NH, 0:S // 2].bitcast(BF16)).then_inc(negmaxT_done, 1)

            def x1T_out(b):
                wait(act, x1T_ps, count(b, 1, 1))
                wait(act, gate_ps, count(b, 2, 0))
                s.copy(x1T[:].rearrange("p k t -> p (k t)"), psG[0][:]).then_inc(x1T_done, 1)

            def gate_out(b):
                for t in range(TILES):
                    wait(act, gate_ps, count(b, 2, t + 1))
                    wait(act, route_step, count(b, ROUTE_STEPS, 0))
                    s.copy(logits[:, t], psG[1 - t][:, 0:E]).then_inc(logits_done, 1)
                    s.copy(hraw[:, bass.ds(tile_of(b, t), 1)].rearrange("p o n -> p (o n)"),
                           psG[1 - t][:, E:E + 2 * SI]).then_inc(hraw_done, 1)

            def keep_x1(b):
                wait(act, x1_done, count(b, TILES, TILES))
                s.copy(x_all[:, bass.ds(tile_of(b, 0), TILES)], row[:, par(b), :, 0:D]).then_inc(x1_kept, 1)

            def router_exp(b):
                wait(act, route_step, count(b, ROUTE_STEPS, 2))
                s.activation(lexp[:], lexp[:], ACT.Exp).then_inc(lexp_done, 1)

            def step(f, m, a, r):
                if r:
                    router_exp(r)
                if a:
                    exponents(a, 0, 8)
                if f:
                    transpose_out(f)
                if r:
                    keep_x1(r)
                if a:
                    exponents(a, 8, 12)
                if f:
                    part1(f, 0)
                    part1(f, 1)
                    part2(f, 0)
                if a:
                    x1T_out(a)
                if f:
                    values(f)
                if m:
                    negmax_out(m)
                if f:
                    part2(f, 1)
                if a:
                    gate_out(a)

            run(act, step)

            act.wait_ge(hraw_done, NT)

            def shared(b, t):
                wait(act, h_done, count(b, TILES, t - 1))
                s.activation(h_gate[:, t], hraw[:, bass.ds(tile_of(b, t), 1), 0:SI].rearrange("p o n -> p (o n)"),
                             ACT.Silu).then_inc(h_silu, 1)

            def shared_T(b, t):
                wait(act, hT_ps, count(b, TILES, t + 1))
                wait(act, sd_ps, count(b, TILES, t - 1))
                s.copy(hT[:, t].rearrange("p c q -> p (c q)"), psM[t][0:FI, 0:2 * P]).then_inc(hT_done, 1)

            tile_steps(act, shared, shared_T)

            def rows_T(p):
                i = p[1] % 2
                wait(act, gT_ps, nth(p, 1, 1))
                wait(act, gu_ps, nth(p, 1, -1))
                s.copy(gxT[:, i].rearrange("p k q -> p (k q)"), psG[i][:, 0:D]).then_inc(gT_done, 1)

            def gates(p):
                i = p[1] % 2
                wait(act, gu_ps, nth(p, 1, 1))
                wait(act, hid_done, nth(p, 1, -1))
                s.activation(gate[:, i], psO[i][:, 0:FI], ACT.Silu).then_inc(silu_done, 1)

            def outputs_high(p):
                i, c = p[1] % 2, p[1] % GRING
                wait(act, dn_ps, nth(p, 1, 1))
                wait(act, eo_out[c], nth_slot(p, GRING, 16, 0))
                s.activation(eo[CAP:2 * CAP, c], psE[i][CAP:2 * CAP, 0:D], ACT.Copy,
                             scale=gx[CAP:2 * CAP, c, bass.ds(nth(p, 2, C_PROB + 1), 1)]).then_inc(eo_high, 1)

            rows_T((None, 0))
            rows_T((None, 1))
            gates((None, 0))

            def pair(p):
                last = p[0] is None and p[1] >= NPAIR - 2
                if not last:
                    rows_T(later(p, 2))
                if not (last and p[1] == NPAIR - 1):
                    gates(later(p, 1))
                outputs_high(p)

            pair_steps(act, pair)

            for n in range(NT):
                i = n % 2
                act.wait_ge(shift3_done, n + 1)
                wait(act, out_out[n % 4], 16 * (n // 4))
                s.activation(result[:, n % 4], y[:, n % 4], ACT.Identity, bias=shift3[:, i:i + 1],
                             scale=rstd3[:, n % 4:n % 4 + 1]).then_inc(result_done, 1)

        @block.vector
        def _(dve):
            v = nc.vector

            def x_tiles(b, t=None):
                if t is None:
                    return x_all[:, bass.ds(tile_of(b, 0), TILES)]
                return x_all[:, bass.ds(tile_of(b, t), 1)].rearrange("p o d -> p (o d)")

            def stats_in(b):
                wait(dve, x_in[min(b[1], 2)], 16)
                for t in range(TILES):
                    v.bn_stats(stats1[:, t], x_tiles(b, t)).then_inc(stats1_done, 1)
                wait_alone(dve, stats1_done, count(b, TILES, TILES))
                for t in range(TILES):
                    v.bn_aggr(mv1[:, t], stats1[:, t]).then_inc(mv1_done, 1)

            stats_in((None, 0))
            v.memset(wo[:], 0.0).then_inc(setup_v, 1)
            v.memset(vs[:], 1.0).then_inc(setup_v, 1)
            v.memset(earlier[:], 0.0).then_inc(route_init, 1)
            v.memset(row[:, :, :, C_SENT:C_SENT + SENT], 2.0).then_inc(rank_read, 1)
            dve.wait_ge(small_in, 32)
            v.tensor_scalar(cols[:, 4:6], cols[:, 4:6], Q_SCALE, None, ALU.mult).then_inc(setup_v, 1)
            rest_row = bias_rest[:]
            v.tensor_copy(bias_part[:, 0], bias_row[:]).then_inc(bias_split, 1)
            dve.wait_ge(bias_split, 1)
            v.tensor_tensor(rest_row, bias_row[:], bias_part[:, 0], ALU.subtract).then_inc(bias_split, 1)
            dve.wait_ge(bias_split, 2)
            v.tensor_copy(bias_part[:, 1], rest_row).then_inc(bias_split, 1)
            dve.wait_ge(bias_split, 3)
            v.tensor_tensor(rest_row, rest_row, bias_part[:, 1], ALU.subtract).then_inc(bias_split, 1)
            dve.wait_ge(bias_split, 4)
            v.tensor_copy(bias_part[:, 2], rest_row).then_inc(bias_split, 1)
            dve.wait_ge(consts, 10)
            v.tensor_copy(ident_bf[:], ident[:]).then_inc(setup_v, 1)
            dve.wait_ge(wq_in, 16)
            v.tensor_scalar(wq[:], wq[:], Q_SCALE, None, ALU.mult).then_inc(setup_v, 1)

            def norm_in(b):
                wait(dve, rstd1_done, count(b, 1, 1))
                wait(dve, xT_ps, count(b, 1, 0))
                for t in range(TILES):
                    v.tensor_scalar(xn[:, t], x_tiles(b, t), mv1[:, t, 0:1], rstd1[:, t:t + 1],
                                    ALU.subtract, ALU.mult).then_inc(xn_done, 1)

            def rest_of(b, i):
                for m in range(2):
                    mm = 2 * i + m
                    wait(dve, part1_done, count(b, 4, 2 * i + 2))
                    v.scalar_tensor_tensor(rest[:, mm], qk_bank[i][:, m * S:(m + 1) * S],
                                           cols[:, 4 + mm:5 + mm], parts[:, mm, 0], ALU.add,
                                           ALU.subtract).then_inc(rest_done, 1)

            def part3(b, i):
                wait(dve, part2_done, count(b, 2, i + 1))
                two = slice(2 * i, 2 * i + 2)
                v.tensor_tensor(parts[:, two, 2], rest[:, two], parts[:, two, 1], ALU.subtract).then_inc(part3_done, 1)

            def maxima(b, lo, hi):
                for u in range(lo, hi):
                    wait(dve, peak_ps, count(b, 12, u + 1))
                    if u < 4:
                        out, src = negmax[:, 0, 4 * u:4 * u + 4], peak_bank[u % 4][:].rearrange("p (h k) -> p h k", h=4)
                    else:
                        w = u - 4
                        out, src = negmax[:, 1, 2 * w:2 * w + 2], peak_bank[u % 4][:].rearrange("p (h k) -> p h k", h=2)
                    v.tensor_reduce(out, src, AX, ALU.max, negate=True).then_inc(peak_read, 1)

            def negmax_split(b):
                wait(dve, peak_read, count(b, 12, 12))
                wait(dve, negmaxT_ps, count(b, 1, 0))
                v.tensor_copy(negmax_part[:, :, 0], negmax[:]).then_inc(negmax_step, 1)
                wait(dve, negmax_step, count(b, 4, 1))
                v.tensor_tensor(negmax_rest[:], negmax[:], negmax_part[:, :, 0], ALU.subtract).then_inc(
                    negmax_step, 1)
                wait(dve, negmax_step, count(b, 4, 2))
                v.tensor_copy(negmax_part[:, :, 1], negmax_rest[:]).then_inc(negmax_step, 1)
                wait(dve, negmax_step, count(b, 4, 3))
                v.tensor_tensor(negmax_part[:, :, 2], negmax_rest[:], negmax_part[:, :, 1],
                                ALU.subtract).then_inc(negmax_step, 1)

            SUM_ROWS = [DH + i % DH for i in range(2 * DH)]

            def normalise(b, grp):
                if grp == 0:
                    wait_alone(dve, wo_ps, count(b, 1, 0))
                wait_alone(dve, pv_ps, count(b, 4, grp + 1))
                v.stream_shuffle(rowsum[:], psO[grp % 2][:, 0:S], SUM_ROWS).then_inc(rowsum_done, 1)
                wait(dve, rowsum_done, count(b, 4, grp + 1))
                v.reciprocal(rinv[:], rowsum[:]).then_inc(rinv_done, 1)
                wait(dve, rinv_done, count(b, 4, grp + 1))
                v.tensor_tensor(oT[:, grp], psO[grp % 2][:, 0:S], rinv[:], ALU.mult).then_inc(oT_done, 1)

            def norm_mid(b):
                wait(dve, wo_ps, count(b, 1, 1))
                v.tensor_tensor(z[:], psG[0][:].rearrange("p (t d) -> p t d", t=TILES), x_tiles(b),
                                ALU.add).then_inc(z_done, 1)
                wait(dve, z_done, count(b, 1, 1))
                for t in range(TILES):
                    v.bn_stats(stats2[:, t], z[:, t]).then_inc(stats2_done, 1)
                wait_alone(dve, stats2_done, count(b, TILES, TILES))
                for t in range(TILES):
                    v.bn_aggr(mv2[:, t], stats2[:, t]).then_inc(mv2_done, 1)

            def norm_mid_end(b):
                wait(dve, rstd2_done, count(b, 1, 1))
                wait(dve, sent[par(b)], count_half(b, 16 * 6 * TILES, 16 * CLEARS))
                wait(dve, x1_kept, count(b, 1, -1))
                for t in range(TILES):
                    v.tensor_scalar(row[:, par(b), t, 0:D], z[:, t], mv2[:, t, 0:1], rstd2[:, t:t + 1],
                                    ALU.subtract, ALU.mult).then_inc(x1_done, 1)

            def route_signals(b, done):
                def chained(ins):
                    done[0] += 1
                    ins.then_inc(route_step, 1)
                    wait_alone(dve, route_step, count(b, ROUTE_STEPS, done[0]))

                def loose(ins):
                    done[0] += 1
                    ins.then_inc(route_step, 1)

                return chained, loose

            def choose(b):
                r = row[:, par(b)]
                chained, loose = route_signals(b, [0])

                wait(dve, logits_done, count(b, TILES, TILES))
                chained(v.reduce_max(lmax[:], logits[:], AX))
                loose(v.tensor_tensor(lexp[:], logits[:], lmax[:].unsqueeze(2).broadcast_to((P, TILES, E)),
                                      ALU.subtract))
                wait(dve, lexp_done, count(b, 1, 1))
                chained(v.reduce_sum(lsum[:], lexp[:], AX))
                chained(v.reciprocal(linv[:], lsum[:]))
                chained(v.tensor_tensor(r[:, :, C_PROB:C_PROB + E], lexp[:],
                                        linv[:].unsqueeze(2).broadcast_to((P, TILES, E)), ALU.mult))
                loose(v.max(top8[:, 0], r[:, 0, C_PROB:C_SENT + SENT]))
                chained(v.max(top8[:, 1], r[:, 1, C_PROB:C_SENT + SENT]))
                loose(v.match_replace(left[:, 0], top8[:, 0], r[:, 0, C_PROB:C_SENT + SENT], -1.0))
                chained(v.match_replace(left[:, 1], top8[:, 1], r[:, 1, C_PROB:C_SENT + SENT], -1.0))
                chained(v.tensor_scalar(chosen[:], left[:, :, 0:E], 0.0, None, ALU.is_lt))
                loose(v.tensor_tensor(earlier[:, 1], earlier[:, 0], chosen[:, 0], ALU.add))

            def read_ranks(b):
                _, loose = route_signals(b, [CHOOSE_STEPS])
                wait(dve, rank_ps, count(b, 1, 1))
                rank = psG[1][:, 0:TILES * E].rearrange("p (t e) -> p t e", t=TILES)
                loose(v.scalar_tensor_tensor(kept[:], rank, float(CAP), chosen[:], ALU.is_lt, ALU.mult))
                v.tensor_tensor(slot[:], rank, slot_base[:], ALU.add).then_inc(rank_read, 1)

            def place(b):
                r = row[:, par(b)]
                chained, loose = route_signals(b, [CHOOSE_STEPS + 1])
                wait_alone(dve, rank_read, count(b, 1, 2))
                loose(v.tensor_tensor(earlier[:, 0], earlier[:, 1], chosen[:, 1], ALU.add))
                chained(v.tensor_tensor(slot[:], slot[:], kept[:], ALU.mult))
                loose(v.max(r[:, 0, C_SLOT:C_SLOT + 8], slot[:, 0]))
                chained(v.max(r[:, 1, C_SLOT:C_SLOT + 8], slot[:, 1]))
                chained(v.tensor_scalar(away[:], r[:, :, C_SLOT:C_SLOT + 8], 0.0, AWAY, ALU.is_equal, ALU.mult))
                loose(v.scalar_tensor_tensor(slot_idx[:, par(b)], r[:, :, C_SLOT:C_SLOT + 8], -1.0, away[:],
                                             ALU.add, ALU.add))

            def step(f, m, a, r):
                if f:
                    if f[0] is not None or f[1] > 0:
                        stats_in(f)
                if r:
                    choose(r)
                if f:
                    norm_in(f)
                if f and f[0] is None and f[1] == 0:
                    v.memset(ks[STACK:STACK + NEGMAX], 1.0).then_inc(setup_v, 1)
                if a:
                    for grp in range(3):
                        normalise(a, grp)
                if r:
                    read_ranks(r)
                if a:
                    normalise(a, 3)
                if m:
                    maxima(m, 0, 4)
                if f:
                    rest_of(f, 0)
                if r:
                    place(r)
                if a:
                    norm_mid(a)
                if m:
                    maxima(m, 4, 6)
                if a:
                    norm_mid_end(a)
                if m:
                    maxima(m, 6, 12)
                    negmax_split(m)
                if f:
                    rest_of(f, 1)
                    part3(f, 0)
                    part3(f, 1)

            dve.wait_ge(route_init, 1)
            dve.wait_ge(rank_read, 1)
            run(dve, step)

            dve.wait_ge(x1_kept, NB)

            def shared(b, t):
                wait(dve, h_silu, count(b, TILES, t + 1))
                wait(dve, hT_ps, count(b, TILES, t - 1))
                v.tensor_tensor(h[:, t], h_gate[:, t],
                                hraw[:, bass.ds(tile_of(b, t), 1), SI:2 * SI].rearrange("p o n -> p (o n)"),
                                ALU.mult).then_inc(h_done, 1)

            def shared_out(b, t):
                wait(dve, sd_ps, count(b, TILES, t + 1))
                v.tensor_tensor(x_tiles(b, t), psE[t][:, 0:D], x_tiles(b, t), ALU.add).then_inc(sh_done, 1)

            tile_steps(dve, shared, shared_out)

            def destinations(p):
                c = p[1] % GRING
                wait_alone(dve, slots_in[c], nth_slot(p, GRING, 16, 16))
                v.tensor_scalar(own_slot[:], own_slot[:], float(P), None, ALU.add).then_inc(dest_step, 1)
                wait_alone(dve, dest_step, nth(p, 3, 1))
                v.scalar_tensor_tensor(match[:], gx[:, c, C_SLOT:C_SLOT + 8], own_slot[:], gx[:, c, C_DEST:C_DEST + 8],
                                       ALU.is_equal, ALU.mult, accum_out=found[:]).then_inc(dest_step, 1)
                wait_alone(dve, dest_step, nth(p, 3, 2))
                v.tensor_scalar(no_token[:], found[:], 0.0, AWAY, ALU.is_equal, ALU.mult).then_inc(dest_step, 1)
                wait_alone(dve, dest_step, nth(p, 3, 3))
                wait_alone(dve, eo_out[c], nth_slot(p, GRING, 16, 0))
                v.scalar_tensor_tensor(dest_idx[:, c:c + 1], found[:], -1.0, no_token[:], ALU.add,
                                       ALU.add).then_inc(dest_done, 1)

            def hidden(p):
                i = p[1] % 2
                wait(dve, silu_done, nth(p, 1, 1))
                wait(dve, hidT_ps, nth(p, 1, -1))
                v.tensor_tensor(hid[:, i], psO[i][:, FI:2 * FI], gate[:, i], ALU.mult).then_inc(hid_done, 1)

            def hidden_T(p):
                i = p[1] % 2
                wait(dve, hidT_ps, nth(p, 1, 1))
                wait(dve, dn_ps, nth(p, 1, -1))
                v.tensor_copy(hidT[:, i], psM[i][0:FI, 0:P]).then_inc(hidT_done, 1)

            def outputs_low(p):
                i, c = p[1] % 2, p[1] % GRING
                wait(dve, dn_ps, nth(p, 1, 1))
                wait(dve, eo_out[c], nth_slot(p, GRING, 16, 0))
                v.tensor_scalar(eo[0:CAP, c], psE[i][0:CAP, 0:D],
                                gx[0:CAP, c, bass.ds(nth(p, 2, C_PROB), 1)], None, ALU.mult).then_inc(eo_low, 1)

            destinations((None, 0))
            hidden((None, 0))

            def pair(p):
                last = p[0] is None and p[1] == NPAIR - 1
                hidden_T(p)
                if not last:
                    hidden(later(p, 1))
                outputs_low(p)
                if not last:
                    destinations(later(p, 1))

            pair_steps(dve, pair)

            def shift(n):
                i = n % 2
                dve.wait_ge(rstd3_done, n + 1)
                wait(dve, result_done, n - 1)
                v.tensor_scalar(shift3[:, i:i + 1], mv3[:, i, 0:1], rstd3[:, n % 4:n % 4 + 1], -1.0, ALU.mult,
                                ALU.mult).then_inc(shift3_done, 1)

            for n in range(NT):
                i, c = n % 2, n % RRING
                dve.wait_ge(routed_in[c], 16 * (n // RRING + 1))
                v.reduce_sum(half_sum[:, i], routed[:, c, 3:].rearrange("p j d -> p d j"), AX).then_inc(half_done, 1)
                dve.wait_ge(half_done, n + 1)
                dve.wait_ge(half_ps, n + 1)
                wait(dve, result_done, n - 3)
                v.tensor_tensor(y[:, n % 4], psE[i][:, 0:D], half_sum[:, i], ALU.add).then_inc(y_done, 1)
                dve.wait_ge(y_done, n + 1)
                v.bn_stats(stats3[:, i], y[:, n % 4]).then_inc(stats3_done, 1)
                dve.wait_ge(stats3_done, n + 1)
                v.bn_aggr(mv3[:, i], stats3[:, i]).then_inc(mv3_done, 1)
                if n:
                    shift(n - 1)
            shift(NT - 1)

        @block.tensor
        def _(pe):
            mm = nc.tensor.matmul
            pe.wait_ge(consts, 10)

            def transpose_in(b):
                wait(pe, xn_done, count(b, TILES, TILES))
                wait(pe, peak_read, count(b, 12, -12))
                for k in range(KD):
                    for t in range(TILES):
                        ins = nc.tensor.transpose(psM[0][:, k * S + t * P:k * S + (t + 1) * P],
                                                  xn[:, t, k * P:(k + 1) * P], ident[:])
                ins.then_inc(xT_ps, 1)

            def project(b, i, a, r):
                if i == 0:
                    if b[0] is None and b[1] == 0:
                        pe.wait_ge(setup_v, 5)
                        pe.wait_ge(wkv_in, 32)
                        pe.wait_ge(bias3_in, 48)
                    wait(pe, xnT_done, count(b, KD, KD))
                    if r:
                        wait(pe, rank_read, count(r, 1, 2))
                    else:
                        wait(pe, vs_done, count(b, 1, 0))
                elif not a:
                    wait(pe, rest_done, count(b, 4, 0))
                w, bank = (wq, wk)[i], qk_bank[i]
                for m in range(2):
                    for k in range(KD):
                        ins = mm(bank[:, m * S:(m + 1) * S], w[:, k, m * P:(m + 1) * P], xnT[:, k],
                                 start=k == 0, stop=k == KD - 1)
                ins.then_inc(qk_ps, 1)

            def values(b):
                wait(pe, rest_done, count(b, 4, 2))
                for t in range(TILES):
                    for k in range(KD):
                        mm(psG[1][:, t * D:(t + 1) * D], xnT[:, k, t * P:(t + 1) * P], wv[:, k],
                           start=k == 0, stop=False)
                    ins = mm(psG[1][:, t * D:(t + 1) * D], ones_bf[0:3, :], bias3[:, 0], start=False, stop=True)
                ins.then_inc(v_ps, 1)

            def peak(b, lo, hi, f=None):
                i = par(b)
                if lo == 0:
                    wait(pe, stack_in[i], count_half(b, 16 * 12, 16 * 12))
                    if b[0] is None and b[1] == 0:
                        pe.wait_ge(setup_v, 6)
                    if f:
                        wait(pe, xnT_done, count(f, KD, KD))
                for u in range(lo, hi):
                    wait(pe, peak_read, count(b, 12, max(u - 3, 0)))
                    bank = peak_bank[u % 4]
                    if u < 4:
                        for j in range(4):
                            mm(bank[:, j * P:(j + 1) * P], qs[0:STACK, i, 4 * u + j, 0:P],
                               ks[0:STACK, i, 4 * u + j, 0:P], start=j == 0, stop=False, skip_group_check=True)
                        out, mask = bank[:].rearrange("p (h k) -> p h k", h=4), (P, 4, P)
                    else:
                        for j in range(2):
                            mm(bank[:, j * S:(j + 1) * S], qs[0:STACK, i, 2 * (u - 4) + j, P:S],
                               ks[0:STACK, i, 2 * (u - 4) + j, :], start=j == 0, stop=False,
                               skip_group_check=True)
                        out, mask = bank[:].rearrange("p (h k) -> p h k", h=2)[:, :, P:S], (P, 2, P)
                    mm(out, ident_bf[:], upper[:].unsqueeze(1).broadcast_to(mask), start=False, stop=True,
                       skip_group_check=True).then_inc(peak_ps, 1)

            def negmax_T(b, a):
                wait_alone(pe, negmax_step, count(b, 4, 4))
                if not a:
                    wait(pe, negmaxT_done, count(b, 1, 0))
                for t in range(TILES):
                    ins = nc.tensor.transpose(psO[1][0:3 * NH, t * P // 2:(t + 1) * P // 2].bitcast(BF16),
                                              negmax_part[:, t].rearrange("p c h -> p (c h)"), ident_bf[:])
                ins.then_inc(negmaxT_ps, 1)

            def scores(b, u):
                i = par(b)
                grp, j = divmod(u, 3)
                if u == 0:
                    wait(pe, negmax_in[i], count_half(b, 48, 48))
                wait(pe, exp_done, count(b, 12, max(u - 1, 0)))
                for n in range(2 if j < 2 else 4):
                    h_, width, q0 = (4 * grp + 2 * j + n, S, 0) if j < 2 else (4 * grp + n, P, P)
                    keys = slice(0, P) if j < 2 else slice(P, S)
                    mm(psE[u % 2][:, n * width:(n + 1) * width], ks[:, i, h_, keys], qs[:, i, h_, q0:S],
                       start=n == 0, stop=False, skip_group_check=True)
                out = psE[u % 2][:].rearrange("p (h q) -> p h q", h=2 if j < 2 else 4)[:, :, 0:P]
                mm(out, ident_bf[:], lower[:].unsqueeze(1).broadcast_to((P, 2 if j < 2 else 4, P)), start=False,
                   stop=True, skip_group_check=True).then_inc(score_ps, 1)

            def weighted(b, grp):
                i, bank = par(b), psO[grp % 2]
                if grp == 0:
                    wait(pe, vs_done, count(b, 1, 1))
                    if b[0] is not None or b[1] + 2 <= NB:
                        wait(pe, rest_done, count(b, 4, 8))
                wait(pe, exp_done, count(b, 12, 3 * grp + 3))
                wait(pe, oT_done, count(b, 4, max(grp - 1, 0)))
                for j in range(4):
                    mm(bank[32 * j:32 * j + 32, 0:S], vs[:, i, 0, 4 * grp + j], probs[:, grp % 2, j * S:(j + 1) * S],
                       start=True, stop=False, skip_group_check=True)
                for j in range(4):
                    ins = mm(bank[32 * j:32 * j + 32, P:S], vs[:, i, 1, 4 * grp + j],
                             probs[:, grp % 2, 1024 + j * P:1024 + (j + 1) * P], start=False, stop=True,
                             skip_group_check=True)
                ins.then_inc(pv_ps, 1)

            def out_project(b, t):
                if t == 0:
                    if b[0] is None and b[1] == 0:
                        pe.wait_ge(weights_in, 16 * 6)
                    wait(pe, oT_done, count(b, 4, 4))
                    wait(pe, hraw_done, count(b, TILES, 0))
                out = psG[0][:, t * D:(t + 1) * D]
                for grp in range(4):
                    mm(out, oT[:, grp, t * P:(t + 1) * P], wo[:, grp], start=grp == 0, stop=False)
                ins = mm(out, ones_bf[0:3, :], bias3[:, 1], start=False, stop=True)
                if t == TILES - 1:
                    ins.then_inc(wo_ps, 1)

            def x1_T(b):
                wait(pe, x1_done, count(b, TILES, TILES))
                for k in range(KD):
                    for t in range(TILES):
                        ins = nc.tensor.transpose(psG[0][:, k * S + t * P:k * S + (t + 1) * P],
                                                  row[:, par(b), t, k * P:(k + 1) * P], ident[:])
                ins.then_inc(x1T_ps, 1)

            def gate_project(b, f, r):
                wait(pe, x1T_done, count(b, 1, 1))
                if f:
                    wait(pe, vs_done, count(f, 1, 1))
                elif r:
                    wait(pe, rank_read, count(r, 1, 2))
                for t in range(TILES):
                    for k in range(KD):
                        ins = mm(psG[1 - t][:, 0:E + 2 * SI], x1T[:, k, t * P:(t + 1) * P], wgate[:, k],
                                 start=k == 0, stop=k == KD - 1)
                    ins.then_inc(gate_ps, 1)

            def rank(b):
                wait(pe, route_step, count(b, ROUTE_STEPS, CHOOSE_STEPS))
                wait(pe, hraw_done, count(b, TILES, 1))
                out = psG[1][:, 0:TILES * E]
                mm(out, before[:], chosen[:].rearrange("p t e -> p (t e)"), start=True, stop=False)
                mm(out, ones_bf[:], earlier[:].rearrange("p t e -> p (t e)"), start=False,
                   stop=True).then_inc(rank_ps, 1)

            def step(f, m, a, r):
                if a:
                    for u in range(12):
                        scores(a, u)
                        if u in (4, 7, 10):
                            weighted(a, (u - 4) // 3)
                        if u == 4 and f:
                            transpose_in(f)
                        if u == 7 and r:
                            rank(r)
                    weighted(a, 3)
                else:
                    if f:
                        transpose_in(f)
                    if r:
                        rank(r)
                if m:
                    peak(m, 0, 4, f)
                if f:
                    project(f, 0, a, r)
                if a:
                    out_project(a, 0)
                    out_project(a, 1)
                if m:
                    peak(m, 4, 6)
                if f:
                    project(f, 1, a, r)
                if m:
                    peak(m, 6, 9)
                if a:
                    x1_T(a)
                if m:
                    peak(m, 9, 12)
                if f:
                    values(f)
                if m:
                    negmax_T(m, a)
                if a:
                    gate_project(a, f, r)

            run(pe, step)

            pe.wait_ge(peak_read, 12 * NB)
            pe.wait_ge(exp_done, 12 * NB)

            def shared_T(b, t):
                wait(pe, h_done, count(b, TILES, t + 1))
                wait(pe, hT_done, count(b, TILES, t - 1))
                for c in range(2):
                    ins = nc.tensor.transpose(psM[t][0:FI, c * P:(c + 1) * P], h[:, t, c * FI:(c + 1) * FI],
                                              ident[:])
                ins.then_inc(hT_ps, 1)

            def shared_down(b, t):
                wait(pe, hT_done, count(b, TILES, t + 1))
                wait(pe, sh_done, count(b, TILES, t - 1))
                for c in range(2):
                    ins = mm(psE[t][:, 0:D], hT[:, t, c], wsd[:, c], start=c == 0, stop=c == 1)
                ins.then_inc(sd_ps, 1)

            tile_steps(pe, shared_T, shared_down)

            pe.wait_ge(wexp_first, 48 * WRING)
            pe.wait_ge(hT_done, NT)
            pe.wait_ge(sh_done, NT)
            pe.wait_ge(route_step, ROUTE_STEPS * NB)
            pe.wait_ge(hraw_done, NT)
            pe.wait_ge(oT_done, 4 * NB)

            def rows_T(p):
                i, c = p[1] % 2, p[1] % GRING
                wait(pe, slots_in[c], nth_slot(p, GRING, 16, 16))
                wait(pe, gT_done, nth(p, 1, -1))
                for k in range(KD):
                    ins = nc.tensor.transpose(psG[i][:, k * P:(k + 1) * P], gx[:, c, k * P:(k + 1) * P], ident[:])
                ins.then_inc(gT_ps, 1)

            def gate_up(p):
                i, c = p[1] % 2, p[1] % WRING
                wait(pe, wexp_in[c], nth_slot(p, WRING, 48, 0))
                wait(pe, gT_done, nth(p, 1, 1))
                wait(pe, hid_done, nth(p, 1, -1))
                for k in range(KD):
                    for e in range(2):
                        ins = mm(psO[i][CAP * e:CAP * (e + 1), 0:2 * FI], gxT[:, i, k, CAP * e:CAP * (e + 1)],
                                 wgu[:, c, e, k], start=k == 0, stop=k == KD - 1)
                ins.then_inc(gu_ps, 1)

            def hidden_T(p):
                i = p[1] % 2
                wait(pe, hid_done, nth(p, 1, 1))
                wait(pe, hidT_done, nth(p, 1, -1))
                nc.tensor.transpose(psM[i][0:FI, 0:P], hid[:, i], ident[:]).then_inc(hidT_ps, 1)

            def down(p):
                i, c = p[1] % 2, p[1] % WRING
                wait(pe, hidT_done, nth(p, 1, 1))
                wait(pe, eo_low, nth(p, 1, -1))
                wait(pe, eo_high, nth(p, 1, -1))
                for e in range(2):
                    ins = mm(psE[i][CAP * e:CAP * (e + 1), 0:D], hidT[:, i, CAP * e:CAP * (e + 1)], wdn[:, c, e],
                             start=True, stop=True)
                ins.then_inc(dn_ps, 1)

            rows_T((None, 0))
            rows_T((None, 1))
            gate_up((None, 0))

            def pair(p):
                last = p[0] is None and p[1] >= NPAIR - 2
                if not last:
                    rows_T(later(p, 2))
                hidden_T(p)
                if not (last and p[1] == NPAIR - 1):
                    gate_up(later(p, 1))
                down(p)

            pair_steps(pe, pair)

            for n in range(NT):
                i, c = n % 2, n % RRING
                pe.wait_ge(routed_in[c], 16 * (n // RRING + 1))
                wait(pe, y_done, n - 1)
                if n < 2:
                    pe.wait_ge(eo_low, NPAIR)
                    pe.wait_ge(eo_high, NPAIR)
                mm(psE[i][:, 0:D], ident[:], x_all[:, n], start=True, stop=False)
                for j in range(3):
                    ins = mm(psE[i][:, 0:D], ident[:], routed[:, c, j], start=False, stop=j == 2)
                ins.then_inc(half_ps, 1)


def kernel(**inputs):
    import concourse.bacc as bacc
    from concourse.bass_utils import run_bass_kernel_spmd

    a = {name: np.asarray(x) for name, x in inputs.items()}

    def by_feature(w):
        return w.reshape(-1, 2, HH, DH).transpose(0, 1, 3, 2).reshape(-1, D)

    def halves(x):
        return x.reshape(2, P).T

    arrays = {
        "X": a["L0_attn_X"],
        "Wq": by_feature(a["L0_attn_Wq"]),
        "Wk": by_feature(a["L0_attn_Wk"]),
        "Wv": a["L0_attn_Wv"],
        "Wo": a["L0_attn_Wo"],
        "cols": np.concatenate([halves(a["L0_attn_ln_g"]), halves(a["L0_attn_ln_b"]),
                                halves(by_feature(a["L0_attn_bq"])), halves(by_feature(a["L0_attn_bk"]))], axis=1),
        "bias_row": np.stack([a["L0_attn_bv"], a["L0_attn_bo"]])[None],
        "Wgate": np.concatenate([a["L0_ffn_gate_w"], a["L0_ffn_shared_gate_w"], a["L0_ffn_shared_up_w"]]).T,
        "Wsd": a["L0_ffn_shared_down_w"].T,
        "gate_up": a["L0_ffn_gate_up_proj"],
        "down": a["L0_ffn_down_proj"],
    }
    arrays = {name: np.ascontiguousarray(x) for name, x in arrays.items()}

    nc = bacc.Bacc("TRN2", target_bir_lowering=False, num_devices=1)
    io = {name: nc.dram_tensor("in_" + name, x.shape, mybir.dt.from_np(x.dtype), kind="ExternalInput").ap()
          for name, x in arrays.items()}
    io["out"] = nc.dram_tensor("out", (NB, S, D), F32, kind="ExternalOutput").ap()
    moe_block_kernel(nc, io)
    r = run_bass_kernel_spmd(nc, [{"in_" + name: x for name, x in arrays.items()}], core_ids=[0])
    return r.results[0]["out"]
```

```python
from contextlib import ExitStack

import numpy as np

import concourse.bass as bass
from concourse import mybir

ALU = mybir.AluOpType
ACT = mybir.ActivationFunctionType
AX = mybir.AxisListType.X
F32 = mybir.dt.float32
BF16 = mybir.dt.bfloat16
U32 = mybir.dt.uint32

P = 128
D = 256
KD = D // P
NB = 8
S = 256
TILES = S // P
NT = NB * TILES
T = NB * S
NH = 16
DH = D // NH
HH = P // DH
E = 64
TOPK = 6
CAP = 64
FI = 96
SI = 2 * FI
NSLOT = E * CAP
NPAIR = E // 2
CLEARS = NSLOT // P // 8
EPS = 1e-5
Q_SCALE = DH ** -0.5
COPIES = ((0, 3), (3, 2), (5, 1))
STACK = 6 * DH
NEGMAX = 3
MASKED = -1e30
SENT = 2
C_PROB = D
C_SENT = C_PROB + E
C_TOKEN = C_SENT + SENT
ROW = C_TOKEN + 1
AWAY = 65536.0
CHOOSE_STEPS = 11
ROUTE_STEPS = 18
WRING = 8
GRING = 4
XRING = 8
XLEAD = 6
EXTRA = 8
SUMS = 4
RRING = 6


def moe_block_kernel(nc, io):
    with ExitStack() as ctx:
        def sb(name, shape, dt=F32):
            return ctx.enter_context(nc.sbuf_tensor(name, shape, dt))

        def sem(name):
            return ctx.enter_context(nc.semaphore(name))

        def sems(name, n):
            return [sem(f"{name}{i}") for i in range(n)]

        def dram(name, shape, dt=F32):
            return nc.dram_tensor(name, shape, dt, kind="Internal").ap()

        parts_d = dram("parts_d", (2, 4, 3, P, S), BF16)
        slots_d = dram("slots_d", (NSLOT, ROW))
        sums_d = dram("sums_d", (SUMS * T, D))

        ident = sb("ident", [P, P])
        ident_bf = sb("ident_bf", [P, P], BF16)
        before = sb("before", [P, P], BF16)
        ones_bf = sb("ones_bf", [P, P], BF16)
        upper = sb("upper", [P, P], BF16)
        lower = sb("lower", [P, P], BF16)
        slot_base = sb("slot_base", [P, TILES, E])
        neg_half = sb("neg_half", [P, TILES])
        sum_base = sb("sum_base", [P, 2])
        wq = sb("wq", [P, KD, D])
        wk = sb("wk", [P, KD, D])
        wv = sb("wv", [P, KD, D])
        wo = sb("wo", [P, NH // 4, D])
        wgate = sb("wgate", [P, KD, E + 2 * SI])
        wsd = sb("wsd", [FI, 2, D])
        cols = sb("cols", [P, 8])
        bias_row = sb("bias_row", [1, 2, D])
        bias_part = sb("bias_part", [1, 3, 2, D], BF16)
        bias_rest = sb("bias_rest", [1, 2, D])
        bias3 = sb("bias3", [3, 2, D], BF16)

        x_all = sb("x_all", [P, NT, D])
        stats1 = sb("stats1", [P, TILES, 6])
        mv1 = sb("mv1", [P, TILES, 2])
        ve1 = sb("ve1", [P, TILES])
        rstd1 = sb("rstd1", [P, TILES])
        xn = sb("xn", [P, TILES, D])
        xnT = sb("xnT", [P, KD, S])
        parts = sb("parts", [P, 4, 3, S], BF16)
        rest = sb("rest", [P, 4, S])
        qs = sb("qs", [P, 2, NH, S], BF16)
        ks = sb("ks", [P, 2, NH, S], BF16)
        vs = sb("vs", [P, 2, TILES, NH, 2 * DH])

        negmax = sb("negmax", [P, TILES, NH])
        negmax_rest = sb("negmax_rest", [P, TILES, NH])
        negmax_part = sb("negmax_part", [P, TILES, 3, NH], BF16)
        negmaxT = sb("negmaxT", [3 * NH, S], BF16)

        probs = sb("probs", [P, 2, 3 * 512])
        rowsum = sb("rowsum", [P, S])
        rinv = sb("rinv", [P, S])
        oT = sb("oT", [P, NH // 4, S])

        z = sb("z", [P, TILES, D])
        stats2 = sb("stats2", [P, TILES, 6])
        mv2 = sb("mv2", [P, TILES, 2])
        ve2 = sb("ve2", [P, TILES])
        rstd2 = sb("rstd2", [P, TILES])
        row = sb("row", [P, 2, TILES, ROW])
        x1T = sb("x1T", [P, KD, S])
        logits = sb("logits", [P, TILES, E])
        lmax = sb("lmax", [P, TILES])
        lexp = sb("lexp", [P, TILES, E])
        lsum = sb("lsum", [P, TILES])
        linv = sb("linv", [P, TILES])
        top8 = sb("top8", [P, TILES, 8])
        left = sb("left", [P, TILES, E + SENT])
        chosen = sb("chosen", [P, TILES, E], BF16)
        earlier = sb("earlier", [P, TILES, E], BF16)
        kept = sb("kept", [P, TILES, E])
        slot = sb("slot", [P, TILES, E])
        slots_of = sb("slots_of", [P, TILES, 8])
        away = sb("away", [P, TILES, 8])
        slot_idx = sb("slot_idx", [P, 2, TILES, 8], U32)
        hraw = sb("hraw", [P, NT, 2 * SI])

        wgu = sb("wgu", [P, WRING, 2, KD, 2 * FI])
        wdn = sb("wdn", [FI, WRING, 2, D])
        zeros = sb("zeros", [P, 4 * ROW])
        hT = sb("hT", [FI, 2, TILES, 2, P])
        gate = sb("gate", [P, 2, FI])
        hid = sb("hid", [P, 2, FI])
        hidT = sb("hidT", [FI, 2, P])
        no_token = sb("no_token", [P, 2])
        table = sb("table", [P, 1])
        dest_idx = sb("dest_idx", [P, GRING], U32)
        stats3 = sb("stats3", [P, 2, 6])
        mv3 = sb("mv3", [P, 2, 2])
        ve3 = sb("ve3", [P, 2])
        rstd3 = sb("rstd3", [P, 4])
        shift3 = sb("shift3", [P, 2])

        attend_flat = probs[:].rearrange("p a b -> p (a b)")
        gx = attend_flat[:, 0:XRING * ROW].rearrange("p (c r) -> p c r", c=XRING)
        eo = oT[:]
        gxT = z[:].rearrange("p i (k q) -> p i k q", k=KD)
        half_sum = xn[:]
        result = rest[:]
        weights_flat = wgu[:].rearrange("p n e k i -> p (n e k i)")
        sums = weights_flat[:, 0:RRING * SUMS * D].rearrange("p (c j d) -> p c j d", c=RRING, j=SUMS)
        places = []
        for n, flat in ((10, qs[:].rearrange("p a h t -> p (a h t)").bitcast(F32)),
                        (4, parts[:].rearrange("p m c t -> p (m c t)").bitcast(F32)),
                        (2, vs[:].rearrange("p a b h d -> p (a b h d)"))):
            width = KD * 2 * FI
            places += [flat[:, i * width:(i + 1) * width].rearrange("p (k i) -> p k i", k=KD) for i in range(n)]
        wdn_extra = ks[:].rearrange("p a h t -> p (a h t)").bitcast(F32).rearrange("p (n e d) -> p n e d", e=2, d=D)

        LATER_EXTRA = {**{c: c % WRING for c in range(2 * WRING, NPAIR - GRING) if c % WRING < GRING},
                       **{c: c % WRING - 1 for c in range(NPAIR - GRING + 1, NPAIR)}}

        def user_before(c):
            first = c in LATER_EXTRA and c - WRING not in LATER_EXTRA
            return LATER_EXTRA[c] if first else c - WRING

        LOADS = dict(zip((1, 3, 5, 7, 9, 11, 12, 14, 15, 17, 18, 20, 21, 23, 24, 25),
                         (*range(2 * WRING, 2 * WRING + GRING), *range(NPAIR - GRING + 1, NPAIR),
                          *range(2 * WRING + GRING, NPAIR - GRING + 1))))

        def gate_up_of(c, e):
            if c < EXTRA or c in LATER_EXTRA:
                return places[2 * LATER_EXTRA.get(c, c) + e]
            return wgu[:, c % WRING, e]

        def down_of(c):
            return wdn_extra[0:FI, LATER_EXTRA.get(c, c)] if c < EXTRA or c in LATER_EXTRA else wdn[:, c % WRING]

        psM = [ctx.enter_context(nc.psum_tensor(f"psM{i}", [P, 512], F32)) for i in range(2)]
        psE = [ctx.enter_context(nc.psum_tensor(f"psE{i}", [P, 512], F32)) for i in range(2)]
        psO = [ctx.enter_context(nc.psum_tensor(f"psO{i}", [P, 512], F32)) for i in range(2)]
        psG = [ctx.enter_context(nc.psum_tensor(f"psG{i}", [P, 512], F32)) for i in range(2)]

        y_bank = [psE[0], psE[1], psG[0], psG[1]]
        qk_bank = [psG[1], psO[0]]
        peak_bank = [psM[0], psM[1], psE[0], psE[1]]

        wq_in = sem("wq_in")
        wkv_in = sem("wkv_in")
        weights_in = sem("weights_in")
        small_in = sem("small_in")
        bias3_in = sem("bias3_in")
        filled = sem("filled")
        x_in = sems("x_in", 3)
        consts = sem("consts")
        pool_step = sem("pool_step")
        setup_v = sem("setup_v")
        route_init = sem("route_init")
        bias_split = sem("bias_split")
        stats1_done = sem("stats1_done")
        mv1_done = sem("mv1_done")
        ve1_done = sem("ve1_done")
        rstd1_done = sem("rstd1_done")
        xn_done = sem("xn_done")
        xT_ps = sem("xT_ps")
        xnT_done = sem("xnT_done")
        qk_ps = sem("qk_ps")
        part1_done = sem("part1_done")
        rest_done = sem("rest_done")
        part2_done = sem("part2_done")
        part3_done = sem("part3_done")
        v_ps = sem("v_ps")
        vs_done = sem("vs_done")
        parts_out = sems("parts_out", 2)
        stack_in = sems("stack_in", 2)
        peak_ps = sem("peak_ps")
        peak_read = sem("peak_read")
        negmax_step = sem("negmax_step")
        negmaxT_ps = sem("negmaxT_ps")
        negmaxT_done = sem("negmaxT_done")
        negmax_in = sems("negmax_in", 2)
        score_ps = sem("score_ps")
        exp_done = sem("exp_done")
        pv_ps = sem("pv_ps")
        rowsum_done = sem("rowsum_done")
        rinv_done = sem("rinv_done")
        oT_done = sem("oT_done")
        wo_ps = sem("wo_ps")
        z_done = sem("z_done")
        stats2_done = sem("stats2_done")
        mv2_done = sem("mv2_done")
        ve2_done = sem("ve2_done")
        rstd2_done = sem("rstd2_done")
        x1_done = sem("x1_done")
        x1T_ps = sem("x1T_ps")
        x1T_done = sem("x1T_done")
        gate_ps = sem("gate_ps")
        logits_done = sem("logits_done")
        hraw_done = sem("hraw_done")
        route_step = sem("route_step")
        lexp_done = sem("lexp_done")
        rank_ps = sem("rank_ps")
        rank_read = sem("rank_read")
        x1_kept = sem("x1_kept")
        sent = sems("sent", 2)
        h_silu = sem("h_silu")
        h_done = sem("h_done")
        hT_ps = sem("hT_ps")
        hT_done = sem("hT_done")
        sd_ps = sem("sd_ps")
        sh_done = sem("sh_done")
        dest_cols = sem("dest_cols")
        slots_in = sems("slots_in", XRING)
        wexp_first = sems("wexp_first", EXTRA)
        wexp_last = sems("wexp_last", GRING - 1)
        wexp_in = sems("wexp_in", WRING)
        gT_ps = sem("gT_ps")
        gT_done = sem("gT_done")
        gu_ps = sem("gu_ps")
        silu_done = sem("silu_done")
        hid_done = sem("hid_done")
        hidT_ps = sem("hidT_ps")
        hidT_done = sem("hidT_done")
        dn_ps = sem("dn_ps")
        eo_low = sem("eo_low")
        eo_high = sem("eo_high")
        dest_step = sem("dest_step")
        dest_done = sem("dest_done")
        eo_out = sems("eo_out", GRING)
        sums_in = sems("sums_in", RRING)
        half_done = sem("half_done")
        y_ps = sem("y_ps")
        stats3_done = sem("stats3_done")
        mv3_done = sem("mv3_done")
        ve3_done = sem("ve3_done")
        rstd3_done = sem("rstd3_done")
        shift3_done = sem("shift3_done")
        result_done = sem("result_done")
        out_out = sems("out_out", 4)


        def count(b, per, k):
            it, c = b
            v = per * c + k
            return v if it is None else it * (2 * per) + v

        def count_half(b, per, k):
            it, c = b
            v = per * (c // 2) + k
            return v if it is None else it * per + v

        def wait(eng, s, value):
            if isinstance(value, int) and value <= 0:
                return
            eng.wait_ge(s, value)

        def wait_alone(eng, s, value):
            if isinstance(value, int) and value <= 0:
                return
            eng.wait_ge(s, value)
            if not isinstance(value, int):
                eng.nop(nofuse=True)

        def later(b, n):
            return (b[0], b[1] + n)

        def par(b):
            return b[1] % 2

        def tile_of(b, t):
            return count(b, TILES, t)

        def run(eng, step):
            def at(it, i):
                step(*[(it, b) if 0 <= b < NB else None for b in (i + 1, i, i - 1, i - 2)])
            for i in range(-1, 2):
                at(None, i)
            with eng.Fori(0, 2) as it:
                for i in range(2, 4):
                    at(it, i)
            for i in range(NB - 2, NB + 2):
                at(None, i)

        H_GROUPS = ((0, 2), (2, NB - 1), (NB - 1, NB))

        def group_of(b):
            return [lo <= b[1] < hi for lo, hi in H_GROUPS].index(True)

        def last_seq(b):
            return b is not None and b[0] is None and b[1] == NB - 1

        def pair_steps(eng, step):
            for c in range(WRING + GRING):
                step((None, c))
            with eng.Fori(0, NPAIR // WRING - 2) as it:
                for c in range(WRING + GRING, 2 * WRING + GRING):
                    step((it, c))
            for c in range(NPAIR - GRING, NPAIR):
                step((None, c))

        def nth(p, per, k):
            it, c = p
            v = per * c + k
            return v if it is None else it * (WRING * per) + v

        def nth_slot(p, ring, per, k):
            it, c = p
            v = per * (c // ring) + k
            return v if it is None else it * (WRING // ring * per) + v

        block = ctx.enter_context(nc.Block())

        @block.sync
        def _(sp):
            x_rows = io["X"].rearrange("b (t p) d -> p (b t) d", p=P)
            sp.dma_start(x_all[:, 0:TILES], x_rows[:, 0:TILES]).then_inc(x_in[0], 16)
            sp.dma_start(cols[:], io["cols"]).then_inc(small_in, 16)
            sp.dma_start(bias_row[:], io["bias_row"]).then_inc(small_in, 16)
            for w, name, s in ((wq, "Wq", wq_in), (wk, "Wk", wkv_in), (wv, "Wv", wkv_in)):
                sp.dma_start(w[:], io[name].rearrange("(k p) n -> p k n", p=P)).then_inc(s, 16)
            sp.dma_start(x_all[:, TILES:2 * TILES], x_rows[:, TILES:2 * TILES]).then_inc(x_in[1], 16)
            sp.dma_start(wgate[:], io["Wgate"].rearrange("(k p) n -> p k n", p=P)).then_inc(weights_in, 16)
            sp.dma_start(wsd[:], io["Wsd"].rearrange("(k p) n -> p k n", p=FI)).then_inc(weights_in, 16)
            sp.wait_ge(setup_v, 1)
            wo_rows = io["Wo"].rearrange("(g j d) n -> j d g n", j=4, d=DH)
            for j in range(4):
                sp.dma_start(wo[32 * j:32 * j + DH], wo_rows[j]).then_inc(weights_in, 16)
            sp.dma_start(x_all[:, 2 * TILES:], x_rows[:, 2 * TILES:]).then_inc(x_in[2], 16)
            sp.wait_ge(bias_split, 5)
            for c in range(3):
                sp.dma_start(bias3[c:c + 1], bias_part[0:1, c]).then_inc(bias3_in, 16)

            def write_parts(b):
                wait_alone(sp, stack_in[par(b)], count_half(b, 16 * 12, 0))
                wait_alone(sp, part3_done, count(b, 2, 2))
                sp.dma_start(parts_d[par(b)].rearrange("m c p t -> p (m c) t"),
                             parts[:].rearrange("p m c t -> p (m c) t")).then_inc(parts_out[par(b)], 16)

            gu_rows = io["gate_up"].rearrange("(n e) (k p) i -> n p e k i", e=2, p=P)
            dn_rows = io["down"].rearrange("(n e) i d -> n i e d", e=2)

            def load_weights(c, signal):
                for e in range(2):
                    sp.dma_start(gate_up_of(c, e), gu_rows[c, :, e]).then_inc(signal, 16)
                sp.dma_start(down_of(c), dn_rows[c]).then_inc(signal, 16)

            def stack(b):
                wait_alone(sp, parts_out[par(b)], count_half(b, 16, 16))
                wait_alone(sp, score_ps, count(b, 12, -12))
                src = parts_d[par(b)].rearrange("m c (d h) t -> m (c d) (h t)", h=HH)
                for m in range(2):
                    heads = slice(HH * m, HH * m + HH)
                    for part, (c0, n) in enumerate(COPIES):
                        sp.dma_start(qs[DH * c0:DH * (c0 + n), par(b), heads, :],
                                     src[m, 0:DH * n]).then_inc(stack_in[par(b)], 16)
                        sp.dma_start(ks[DH * c0:DH * (c0 + n), par(b), heads, :],
                                     src[2 + m, DH * part:DH * (part + 1)].unsqueeze(0).broadcast_to(
                                         (n, DH, HH * S))).then_inc(stack_in[par(b)], 16)

            def negmax_rows(b):
                wait_alone(sp, negmaxT_done, count(b, 1, 1))
                for c in range(3):
                    sp.dma_start(qs[STACK + c:STACK + c + 1, par(b)],
                                 negmaxT[NH * c:NH * (c + 1), :]).then_inc(negmax_in[par(b)], 16)

            def step(f, m, a, r):
                if m:
                    negmax_rows(m)
                if f:
                    write_parts(f)
                    stack(f)
                if f and f[0] is None and f[1] == NB - 1:
                    for c in range(EXTRA, EXTRA + WRING):
                        load_weights(c, wexp_in[c % WRING])

            run(sp, step)

            sp.wait_ge(score_ps, 12 * NB)
            sp.wait_ge(pv_ps, 4 * NB)
            for i in range(2):
                sp.wait_ge(parts_out[i], 16 * NB // 2)
            for c in range(EXTRA):
                load_weights(c, wexp_first[c])

            for i in range(2):
                sp.wait_ge(sent[i], 16 * CLEARS + 16 * 6 * TILES * NB // 2)

            slot_rows = slots_d.rearrange("(n p) r -> p n r", p=P)

            def load_pair(c):
                for used in (eo_low, eo_high, dest_done):
                    wait(sp, used, c - XRING + 1)
                sp.dma_start(gx[:, c % XRING], slot_rows[:, c]).then_inc(slots_in[c % XRING], 16)

            for c in range(XLEAD):
                load_pair(c)
            for p in range(NPAIR):
                if p + XLEAD < NPAIR:
                    load_pair(p + XLEAD)
                if p in LOADS:
                    c = LOADS[p]
                    sp.wait_ge(dn_ps, user_before(c) + 1)
                    load_weights(c, wexp_last[c - (NPAIR - GRING + 1)] if c > NPAIR - GRING else wexp_in[c % WRING])

            for c in range(GRING):
                sp.wait_ge(eo_out[c], 16 * NPAIR // GRING)
            sum_rows = sums_d.rearrange("(j n p) d -> n p j d", j=SUMS, p=P)
            for n in range(NT):
                c = n % RRING
                wait(sp, y_ps, n - RRING + 1)
                wait(sp, half_done, n - RRING + 1)
                sp.dma_start(sums[:, c], sum_rows[n]).then_inc(sums_in[c], 16)
            for c in range(4):
                sp.wait_ge(out_out[c], 16 * NT // 4)

        @block.gpsimd
        def _(pool):
            g = nc.gpsimd
            def power_in(b):
                wait_alone(pool, mv1_done, count(b, TILES, TILES))
                g.tensor_scalar(ve1[:], mv1[:, :, 1], EPS, None, ALU.add).then_inc(ve1_done, 1)
                wait(pool, ve1_done, count(b, 1, 1))
                g.tensor_tensor(rstd1[:], ve1[:], neg_half[:], ALU.pow).then_inc(rstd1_done, 1)

            g.memset(zeros[:], 0.0).then_inc(pool_step, 1)
            g.memset(ident[:], 0.0).then_inc(pool_step, 1)
            g.memset(before[:], 1.0).then_inc(pool_step, 1)
            g.memset(upper[:], 0.0).then_inc(pool_step, 1)
            g.memset(neg_half[:], -0.5).then_inc(consts, 1)
            g.memset(ones_bf[:], 1.0).then_inc(consts, 1)
            g.memset(lower[:], 0.0).then_inc(pool_step, 1)
            pool.wait_ge(pool_step, 5)
            g.affine_select(ident[:], ident[:], [[-1, P]], ALU.not_equal, 1.0, base=0,
                            channel_multiplier=1).then_inc(consts, 1)
            g.affine_select(before[:], before[:], [[1, P]], ALU.is_gt, 0.0, base=0,
                            channel_multiplier=-1).then_inc(consts, 1)
            g.affine_select(upper[:], upper[:], [[-1, P]], ALU.is_ge, MASKED, base=0,
                            channel_multiplier=1).then_inc(consts, 1)
            g.affine_select(lower[:], lower[:], [[1, P]], ALU.is_ge, MASKED, base=0,
                            channel_multiplier=-1).then_inc(consts, 1)
            g.iota(slot_base[:], [[0, TILES], [CAP, E]], base=1, channel_multiplier=0,
                   allow_small_or_imprecise_dtypes=True).then_inc(consts, 1)
            for i in range(2):
                g.iota(row[:, i, :, C_TOKEN], [[P, TILES]], base=1 + (i - 2) * S, channel_multiplier=1,
                       allow_small_or_imprecise_dtypes=True).then_inc(consts, 1)
            power_in((None, 0))
            slots_flat = slots_d.rearrange("(p n) r -> p (n r)", p=P)
            sums_flat = sums_d.rearrange("(p n) d -> p (n d)", p=P)
            piece = SUMS * T // P * D // NB
            blank = 4 * D

            def background(b):
                wait_alone(pool, stack_in[par(b)], count_half(b, 16 * 12, 16 * 12))
                pool.dma_start(sums_flat[:, bass.ds(count(b, piece, 0), piece)].rearrange("p (n w) -> p n w", w=blank),
                               zeros[:, 0:blank].unsqueeze(1).broadcast_to((P, piece // blank, blank))
                               ).then_inc(filled, 16)

            def clear_slots(i):
                for n in range(CLEARS * i, CLEARS * (i + 1)):
                    pool.dma_start(slots_flat[:, n * 4 * ROW:(n + 1) * 4 * ROW], zeros[:]).then_inc(sent[n % 2], 16)

            def power_mid(b):
                wait_alone(pool, mv2_done, count(b, TILES, TILES))
                g.tensor_scalar(ve2[:], mv2[:, :, 1], EPS, None, ALU.add).then_inc(ve2_done, 1)
                wait(pool, ve2_done, count(b, 1, 1))
                g.tensor_tensor(rstd2[:], ve2[:], neg_half[:], ALU.pow).then_inc(rstd2_done, 1)

            def dispatch(b, t):
                if t == 0:
                    wait_alone(pool, sent[par(b)], count_half(b, 16 * 6 * TILES, 16 * CLEARS))
                    token = row[:, par(b), :, C_TOKEN]
                    g.tensor_scalar(token, token, float(2 * S), None, ALU.add).then_inc(dest_cols, 1)
                    wait_alone(pool, dest_cols, count(b, 1, 1))
                    wait_alone(pool, x1_done, count(b, TILES, TILES))
                    wait_alone(pool, route_step, count(b, ROUTE_STEPS, ROUTE_STEPS))
                for j in range(TOPK):
                    g.indirect_dma_start(
                        out=slots_d, out_offset=bass.IndirectOffsetOnAxis(
                            ap=slot_idx[:, par(b), t, j:j + 1], axis=0),
                        in_=row[:, par(b), t, :], in_offset=None, bounds_check=NSLOT - 1,
                        oob_is_err=False).then_inc(sent[par(b)], 16)

            def step(f, m, a, r):
                if f and (f[0] is not None or f[1] < NB - 1):
                    power_in(later(f, 1))
                if m:
                    background(m)
                if a:
                    power_mid(a)
                if r:
                    dispatch(r, 0)
                    dispatch(r, 1)
                if f and f[0] is None and f[1] < 2:
                    clear_slots(f[1])
                if f and f[0] is None and f[1] == 2:
                    for i in range(2):
                        pool.wait_ge(sent[i], 16 * CLEARS)

            run(pool, step)
            pool.wait_ge(filled, 16 * NB)

            def scatter(p):
                c = p[1] % GRING
                wait_alone(pool, eo_low, nth(p, 1, 1))
                wait_alone(pool, eo_high, nth(p, 1, 1))
                wait_alone(pool, dest_done, nth(p, 1, 1))
                if p[1] >= 2:
                    q = later(p, -2)
                    wait_alone(pool, eo_out[q[1] % GRING], nth_slot(q, GRING, 16, 16))
                g.indirect_dma_start(out=sums_d, out_offset=bass.IndirectOffsetOnAxis(
                    ap=dest_idx[:, c:c + 1], axis=0), in_=eo[:, c], in_offset=None,
                    bounds_check=SUMS * T - 1, oob_is_err=False, compute_op=ALU.add).then_inc(eo_out[c], 16)

            pair_steps(pool, scatter)

            for n in range(NT):
                i = n % 2
                pool.wait_ge(mv3_done, n + 1)
                g.tensor_scalar(ve3[:, i:i + 1], mv3[:, i, 1:2], EPS, None, ALU.add).then_inc(ve3_done, 1)
                pool.wait_ge(ve3_done, n + 1)
                g.tensor_tensor(rstd3[:, n % 4:n % 4 + 1], ve3[:, i:i + 1], neg_half[:, 0:1], ALU.pow).then_inc(
                    rstd3_done, 1)

        @block.scalar
        def _(act):
            s = nc.scalar
            act.wait_ge(small_in, 32)

            def transpose_out(b):
                wait(act, xT_ps, count(b, 1, 1))
                wait(act, v_ps, count(b, 1, 0))
                for k in range(KD):
                    s.activation(xnT[:, k], psM[0][:, k * S:(k + 1) * S], ACT.Identity,
                                 bias=cols[:, 2 + k:3 + k], scale=cols[:, k:k + 1]).then_inc(xnT_done, 1)

            def part1(b, i):
                if i == 0:
                    if b[0] is None and b[1] == 0:
                        act.wait_ge(setup_v, 2)
                    before_b = later(b, -1)
                    if before_b[0] is not None or before_b[1] >= 0:
                        wait(act, parts_out[par(before_b)], count_half(before_b, 16, 16))
                wait(act, qk_ps, count(b, 2, i + 1))
                for m in range(2):
                    s.activation(parts[:, 2 * i + m, 0], qk_bank[i][:, m * S:(m + 1) * S], ACT.Identity,
                                 bias=cols[:, 4 + 2 * i + m:5 + 2 * i + m]).then_inc(part1_done, 1)

            def part2(b, i):
                wait(act, rest_done, count(b, 4, 2 * i + 2))
                s.copy(parts[:, 2 * i:2 * i + 2, 1], rest[:, 2 * i:2 * i + 2]).then_inc(part2_done, 1)

            def values(b):
                wait(act, v_ps, count(b, 1, 1))
                wait(act, pv_ps, count(b, 4, -4))
                if b[0] is None and b[1] == 0:
                    act.wait_ge(setup_v, 5)
                s.copy(vs[:, par(b), :, :, 0:DH],
                       psG[1][:].rearrange("p (t h d) -> p t h d", t=TILES, h=NH)).then_inc(vs_done, 1)

            def exponents(b, lo, hi):
                for u in range(lo, hi):
                    grp, j = divmod(u, 3)
                    wait(act, score_ps, count(b, 12, u + 1))
                    if j == 0:
                        wait(act, pv_ps, count(b, 4, max(grp - 1, 0)))
                    s.activation(probs[:, grp % 2, 512 * j:512 * (j + 1)], psE[u % 2][:],
                                 ACT.Exp).then_inc(exp_done, 1)

            def negmax_out(b):
                wait(act, negmaxT_ps, count(b, 1, 1))
                prev = later(b, -1)
                if prev[0] is not None or prev[1] >= 0:
                    wait(act, negmax_in[par(prev)], count_half(prev, 48, 48))
                s.copy(negmaxT[:], psO[1][0:3 * NH, 0:S // 2].bitcast(BF16)).then_inc(negmaxT_done, 1)

            def x1T_out(b):
                wait(act, x1T_ps, count(b, 1, 1))
                wait(act, gate_ps, count(b, 2, 0))
                s.copy(x1T[:].rearrange("p k t -> p (k t)"), psG[0][:]).then_inc(x1T_done, 1)

            def gate_out(b):
                for t in range(TILES):
                    wait(act, gate_ps, count(b, 2, t + 1))
                    wait(act, route_step, count(b, ROUTE_STEPS, 0))
                    s.copy(logits[:, t], psG[1 - t][:, 0:E]).then_inc(logits_done, 1)
                    s.copy(hraw[:, bass.ds(tile_of(b, t), 1)].rearrange("p o n -> p (o n)"),
                           psG[1 - t][:, E:E + 2 * SI]).then_inc(hraw_done, 1)

            def keep_x1(b):
                wait(act, x1_done, count(b, TILES, TILES))
                s.copy(x_all[:, bass.ds(tile_of(b, 0), TILES)], row[:, par(b), :, 0:D]).then_inc(x1_kept, 1)

            def router_exp(b):
                wait(act, route_step, count(b, ROUTE_STEPS, 2))
                s.activation(lexp[:], lexp[:], ACT.Exp).then_inc(lexp_done, 1)

            def shared_silu(n):
                lo, hi = H_GROUPS[n]
                act.wait_ge(hraw_done, TILES * hi)
                gates_of = hraw[:, TILES * lo:TILES * hi, 0:SI]
                s.activation(gates_of, gates_of, ACT.Silu).then_inc(h_silu, 1)

            def shared_T(b):
                wait(act, hT_ps, count(b, 1, 1))
                wait(act, sd_ps, count(b, 1, -1))
                s.copy(hT[:, par(b)].rearrange("p t c q -> p (t c q)"), psM[par(b)][0:FI, :]).then_inc(hT_done, 1)

            def step(f, m, a, r):
                if r:
                    router_exp(r)
                if last_seq(r):
                    shared_T((None, 3))
                    shared_T((None, 4))
                if a:
                    exponents(a, 0, 8)
                if f:
                    transpose_out(f)
                if r:
                    keep_x1(r)
                if a:
                    exponents(a, 8, 12)
                if last_seq(a):
                    shared_silu(0)
                    shared_silu(1)
                    s.activation(table[:], zeros[:, 0:1], ACT.Exp)
                    shared_T((None, 0))
                    shared_T((None, 1))
                if f:
                    part1(f, 0)
                    part1(f, 1)
                    part2(f, 0)
                if a:
                    x1T_out(a)
                if last_seq(a):
                    shared_T((None, 2))
                if f:
                    values(f)
                if m:
                    negmax_out(m)
                if f:
                    part2(f, 1)
                if a:
                    gate_out(a)

            run(act, step)
            shared_silu(2)
            for b in range(5, NB):
                shared_T((None, b))

            def rows_T(p):
                i = p[1] % 2
                wait(act, gT_ps, nth(p, 1, 1))
                wait(act, gu_ps, nth(p, 1, -1))
                s.copy(gxT[:, i].rearrange("p k q -> p (k q)"), psG[i][:, 0:D]).then_inc(gT_done, 1)

            def gates(p):
                i = p[1] % 2
                wait(act, gu_ps, nth(p, 1, 1))
                wait(act, hid_done, nth(p, 1, -1))
                s.activation(gate[:, i], psO[i][:, 0:FI], ACT.Silu).then_inc(silu_done, 1)

            def outputs_high(p):
                i, c = p[1] % 2, p[1] % GRING
                wait(act, dn_ps, nth(p, 1, 1))
                wait(act, eo_out[c], nth_slot(p, GRING, 16, 0))
                s.activation(eo[CAP:2 * CAP, c], psE[i][CAP:2 * CAP, 0:D], ACT.Copy,
                             scale=gx[CAP:2 * CAP, p[1] % XRING, bass.ds(nth(p, 2, C_PROB + 1), 1)]).then_inc(eo_high, 1)

            rows_T((None, 0))
            rows_T((None, 1))
            gates((None, 0))

            def pair(p):
                last = p[0] is None and p[1] >= NPAIR - 2
                if not last:
                    rows_T(later(p, 2))
                if not (last and p[1] == NPAIR - 1):
                    gates(later(p, 1))
                outputs_high(p)

            pair_steps(act, pair)

            out_rows = io["out"].rearrange("b (t p) d -> (b t) p d", p=P)
            for n in range(NT):
                act.wait_ge(shift3_done, n + 1)
                wait(act, out_out[n % 4], 16 * (n // 4))
                s.activation(result[:, n % 4], y_bank[n % 4][:, 0:D], ACT.Identity, bias=shift3[:, n % 2:n % 2 + 1],
                             scale=rstd3[:, n % 4:n % 4 + 1]).then_inc(result_done, 1)
                act.wait_ge(result_done, n + 1)
                act.dma_start(out_rows[n], result[:, n % 4]).then_inc(out_out[n % 4], 16)

        @block.vector
        def _(dve):
            v = nc.vector

            def x_tiles(b, t=None):
                if t is None:
                    return x_all[:, bass.ds(tile_of(b, 0), TILES)]
                return x_all[:, bass.ds(tile_of(b, t), 1)].rearrange("p o d -> p (o d)")

            def stats_in(b):
                wait(dve, x_in[min(b[1], 2)], 16)
                for t in range(TILES):
                    v.bn_stats(stats1[:, t], x_tiles(b, t)).then_inc(stats1_done, 1)
                wait_alone(dve, stats1_done, count(b, TILES, TILES))
                wait_alone(dve, xn_done, count(b, TILES, 0))
                for t in range(TILES):
                    v.bn_aggr(mv1[:, t], stats1[:, t]).then_inc(mv1_done, 1)

            stats_in((None, 0))
            v.memset(wo[:], 0.0).then_inc(setup_v, 1)
            v.memset(earlier[:], 0.0).then_inc(route_init, 1)
            for i in range(2):
                for e in range(2):
                    v.memset(sum_base[CAP * e:CAP * (e + 1), i:i + 1], float((2 * i + e) * T - 1)).then_inc(
                        route_init, 1)
            v.memset(row[:, :, :, C_SENT:C_SENT + SENT], 2.0).then_inc(rank_read, 1)
            dve.wait_ge(small_in, 32)
            v.tensor_scalar(cols[:, 4:6], cols[:, 4:6], Q_SCALE, None, ALU.mult).then_inc(setup_v, 1)

            def norm_in(b):
                wait(dve, rstd1_done, count(b, 1, 1))
                wait(dve, xT_ps, count(b, 1, 0))
                for t in range(TILES):
                    v.tensor_scalar(xn[:, t], x_tiles(b, t), mv1[:, t, 0:1], rstd1[:, t:t + 1],
                                    ALU.subtract, ALU.mult).then_inc(xn_done, 1)

            norm_in((None, 0))
            dve.wait_ge(wq_in, 16)
            v.tensor_scalar(wq[:], wq[:], Q_SCALE, None, ALU.mult).then_inc(setup_v, 1)
            dve.wait_ge(consts, 9)
            v.tensor_copy(ident_bf[:], ident[:]).then_inc(setup_v, 1)
            v.memset(vs[:], 1.0).then_inc(setup_v, 1)
            rest_row = bias_rest[:]
            v.tensor_copy(bias_part[:, 0], bias_row[:]).then_inc(bias_split, 1)
            dve.wait_ge(bias_split, 1)
            v.tensor_tensor(rest_row, bias_row[:], bias_part[:, 0], ALU.subtract).then_inc(bias_split, 1)
            dve.wait_ge(bias_split, 2)
            v.tensor_copy(bias_part[:, 1], rest_row).then_inc(bias_split, 1)
            dve.wait_ge(bias_split, 3)
            v.tensor_tensor(rest_row, rest_row, bias_part[:, 1], ALU.subtract).then_inc(bias_split, 1)
            dve.wait_ge(bias_split, 4)
            v.tensor_copy(bias_part[:, 2], rest_row).then_inc(bias_split, 1)

            def rest_of(b, i):
                for m in range(2):
                    mm = 2 * i + m
                    wait(dve, part1_done, count(b, 4, 2 * i + 2))
                    v.scalar_tensor_tensor(rest[:, mm], qk_bank[i][:, m * S:(m + 1) * S],
                                           cols[:, 4 + mm:5 + mm], parts[:, mm, 0], ALU.add,
                                           ALU.subtract).then_inc(rest_done, 1)

            def part3(b, i):
                wait(dve, part2_done, count(b, 2, i + 1))
                two = slice(2 * i, 2 * i + 2)
                v.tensor_tensor(parts[:, two, 2], rest[:, two], parts[:, two, 1], ALU.subtract).then_inc(part3_done, 1)

            def maxima(b, lo, hi):
                for u in range(lo, hi):
                    wait(dve, peak_ps, count(b, 12, u + 1))
                    if u < 4:
                        out, src = negmax[:, 0, 4 * u:4 * u + 4], peak_bank[u % 4][:].rearrange("p (h k) -> p h k", h=4)
                    else:
                        w = u - 4
                        out, src = negmax[:, 1, 2 * w:2 * w + 2], peak_bank[u % 4][:].rearrange("p (h k) -> p h k", h=2)
                    v.tensor_reduce(out, src, AX, ALU.max, negate=True).then_inc(peak_read, 1)

            def negmax_split(b):
                wait(dve, peak_read, count(b, 12, 12))
                wait(dve, negmaxT_ps, count(b, 1, 0))
                v.tensor_copy(negmax_part[:, :, 0], negmax[:]).then_inc(negmax_step, 1)
                wait(dve, negmax_step, count(b, 4, 1))
                v.tensor_tensor(negmax_rest[:], negmax[:], negmax_part[:, :, 0], ALU.subtract).then_inc(
                    negmax_step, 1)
                wait(dve, negmax_step, count(b, 4, 2))
                v.tensor_copy(negmax_part[:, :, 1], negmax_rest[:]).then_inc(negmax_step, 1)
                wait(dve, negmax_step, count(b, 4, 3))
                v.tensor_tensor(negmax_part[:, :, 2], negmax_rest[:], negmax_part[:, :, 1],
                                ALU.subtract).then_inc(negmax_step, 1)

            SUM_ROWS = [DH + i % DH for i in range(2 * DH)]

            def normalise(b, grp):
                if grp == 0:
                    wait_alone(dve, wo_ps, count(b, 1, 0))
                wait_alone(dve, pv_ps, count(b, 4, grp + 1))
                v.stream_shuffle(rowsum[:], psO[grp % 2][:, 0:S], SUM_ROWS).then_inc(rowsum_done, 1)
                wait(dve, rowsum_done, count(b, 4, grp + 1))
                v.reciprocal(rinv[:], rowsum[:]).then_inc(rinv_done, 1)
                wait(dve, rinv_done, count(b, 4, grp + 1))
                v.tensor_tensor(oT[:, grp], psO[grp % 2][:, 0:S], rinv[:], ALU.mult).then_inc(oT_done, 1)

            def norm_mid(b):
                wait(dve, wo_ps, count(b, 1, 1))
                v.tensor_tensor(z[:], psG[0][:].rearrange("p (t d) -> p t d", t=TILES), x_tiles(b),
                                ALU.add).then_inc(z_done, 1)
                wait(dve, z_done, count(b, 1, 1))
                for t in range(TILES):
                    v.bn_stats(stats2[:, t], z[:, t]).then_inc(stats2_done, 1)
                wait_alone(dve, stats2_done, count(b, TILES, TILES))
                for t in range(TILES):
                    v.bn_aggr(mv2[:, t], stats2[:, t]).then_inc(mv2_done, 1)

            def norm_mid_end(b):
                wait(dve, rstd2_done, count(b, 1, 1))
                wait(dve, sent[par(b)], count_half(b, 16 * 6 * TILES, 16 * CLEARS))
                wait(dve, x1_kept, count(b, 1, 0))
                for t in range(TILES):
                    v.tensor_scalar(row[:, par(b), t, 0:D], z[:, t], mv2[:, t, 0:1], rstd2[:, t:t + 1],
                                    ALU.subtract, ALU.mult).then_inc(x1_done, 1)

            def route_signals(b, done):
                def chained(ins):
                    done[0] += 1
                    ins.then_inc(route_step, 1)
                    wait_alone(dve, route_step, count(b, ROUTE_STEPS, done[0]))

                def loose(ins):
                    done[0] += 1
                    ins.then_inc(route_step, 1)

                return chained, loose

            def choose(b):
                r = row[:, par(b)]
                chained, loose = route_signals(b, [0])

                wait(dve, logits_done, count(b, TILES, TILES))
                chained(v.reduce_max(lmax[:], logits[:], AX))
                loose(v.tensor_tensor(lexp[:], logits[:], lmax[:].unsqueeze(2).broadcast_to((P, TILES, E)),
                                      ALU.subtract))
                wait(dve, lexp_done, count(b, 1, 1))
                chained(v.reduce_sum(lsum[:], lexp[:], AX))
                chained(v.reciprocal(linv[:], lsum[:]))
                chained(v.tensor_tensor(r[:, :, C_PROB:C_PROB + E], lexp[:],
                                        linv[:].unsqueeze(2).broadcast_to((P, TILES, E)), ALU.mult))
                loose(v.max(top8[:, 0], r[:, 0, C_PROB:C_SENT + SENT]))
                chained(v.max(top8[:, 1], r[:, 1, C_PROB:C_SENT + SENT]))
                loose(v.match_replace(left[:, 0], top8[:, 0], r[:, 0, C_PROB:C_SENT + SENT], -1.0))
                chained(v.match_replace(left[:, 1], top8[:, 1], r[:, 1, C_PROB:C_SENT + SENT], -1.0))
                chained(v.tensor_scalar(chosen[:], left[:, :, 0:E], 0.0, None, ALU.is_lt))
                loose(v.tensor_tensor(earlier[:, 1], earlier[:, 0], chosen[:, 0], ALU.add))

            def read_ranks(b):
                _, loose = route_signals(b, [CHOOSE_STEPS])
                wait(dve, rank_ps, count(b, 1, 1))
                rank = psG[1][:, 0:TILES * E].rearrange("p (t e) -> p t e", t=TILES)
                loose(v.scalar_tensor_tensor(kept[:], rank, float(CAP), chosen[:], ALU.is_lt, ALU.mult))
                v.tensor_tensor(slot[:], rank, slot_base[:], ALU.add).then_inc(rank_read, 1)

            def place(b):
                chained, loose = route_signals(b, [CHOOSE_STEPS + 1])
                wait_alone(dve, rank_read, count(b, 1, 2))
                loose(v.tensor_tensor(earlier[:, 0], earlier[:, 1], chosen[:, 1], ALU.add))
                chained(v.tensor_tensor(slot[:], slot[:], kept[:], ALU.mult))
                loose(v.max(slots_of[:, 0], slot[:, 0]))
                chained(v.max(slots_of[:, 1], slot[:, 1]))
                chained(v.tensor_scalar(away[:], slots_of[:], 0.0, AWAY, ALU.is_equal, ALU.mult))
                loose(v.scalar_tensor_tensor(slot_idx[:, par(b)], slots_of[:], -1.0, away[:],
                                             ALU.add, ALU.add))

            def shared_hidden(n):
                lo, hi = H_GROUPS[n]
                rows = hraw[:, TILES * lo:TILES * hi]
                dve.wait_ge(h_silu, n + 1)
                v.tensor_tensor(rows[:, :, 0:SI], rows[:, :, 0:SI], rows[:, :, SI:2 * SI], ALU.mult).then_inc(h_done, 1)

            def shared_out(b):
                wait(dve, x1_kept, count(b, 1, 1))
                wait(dve, sd_ps, count(b, 1, 1))
                v.tensor_tensor(x_tiles(b), psE[par(b)][:].rearrange("p (t d) -> p t d", t=TILES), x_tiles(b),
                                ALU.add).then_inc(sh_done, 1)

            def step(f, m, a, r):
                if f and (f[0] is not None or f[1] > 0):
                    norm_in(f)
                if f and (f[0] is not None or f[1] < NB - 1):
                    stats_in(later(f, 1))
                if f and f[0] is None and f[1] == 1:
                    v.memset(ks[STACK:STACK + NEGMAX], 1.0).then_inc(setup_v, 1)
                if r:
                    choose(r)
                if a:
                    for grp in range(3):
                        normalise(a, grp)
                if r:
                    read_ranks(r)
                if a:
                    normalise(a, 3)
                if last_seq(a):
                    shared_hidden(0)
                if m:
                    maxima(m, 0, 4)
                if f:
                    rest_of(f, 0)
                if r:
                    place(r)
                if a:
                    norm_mid(a)
                if m:
                    maxima(m, 4, 6)
                if a:
                    norm_mid_end(a)
                if last_seq(a):
                    shared_hidden(1)
                    shared_out((None, 0))
                    shared_out((None, 1))
                if m:
                    maxima(m, 6, 12)
                    negmax_split(m)
                if f:
                    rest_of(f, 1)
                    part3(f, 0)
                    part3(f, 1)

            dve.wait_ge(route_init, 5)
            dve.wait_ge(rank_read, 1)
            run(dve, step)
            shared_out((None, 2))
            shared_hidden(2)
            for b in range(3, NB):
                shared_out((None, b))

            def empty_slots(p):
                rows = gx[:, p[1] % XRING]
                wait_alone(dve, slots_in[p[1] % XRING], nth_slot(p, XRING, 16, 16))
                wait_alone(dve, dest_done, nth(p, 1, -1))
                v.tensor_scalar(no_token[:, p[1] % 2:p[1] % 2 + 1], rows[:, C_TOKEN:C_TOKEN + 1], 0.0, AWAY, ALU.is_equal,
                                ALU.mult).then_inc(dest_step, 1)

            def destinations(p):
                c = p[1] % GRING
                rows = gx[:, p[1] % XRING]
                wait_alone(dve, dest_step, nth(p, 1, 1))
                wait_alone(dve, eo_out[c], nth_slot(p, GRING, 16, 0))
                v.scalar_tensor_tensor(dest_idx[:, c:c + 1], rows[:, C_TOKEN:C_TOKEN + 1],
                                       sum_base[:, p[1] % 2:p[1] % 2 + 1], no_token[:, p[1] % 2:p[1] % 2 + 1], ALU.add,
                                       ALU.add).then_inc(dest_done, 1)

            def hidden(p):
                i = p[1] % 2
                wait(dve, silu_done, nth(p, 1, 1))
                wait(dve, hidT_ps, nth(p, 1, -1))
                v.tensor_tensor(hid[:, i], psO[i][:, FI:2 * FI], gate[:, i], ALU.mult).then_inc(hid_done, 1)

            def hidden_T(p):
                i = p[1] % 2
                wait(dve, hidT_ps, nth(p, 1, 1))
                wait(dve, dn_ps, nth(p, 1, -1))
                v.tensor_copy(hidT[:, i], psM[i][0:FI, 0:P]).then_inc(hidT_done, 1)

            def outputs_low(p):
                i, c = p[1] % 2, p[1] % GRING
                wait(dve, dn_ps, nth(p, 1, 1))
                wait(dve, eo_out[c], nth_slot(p, GRING, 16, 0))
                v.tensor_scalar(eo[0:CAP, c], psE[i][0:CAP, 0:D],
                                gx[0:CAP, p[1] % XRING, bass.ds(nth(p, 2, C_PROB), 1)], None, ALU.mult).then_inc(eo_low, 1)

            hidden((None, 0))

            def pair(p):
                hidden_T(p)
                if p[0] is not None or p[1] > 0:
                    outputs_low(later(p, -1))
                empty_slots(p)
                if p[0] is not None or p[1] < NPAIR - 1:
                    hidden(later(p, 1))
                destinations(p)

            pair_steps(dve, pair)
            outputs_low((None, NPAIR - 1))

            def shift(n):
                i = n % 2
                dve.wait_ge(rstd3_done, n + 1)
                wait(dve, result_done, n - 1)
                v.tensor_scalar(shift3[:, i:i + 1], mv3[:, i, 0:1], rstd3[:, n % 4:n % 4 + 1], -1.0, ALU.mult,
                                ALU.mult).then_inc(shift3_done, 1)

            def half(n):
                i, c = n % 2, n % RRING
                dve.wait_ge(sums_in[c], 16 * (n // RRING + 1))
                wait(dve, y_ps, n - 1)
                v.tensor_tensor(half_sum[:, i], sums[:, c, 2], sums[:, c, 3], ALU.add).then_inc(half_done, 1)

            half(0)
            for n in range(NT):
                i = n % 2
                if n < NT - 1:
                    half(n + 1)
                dve.wait_ge(y_ps, n + 1)
                v.bn_stats(stats3[:, i], y_bank[n % 4][:, 0:D]).then_inc(stats3_done, 1)
                dve.wait_ge(stats3_done, n + 1)
                v.bn_aggr(mv3[:, i], stats3[:, i]).then_inc(mv3_done, 1)
                if n:
                    shift(n - 1)
            shift(NT - 1)

        @block.tensor
        def _(pe):
            mm = nc.tensor.matmul
            pe.wait_ge(consts, 9)

            def transpose_in(b):
                wait(pe, xn_done, count(b, TILES, TILES))
                wait(pe, peak_read, count(b, 12, -12))
                for k in range(KD):
                    for t in range(TILES):
                        ins = nc.tensor.transpose(psM[0][:, k * S + t * P:k * S + (t + 1) * P],
                                                  xn[:, t, k * P:(k + 1) * P], ident[:])
                ins.then_inc(xT_ps, 1)

            def project(b, i, a, r):
                if i == 0:
                    if b[0] is None and b[1] == 0:
                        pe.wait_ge(setup_v, 3)
                        pe.wait_ge(wkv_in, 32)
                    wait(pe, xnT_done, count(b, KD, KD))
                    if r:
                        wait(pe, rank_read, count(r, 1, 2))
                    else:
                        wait(pe, vs_done, count(b, 1, 0))
                elif not a:
                    wait(pe, rest_done, count(b, 4, 0))
                w, bank = (wq, wk)[i], qk_bank[i]
                for m in range(2):
                    for k in range(KD):
                        ins = mm(bank[:, m * S:(m + 1) * S], w[:, k, m * P:(m + 1) * P], xnT[:, k],
                                 start=k == 0, stop=k == KD - 1)
                ins.then_inc(qk_ps, 1)

            def values(b):
                if b[0] is None and b[1] == 0:
                    pe.wait_ge(bias3_in, 48)
                wait(pe, rest_done, count(b, 4, 2))
                for t in range(TILES):
                    for k in range(KD):
                        mm(psG[1][:, t * D:(t + 1) * D], xnT[:, k, t * P:(t + 1) * P], wv[:, k],
                           start=k == 0, stop=False)
                    ins = mm(psG[1][:, t * D:(t + 1) * D], ones_bf[0:3, :], bias3[:, 0], start=False, stop=True)
                ins.then_inc(v_ps, 1)

            def peak(b, lo, hi, f=None):
                i = par(b)
                if lo == 0:
                    wait(pe, stack_in[i], count_half(b, 16 * 12, 16 * 12))
                    if b[0] is None and b[1] == 0:
                        pe.wait_ge(setup_v, 6)
                    if f:
                        wait(pe, xnT_done, count(f, KD, KD))
                for u in range(lo, hi):
                    wait(pe, peak_read, count(b, 12, max(u - 3, 0)))
                    bank = peak_bank[u % 4]
                    if u < 4:
                        for j in range(4):
                            mm(bank[:, j * P:(j + 1) * P], qs[0:STACK, i, 4 * u + j, 0:P],
                               ks[0:STACK, i, 4 * u + j, 0:P], start=j == 0, stop=False, skip_group_check=True)
                        out, mask = bank[:].rearrange("p (h k) -> p h k", h=4), (P, 4, P)
                    else:
                        for j in range(2):
                            mm(bank[:, j * S:(j + 1) * S], qs[0:STACK, i, 2 * (u - 4) + j, P:S],
                               ks[0:STACK, i, 2 * (u - 4) + j, :], start=j == 0, stop=False,
                               skip_group_check=True)
                        out, mask = bank[:].rearrange("p (h k) -> p h k", h=2)[:, :, P:S], (P, 2, P)
                    mm(out, ident_bf[:], upper[:].unsqueeze(1).broadcast_to(mask), start=False, stop=True,
                       skip_group_check=True).then_inc(peak_ps, 1)

            def negmax_T(b, a):
                wait_alone(pe, negmax_step, count(b, 4, 4))
                if not a:
                    wait(pe, negmaxT_done, count(b, 1, 0))
                for t in range(TILES):
                    ins = nc.tensor.transpose(psO[1][0:3 * NH, t * P // 2:(t + 1) * P // 2].bitcast(BF16),
                                              negmax_part[:, t].rearrange("p c h -> p (c h)"), ident_bf[:])
                ins.then_inc(negmaxT_ps, 1)

            def scores(b, u):
                i = par(b)
                grp, j = divmod(u, 3)
                if u == 0:
                    wait(pe, negmax_in[i], count_half(b, 48, 48))
                wait(pe, exp_done, count(b, 12, max(u - 1, 0)))
                for n in range(2 if j < 2 else 4):
                    h_, width, q0 = (4 * grp + 2 * j + n, S, 0) if j < 2 else (4 * grp + n, P, P)
                    keys = slice(0, P) if j < 2 else slice(P, S)
                    mm(psE[u % 2][:, n * width:(n + 1) * width], ks[0:STACK + NEGMAX, i, h_, keys], qs[0:STACK + NEGMAX, i, h_, q0:S],
                       start=n == 0, stop=False, skip_group_check=True)
                out = psE[u % 2][:].rearrange("p (h q) -> p h q", h=2 if j < 2 else 4)[:, :, 0:P]
                mm(out, ident_bf[:], lower[:].unsqueeze(1).broadcast_to((P, 2 if j < 2 else 4, P)), start=False,
                   stop=True, skip_group_check=True).then_inc(score_ps, 1)

            def weighted(b, grp):
                i, bank = par(b), psO[grp % 2]
                if grp == 0:
                    wait(pe, vs_done, count(b, 1, 1))
                    if b[0] is not None or b[1] + 2 <= NB:
                        wait(pe, rest_done, count(b, 4, 8))
                wait(pe, exp_done, count(b, 12, 3 * grp + 3))
                wait(pe, oT_done, count(b, 4, max(grp - 1, 0)))
                for j in range(4):
                    mm(bank[32 * j:32 * j + 32, 0:S], vs[:, i, 0, 4 * grp + j], probs[:, grp % 2, j * S:(j + 1) * S],
                       start=True, stop=False, skip_group_check=True)
                for j in range(4):
                    ins = mm(bank[32 * j:32 * j + 32, P:S], vs[:, i, 1, 4 * grp + j],
                             probs[:, grp % 2, 1024 + j * P:1024 + (j + 1) * P], start=False, stop=True,
                             skip_group_check=True)
                ins.then_inc(pv_ps, 1)

            def out_project(b, t):
                if t == 0:
                    if b[0] is None and b[1] == 0:
                        pe.wait_ge(weights_in, 16 * 6)
                    wait(pe, oT_done, count(b, 4, 4))
                    wait(pe, hraw_done, count(b, TILES, 0))
                out = psG[0][:, t * D:(t + 1) * D]
                for grp in range(4):
                    mm(out, oT[:, grp, t * P:(t + 1) * P], wo[:, grp], start=grp == 0, stop=False)
                ins = mm(out, ones_bf[0:3, :], bias3[:, 1], start=False, stop=True)
                if t == TILES - 1:
                    ins.then_inc(wo_ps, 1)

            def x1_T(b):
                wait(pe, x1_done, count(b, TILES, TILES))
                for k in range(KD):
                    for t in range(TILES):
                        ins = nc.tensor.transpose(psG[0][:, k * S + t * P:k * S + (t + 1) * P],
                                                  row[:, par(b), t, k * P:(k + 1) * P], ident[:])
                ins.then_inc(x1T_ps, 1)

            def gate_project(b, f, r):
                wait(pe, x1T_done, count(b, 1, 1))
                if f:
                    wait(pe, vs_done, count(f, 1, 1))
                elif r:
                    wait(pe, rank_read, count(r, 1, 2))
                for t in range(TILES):
                    for k in range(KD):
                        ins = mm(psG[1 - t][:, 0:E + 2 * SI], x1T[:, k, t * P:(t + 1) * P], wgate[:, k],
                                 start=k == 0, stop=k == KD - 1)
                    ins.then_inc(gate_ps, 1)

            def rank(b):
                wait(pe, route_step, count(b, ROUTE_STEPS, CHOOSE_STEPS))
                wait(pe, hraw_done, count(b, TILES, 1))
                out = psG[1][:, 0:TILES * E]
                mm(out, before[:], chosen[:].rearrange("p t e -> p (t e)"), start=True, stop=False)
                mm(out, ones_bf[:], earlier[:].rearrange("p t e -> p (t e)"), start=False,
                   stop=True).then_inc(rank_ps, 1)

            def shared_T(b):
                if b[1] == 0:
                    pe.wait_ge(peak_read, 12 * NB)
                    pe.wait_ge(exp_done, 12 * NB)
                pe.wait_ge(h_done, group_of(b) + 1)
                wait(pe, hT_done, count(b, 1, -1))
                for t in range(TILES):
                    for c in range(2):
                        ins = nc.tensor.transpose(psM[par(b)][0:FI, (2 * t + c) * P:(2 * t + c + 1) * P],
                                                  hraw[:, TILES * b[1] + t, c * FI:(c + 1) * FI], ident[:])
                ins.then_inc(hT_ps, 1)

            def shared_down(b):
                wait(pe, hT_done, count(b, 1, 1))
                wait(pe, sh_done, count(b, 1, -1))
                for t in range(TILES):
                    for c in range(2):
                        ins = mm(psE[par(b)][:, t * D:(t + 1) * D], hT[:, par(b), t, c], wsd[:, c], start=c == 0,
                                 stop=c == 1)
                ins.then_inc(sd_ps, 1)

            def step(f, m, a, r):
                if a:
                    for u in range(12):
                        scores(a, u)
                        if u in (4, 7, 10):
                            weighted(a, (u - 4) // 3)
                        if u == 4 and f:
                            transpose_in(f)
                        if u == 7 and r:
                            rank(r)
                    weighted(a, 3)
                else:
                    if f:
                        transpose_in(f)
                    if r:
                        rank(r)
                if m:
                    peak(m, 0, 4, f)
                if f:
                    project(f, 0, a, r)
                if a:
                    out_project(a, 0)
                    out_project(a, 1)
                if m:
                    peak(m, 4, 6)
                if f:
                    project(f, 1, a, r)
                if m:
                    peak(m, 6, 9)
                if last_seq(a):
                    shared_T((None, 0))
                    shared_T((None, 1))
                    shared_down((None, 0))
                    shared_down((None, 1))
                if a:
                    x1_T(a)
                if last_seq(a):
                    shared_T((None, 2))
                if m:
                    peak(m, 9, 12)
                if f:
                    values(f)
                if m:
                    negmax_T(m, a)
                if a:
                    gate_project(a, f, r)
                if last_seq(a):
                    shared_T((None, 3))
                    shared_down((None, 2))
                    shared_T((None, 4))
                    shared_down((None, 3))

            run(pe, step)

            shared_T((None, 5))
            shared_down((None, 4))
            shared_T((None, 6))
            shared_down((None, 5))
            shared_T((None, 7))
            shared_down((None, 6))
            shared_down((None, 7))

            pe.wait_ge(hT_done, NB)
            pe.wait_ge(sh_done, NB)
            pe.wait_ge(route_step, ROUTE_STEPS * NB)
            pe.wait_ge(hraw_done, NT)
            pe.wait_ge(oT_done, 4 * NB)

            def rows_T(p):
                i, c = p[1] % 2, p[1] % XRING
                wait(pe, slots_in[c], nth_slot(p, XRING, 16, 16))
                wait(pe, gT_done, nth(p, 1, -1))
                for k in range(KD):
                    ins = nc.tensor.transpose(psG[i][:, k * P:(k + 1) * P], gx[:, c, k * P:(k + 1) * P], ident[:])
                ins.then_inc(gT_ps, 1)

            def gate_up(p):
                i, c = p[1] % 2, p[1]
                if c < EXTRA:
                    pe.wait_ge(wexp_first[c], 48)
                elif c > NPAIR - GRING:
                    pe.wait_ge(wexp_last[c - (NPAIR - GRING + 1)], 48)
                else:
                    wait(pe, wexp_in[c % WRING], nth_slot(p, WRING, 48, 0))
                wait(pe, gT_done, nth(p, 1, 1))
                wait(pe, hid_done, nth(p, 1, -1))
                for k in range(KD):
                    for e in range(2):
                        ins = mm(psO[i][CAP * e:CAP * (e + 1), 0:2 * FI], gxT[:, i, k, CAP * e:CAP * (e + 1)],
                                 gate_up_of(c, e)[:, k], start=k == 0, stop=k == KD - 1)
                ins.then_inc(gu_ps, 1)

            def hidden_T(p):
                i = p[1] % 2
                wait(pe, hid_done, nth(p, 1, 1))
                wait(pe, hidT_done, nth(p, 1, -1))
                nc.tensor.transpose(psM[i][0:FI, 0:P], hid[:, i], ident[:]).then_inc(hidT_ps, 1)

            def down(p):
                i, c = p[1] % 2, p[1]
                wait(pe, hidT_done, nth(p, 1, 1))
                wait(pe, eo_low, nth(p, 1, -1))
                wait(pe, eo_high, nth(p, 1, -1))
                for e in range(2):
                    ins = mm(psE[i][CAP * e:CAP * (e + 1), 0:D], hidT[:, i, CAP * e:CAP * (e + 1)], down_of(c)[:, e],
                             start=True, stop=True)
                ins.then_inc(dn_ps, 1)

            rows_T((None, 0))
            rows_T((None, 1))
            gate_up((None, 0))

            def pair(p):
                last = p[0] is None and p[1] >= NPAIR - 2
                if not last:
                    rows_T(later(p, 2))
                hidden_T(p)
                if not (last and p[1] == NPAIR - 1):
                    gate_up(later(p, 1))
                down(p)

            pair_steps(pe, pair)

            pe.wait_ge(gT_done, NPAIR)
            pe.wait_ge(eo_low, NPAIR)
            pe.wait_ge(eo_high, NPAIR)
            for n in range(NT):
                c, y = n % RRING, y_bank[n % 4][:, 0:D]
                wait(pe, result_done, n - 3)
                mm(y, ident[:], x_all[:, n], start=True, stop=False)
                pe.wait_ge(sums_in[c], 16 * (n // RRING + 1))
                for j in range(2):
                    mm(y, ident[:], sums[:, c, j], start=False, stop=False)
                pe.wait_ge(half_done, n + 1)
                mm(y, ident[:], half_sum[:, n % 2], start=False, stop=True).then_inc(y_ps, 1)


def kernel(**inputs):
    import concourse.bacc as bacc
    from concourse.bass_utils import run_bass_kernel_spmd

    a = {name: np.asarray(x) for name, x in inputs.items()}

    def by_feature(w):
        return w.reshape(-1, 2, HH, DH).transpose(0, 1, 3, 2).reshape(-1, D)

    def halves(x):
        return x.reshape(2, P).T

    arrays = {
        "X": a["L0_attn_X"],
        "Wq": by_feature(a["L0_attn_Wq"]),
        "Wk": by_feature(a["L0_attn_Wk"]),
        "Wv": a["L0_attn_Wv"],
        "Wo": a["L0_attn_Wo"],
        "cols": np.concatenate([halves(a["L0_attn_ln_g"]), halves(a["L0_attn_ln_b"]),
                                halves(by_feature(a["L0_attn_bq"])), halves(by_feature(a["L0_attn_bk"]))], axis=1),
        "bias_row": np.stack([a["L0_attn_bv"], a["L0_attn_bo"]])[None],
        "Wgate": np.concatenate([a["L0_ffn_gate_w"], a["L0_ffn_shared_gate_w"], a["L0_ffn_shared_up_w"]]).T,
        "Wsd": a["L0_ffn_shared_down_w"].T,
        "gate_up": a["L0_ffn_gate_up_proj"],
        "down": a["L0_ffn_down_proj"],
    }
    arrays = {name: np.ascontiguousarray(x) for name, x in arrays.items()}

    nc = bacc.Bacc("TRN2", target_bir_lowering=False, num_devices=1)
    io = {name: nc.dram_tensor("in_" + name, x.shape, mybir.dt.from_np(x.dtype), kind="ExternalInput").ap()
          for name, x in arrays.items()}
    io["out"] = nc.dram_tensor("out", (NB, S, D), F32, kind="ExternalOutput").ap()
    moe_block_kernel(nc, io)
    r = run_bass_kernel_spmd(nc, [{"in_" + name: x for name, x in arrays.items()}], core_ids=[0])
    return r.results[0]["out"]
```
